# Optimizing a Trainium2 kernel written in Bass

```python
import numpy as np
import jax
import jax.numpy as jnp

def _softmax(x, axis=-1):
    return jax.nn.softmax(x, axis=axis)

def _gelu(x):
    return jax.nn.gelu(x, approximate=True)

def _silu(x):
    return jax.nn.silu(x)

def _sigmoid(x):
    return jax.nn.sigmoid(x)

def _layernorm(x, axis=-1, eps=1e-05):
    m = jnp.mean(x, axis=axis, keepdims=True)
    v = jnp.var(x, axis=axis, keepdims=True)
    return (x - m) / jnp.sqrt(v + eps)

def _scatter_add(tgt, idx, src, axis=0):
    return tgt.at[idx].add(src)

def _segment_sum(src, seg, n):
    return jax.ops.segment_sum(src, seg, n)
kernel_name = 'mk_early_fusion_d1_tok_img256_r4_0afba8'

def setup_inputs(seed: int=0):
    np.random.seed(seed)
    _w = jnp.asarray

    def _rec_inputs():
        import jax
        import jax.numpy as jnp
        _rk = jax.random.key(seed)
        x = 9.04603e-05 + 1.00016 * jax.random.normal(jax.random.fold_in(_rk, 1), (16, 1, 224, 224), jnp.float32)
        txt = -0.0014814 + 1.01018 * jax.random.normal(jax.random.fold_in(_rk, 2), (16, 32, 64), jnp.float32)
        return (x, txt)
    x, txt = _rec_inputs()

    def _L0_tok_setup():
        import jax, jax.numpy as jnp
        import numpy as np
        WS = 7
        H = W = 56
        C = 64
        NH = 8
        HD = C // NH
        SCALE = HD ** (-0.5)
        SHIFT = WS // 2
        N = WS * WS

        def _rel_pos_index():
            coords = np.stack(np.meshgrid(np.arange(WS), np.arange(WS), indexing='ij'))
            cf = coords.reshape(2, -1)
            rel = (cf[:, :, None] - cf[:, None, :]).transpose(1, 2, 0).copy()
            rel[..., 0] += WS - 1
            rel[..., 1] += WS - 1
            rel[..., 0] *= 2 * WS - 1
            return jnp.array(rel.sum(-1))

        def _attn_mask():
            img = np.zeros((H, W), np.int32)
            cnt = 0
            for h in (slice(0, -WS), slice(-WS, -SHIFT), slice(-SHIFT, None)):
                for w in (slice(0, -WS), slice(-WS, -SHIFT), slice(-SHIFT, None)):
                    cnt += 1
                    img[h, w] = cnt
            mw = img.reshape(H // WS, WS, W // WS, WS).transpose(0, 2, 1, 3).reshape(-1, N)
            diff = mw[:, None, :] - mw[:, :, None]
            return jnp.array(np.where(diff != 0, -100.0, 0.0).astype(np.float32))

        def _layernorm(x, g, b):
            m = x.mean(-1, keepdims=True)
            v = ((x - m) ** 2).mean(-1, keepdims=True)
            return (x - m) * jax.lax.rsqrt(v + 1e-05) * g + b

        def _window_partition(x):
            B = x.shape[0]
            x = x.reshape(B, H // WS, WS, W // WS, WS, C).transpose(0, 1, 3, 2, 4, 5)
            return x.reshape(-1, N, C)

        def _window_reverse(xw, B):
            x = xw.reshape(B, H // WS, W // WS, WS, WS, C).transpose(0, 1, 3, 2, 4, 5)
            return x.reshape(B, H, W, C)

        def _swin_block(x, p, shift, rpi, amask):
            B = x.shape[0]
            shortcut = x
            h = _layernorm(x, p['n1g'], p['n1b']).reshape(B, H, W, C)
            if shift > 0:
                h = jnp.roll(h, (-shift, -shift), axis=(1, 2))
            xw = _window_partition(h)
            B_ = xw.shape[0]
            qkv = (xw @ p['qkv_w'].T + p['qkv_b']).reshape(B_, N, 3, NH, HD).transpose(2, 0, 3, 1, 4)
            q, k, v = (qkv[0], qkv[1], qkv[2])
            attn = jnp.einsum('bhnd,bhmd->bhnm', q * SCALE, k)
            attn = attn + p['rpb'][rpi].transpose(2, 0, 1)[None]
            if shift > 0:
                nW = amask.shape[0]
                attn = attn.reshape(B_ // nW, nW, NH, N, N) + amask[None, :, None]
                attn = attn.reshape(B_, NH, N, N)
            attn = jax.nn.softmax(attn, axis=-1)
            o = jnp.einsum('bhnm,bhmd->bhnd', attn, v).transpose(0, 2, 1, 3).reshape(B_, N, C)
            o = o @ p['proj_w'].T + p['proj_b']
            h = _window_reverse(o, B)
            if shift > 0:
                h = jnp.roll(h, (shift, shift), axis=(1, 2))
            x = shortcut + h.reshape(B, H * W, C)
            y = _layernorm(x, p['n2g'], p['n2b'])
            y = jax.nn.gelu(y @ p['w1'].T + p['b1'], approximate=False)
            return x + y @ p['w2'].T + p['b2']
        key = jax.random.key(seed)
        ks = jax.random.split(key, 8)
        s = 0.02
        return {'x': jax.random.normal(ks[0], (16, 1, 224, 224), jnp.float32), 'pe_w': jax.random.normal(ks[1], (C, 1, 4, 4), jnp.float32) * s, 'pe_b': jnp.zeros((C,), jnp.float32), 'pe_ng': jnp.ones((C,), jnp.float32), 'pe_nb': jnp.zeros((C,), jnp.float32), 'n1g': jnp.ones((2, C), jnp.float32), 'n1b': jnp.zeros((2, C), jnp.float32), 'qkv_w': jax.random.normal(ks[2], (2, 3 * C, C), jnp.float32) * s, 'qkv_b': jnp.zeros((2, 3 * C), jnp.float32), 'rpb': jax.random.normal(ks[3], (2, (2 * WS - 1) ** 2, NH), jnp.float32) * s, 'proj_w': jax.random.normal(ks[4], (2, C, C), jnp.float32) * s, 'proj_b': jnp.zeros((2, C), jnp.float32), 'n2g': jnp.ones((2, C), jnp.float32), 'n2b': jnp.zeros((2, C), jnp.float32), 'w1': jax.random.normal(ks[5], (2, 4 * C, C), jnp.float32) * s, 'b1': jnp.zeros((2, 4 * C), jnp.float32), 'w2': jax.random.normal(ks[6], (2, C, 4 * C), jnp.float32) * s, 'b2': jnp.zeros((2, C), jnp.float32)}
    _L0_tok_all = _L0_tok_setup()
    _L0_tok_in = {k: v for k, v in _L0_tok_all.items() if k in ('pe_w', 'pe_b', 'pe_ng', 'pe_nb', 'n1g', 'n1b', 'qkv_w', 'qkv_b', 'rpb', 'proj_w', 'proj_b', 'n2g', 'n2b', 'w1', 'b1', 'w2', 'b2')}
    del _L0_tok_all

    def _L0_attn_setup():
        import jax, jax.numpy as jnp
        import numpy as np
        B, S, D = (32, 512, 64)
        LN_EPS = 1e-05

        def layer_norm(x, g, b):
            mu = jnp.mean(x, axis=-1, keepdims=True)
            var = jnp.mean(jnp.square(x - mu), axis=-1, keepdims=True)
            return (x - mu) * jax.lax.rsqrt(var + LN_EPS) * g + b

        def gru_scan(x, w_ih, w_hh, b_ih, b_hh):
            H = w_hh.shape[1]
            xp = jnp.einsum('bsd,hd->bsh', x, w_ih) + b_ih
            xp = jnp.swapaxes(xp, 0, 1)
            h0 = jnp.zeros((x.shape[0], H), x.dtype)

            def step(h, xt):
                gh = h @ w_hh.T + b_hh
                r = jax.nn.sigmoid(xt[:, :H] + gh[:, :H])
                z = jax.nn.sigmoid(xt[:, H:2 * H] + gh[:, H:2 * H])
                n = jnp.tanh(xt[:, 2 * H:] + r * gh[:, 2 * H:])
                h_new = (1.0 - z) * n + z * h
                return (h_new, h_new)
            _, ys = jax.lax.scan(step, h0, xp)
            return jnp.swapaxes(ys, 0, 1)
        key = jax.random.key(seed)
        ks = jax.random.split(key, 16)
        s = 1.0 / np.sqrt(D)
        u = lambda k, shape: jax.random.uniform(k, shape, jnp.float32, -s, s)
        return {'x': jax.random.normal(ks[0], (B, S, D), jnp.float32), 'ln_g': jnp.ones((D,), jnp.float32), 'ln_b': jnp.zeros((D,), jnp.float32), 'fwd_w_ih': u(ks[1], (3 * D, D)), 'fwd_w_hh': u(ks[2], (3 * D, D)), 'fwd_b_ih': u(ks[3], (3 * D,)), 'fwd_b_hh': u(ks[4], (3 * D,)), 'rev_w_ih': u(ks[5], (3 * D, D)), 'rev_w_hh': u(ks[6], (3 * D, D)), 'rev_b_ih': u(ks[7], (3 * D,)), 'rev_b_hh': u(ks[8], (3 * D,)), 'gate_w': u(ks[9], (D, 2 * D)), 'gate_b': u(ks[10], (D,)), 'out_w': u(ks[11], (D, D)), 'out_b': u(ks[12], (D,))}
    _L0_attn_all = _L0_attn_setup()
    _L0_attn_in = {k: v for k, v in _L0_attn_all.items() if k in ('ln_g', 'ln_b', 'fwd_w_ih', 'fwd_w_hh', 'fwd_b_ih', 'fwd_b_hh', 'rev_w_ih', 'rev_w_hh', 'rev_b_ih', 'rev_b_hh', 'gate_w', 'gate_b', 'out_w', 'out_b')}
    del _L0_attn_all

    def _L0_ffn_setup():
        import jax, jax.numpy as jnp
        import numpy as np
        NUM_EXPERTS = 8
        TOP_K = 2
        B, S, D = (8, 2048, 64)

        def _moe(tokens, router_w, w1, b1, w2, b2):
            N = tokens.shape[0]
            E = router_w.shape[0]
            logits = tokens.astype(jnp.float32) @ router_w.astype(jnp.float32).T
            probs = jax.nn.softmax(logits, axis=-1)
            rw, re = jax.lax.top_k(probs, TOP_K)
            if TOP_K > 1:
                rw = rw / jnp.maximum(rw.sum(-1, keepdims=True), 1e-12)
            rw = rw.astype(tokens.dtype)
            combine = jnp.zeros((N, E), tokens.dtype).at[jnp.arange(N)[:, None], re].set(rw)
            out = tokens
            for e in range(E):
                h = jax.nn.gelu(tokens @ w1[e] + b1[e], approximate=False)
                y = h @ w2[e] + b2[e]
                out = out + combine[:, e:e + 1] * y
            return out
        key = jax.random.key(seed)
        ks = jax.random.split(key, 4)
        scale = 1.0 / np.sqrt(D).astype(np.float32)
        return {'input_embeddings': jax.random.normal(ks[0], (B, S, D), jnp.float32), 'router_w': jax.random.normal(ks[1], (NUM_EXPERTS, D), jnp.float32) * scale, 'w1': jax.random.normal(ks[2], (NUM_EXPERTS, D, D), jnp.float32) * scale, 'b1': jnp.zeros((NUM_EXPERTS, D), jnp.float32), 'w2': jax.random.normal(ks[3], (NUM_EXPERTS, D, D), jnp.float32) * scale, 'b2': jnp.zeros((NUM_EXPERTS, D), jnp.float32)}
    _L0_ffn_all = _L0_ffn_setup()
    _L0_ffn_in = {k: v for k, v in _L0_ffn_all.items() if k in ('router_w', 'w1', 'b1', 'w2', 'b2')}
    del _L0_ffn_all
    return {'x': x, 'txt': txt, 'L0_tok_pe_w': _L0_tok_in['pe_w'], 'L0_tok_pe_b': _L0_tok_in['pe_b'], 'L0_tok_pe_ng': _L0_tok_in['pe_ng'], 'L0_tok_pe_nb': _L0_tok_in['pe_nb'], 'L0_tok_n1g': _L0_tok_in['n1g'], 'L0_tok_n1b': _L0_tok_in['n1b'], 'L0_tok_qkv_w': _L0_tok_in['qkv_w'], 'L0_tok_qkv_b': _L0_tok_in['qkv_b'], 'L0_tok_rpb': _L0_tok_in['rpb'], 'L0_tok_proj_w': _L0_tok_in['proj_w'], 'L0_tok_proj_b': _L0_tok_in['proj_b'], 'L0_tok_n2g': _L0_tok_in['n2g'], 'L0_tok_n2b': _L0_tok_in['n2b'], 'L0_tok_w1': _L0_tok_in['w1'], 'L0_tok_b1': _L0_tok_in['b1'], 'L0_tok_w2': _L0_tok_in['w2'], 'L0_tok_b2': _L0_tok_in['b2'], 'L0_attn_ln_g': _L0_attn_in['ln_g'], 'L0_attn_ln_b': _L0_attn_in['ln_b'], 'L0_attn_fwd_w_ih': _L0_attn_in['fwd_w_ih'], 'L0_attn_fwd_w_hh': _L0_attn_in['fwd_w_hh'], 'L0_attn_fwd_b_ih': _L0_attn_in['fwd_b_ih'], 'L0_attn_fwd_b_hh': _L0_attn_in['fwd_b_hh'], 'L0_attn_rev_w_ih': _L0_attn_in['rev_w_ih'], 'L0_attn_rev_w_hh': _L0_attn_in['rev_w_hh'], 'L0_attn_rev_b_ih': _L0_attn_in['rev_b_ih'], 'L0_attn_rev_b_hh': _L0_attn_in['rev_b_hh'], 'L0_attn_gate_w': _L0_attn_in['gate_w'], 'L0_attn_gate_b': _L0_attn_in['gate_b'], 'L0_attn_out_w': _L0_attn_in['out_w'], 'L0_attn_out_b': _L0_attn_in['out_b'], 'L0_ffn_router_w': _L0_ffn_in['router_w'], 'L0_ffn_w1': _L0_ffn_in['w1'], 'L0_ffn_b1': _L0_ffn_in['b1'], 'L0_ffn_w2': _L0_ffn_in['w2'], 'L0_ffn_b2': _L0_ffn_in['b2']}

def reference(x, txt, L0_tok_pe_w, L0_tok_pe_b, L0_tok_pe_ng, L0_tok_pe_nb, L0_tok_n1g, L0_tok_n1b, L0_tok_qkv_w, L0_tok_qkv_b, L0_tok_rpb, L0_tok_proj_w, L0_tok_proj_b, L0_tok_n2g, L0_tok_n2b, L0_tok_w1, L0_tok_b1, L0_tok_w2, L0_tok_b2, L0_attn_ln_g, L0_attn_ln_b, L0_attn_fwd_w_ih, L0_attn_fwd_w_hh, L0_attn_fwd_b_ih, L0_attn_fwd_b_hh, L0_attn_rev_w_ih, L0_attn_rev_w_hh, L0_attn_rev_b_ih, L0_attn_rev_b_hh, L0_attn_gate_w, L0_attn_gate_b, L0_attn_out_w, L0_attn_out_b, L0_ffn_router_w, L0_ffn_w1, L0_ffn_b1, L0_ffn_w2, L0_ffn_b2):
    import jax
    import jax.numpy as jnp

    def _L0_tok_ref(x, pe_w, pe_b, pe_ng, pe_nb, n1g, n1b, qkv_w, qkv_b, rpb, proj_w, proj_b, n2g, n2b, w1, b1, w2, b2):
        import jax, jax.numpy as jnp
        import numpy as np
        WS = 7
        H = W = 56
        C = 64
        NH = 8
        HD = C // NH
        SCALE = HD ** (-0.5)
        SHIFT = WS // 2
        N = WS * WS

        def _rel_pos_index():
            coords = np.stack(np.meshgrid(np.arange(WS), np.arange(WS), indexing='ij'))
            cf = coords.reshape(2, -1)
            rel = (cf[:, :, None] - cf[:, None, :]).transpose(1, 2, 0).copy()
            rel[..., 0] += WS - 1
            rel[..., 1] += WS - 1
            rel[..., 0] *= 2 * WS - 1
            return jnp.array(rel.sum(-1))

        def _attn_mask():
            img = np.zeros((H, W), np.int32)
            cnt = 0
            for h in (slice(0, -WS), slice(-WS, -SHIFT), slice(-SHIFT, None)):
                for w in (slice(0, -WS), slice(-WS, -SHIFT), slice(-SHIFT, None)):
                    cnt += 1
                    img[h, w] = cnt
            mw = img.reshape(H // WS, WS, W // WS, WS).transpose(0, 2, 1, 3).reshape(-1, N)
            diff = mw[:, None, :] - mw[:, :, None]
            return jnp.array(np.where(diff != 0, -100.0, 0.0).astype(np.float32))

        def _layernorm(x, g, b):
            m = x.mean(-1, keepdims=True)
            v = ((x - m) ** 2).mean(-1, keepdims=True)
            return (x - m) * jax.lax.rsqrt(v + 1e-05) * g + b

        def _window_partition(x):
            B = x.shape[0]
            x = x.reshape(B, H // WS, WS, W // WS, WS, C).transpose(0, 1, 3, 2, 4, 5)
            return x.reshape(-1, N, C)

        def _window_reverse(xw, B):
            x = xw.reshape(B, H // WS, W // WS, WS, WS, C).transpose(0, 1, 3, 2, 4, 5)
            return x.reshape(B, H, W, C)

        def _swin_block(x, p, shift, rpi, amask):
            B = x.shape[0]
            shortcut = x
            h = _layernorm(x, p['n1g'], p['n1b']).reshape(B, H, W, C)
            if shift > 0:
                h = jnp.roll(h, (-shift, -shift), axis=(1, 2))
            xw = _window_partition(h)
            B_ = xw.shape[0]
            qkv = (xw @ p['qkv_w'].T + p['qkv_b']).reshape(B_, N, 3, NH, HD).transpose(2, 0, 3, 1, 4)
            q, k, v = (qkv[0], qkv[1], qkv[2])
            attn = jnp.einsum('bhnd,bhmd->bhnm', q * SCALE, k)
            attn = attn + p['rpb'][rpi].transpose(2, 0, 1)[None]
            if shift > 0:
                nW = amask.shape[0]
                attn = attn.reshape(B_ // nW, nW, NH, N, N) + amask[None, :, None]
                attn = attn.reshape(B_, NH, N, N)
            attn = jax.nn.softmax(attn, axis=-1)
            o = jnp.einsum('bhnm,bhmd->bhnd', attn, v).transpose(0, 2, 1, 3).reshape(B_, N, C)
            o = o @ p['proj_w'].T + p['proj_b']
            h = _window_reverse(o, B)
            if shift > 0:
                h = jnp.roll(h, (shift, shift), axis=(1, 2))
            x = shortcut + h.reshape(B, H * W, C)
            y = _layernorm(x, p['n2g'], p['n2b'])
            y = jax.nn.gelu(y @ p['w1'].T + p['b1'], approximate=False)
            return x + y @ p['w2'].T + p['b2']
        B = x.shape[0]
        h = jax.lax.conv_general_dilated(x, pe_w, (4, 4), 'VALID', dimension_numbers=('NCHW', 'OIHW', 'NCHW'))
        h = h + pe_b[None, :, None, None]
        t = h.reshape(B, C, H * W).transpose(0, 2, 1)
        t = _layernorm(t, pe_ng, pe_nb)
        rpi = _rel_pos_index()
        amask = _attn_mask()
        for i, shift in enumerate((0, SHIFT)):
            p = {'n1g': n1g[i], 'n1b': n1b[i], 'qkv_w': qkv_w[i], 'qkv_b': qkv_b[i], 'rpb': rpb[i], 'proj_w': proj_w[i], 'proj_b': proj_b[i], 'n2g': n2g[i], 'n2b': n2b[i], 'w1': w1[i], 'b1': b1[i], 'w2': w2[i], 'b2': b2[i]}
            t = _swin_block(t, p, shift, rpi, amask)
        return t

    def _L0_attn_ref(x, ln_g, ln_b, fwd_w_ih, fwd_w_hh, fwd_b_ih, fwd_b_hh, rev_w_ih, rev_w_hh, rev_b_ih, rev_b_hh, gate_w, gate_b, out_w, out_b):
        import jax, jax.numpy as jnp
        import numpy as np
        B, S, D = (32, 512, 64)
        LN_EPS = 1e-05

        def layer_norm(x, g, b):
            mu = jnp.mean(x, axis=-1, keepdims=True)
            var = jnp.mean(jnp.square(x - mu), axis=-1, keepdims=True)
            return (x - mu) * jax.lax.rsqrt(var + LN_EPS) * g + b

        def gru_scan(x, w_ih, w_hh, b_ih, b_hh):
            H = w_hh.shape[1]
            xp = jnp.einsum('bsd,hd->bsh', x, w_ih) + b_ih
            xp = jnp.swapaxes(xp, 0, 1)
            h0 = jnp.zeros((x.shape[0], H), x.dtype)

            def step(h, xt):
                gh = h @ w_hh.T + b_hh
                r = jax.nn.sigmoid(xt[:, :H] + gh[:, :H])
                z = jax.nn.sigmoid(xt[:, H:2 * H] + gh[:, H:2 * H])
                n = jnp.tanh(xt[:, 2 * H:] + r * gh[:, 2 * H:])
                h_new = (1.0 - z) * n + z * h
                return (h_new, h_new)
            _, ys = jax.lax.scan(step, h0, xp)
            return jnp.swapaxes(ys, 0, 1)
        residual = x
        xn = layer_norm(x, ln_g, ln_b)
        fwd_out = gru_scan(xn, fwd_w_ih, fwd_w_hh, fwd_b_ih, fwd_b_hh)
        rev_out = gru_scan(xn[:, ::-1], rev_w_ih, rev_w_hh, rev_b_ih, rev_b_hh)[:, ::-1]
        g = jax.nn.sigmoid(jnp.concatenate([fwd_out, rev_out], axis=-1) @ gate_w.T + gate_b)
        combined = g * fwd_out + (1.0 - g) * rev_out
        out = combined @ out_w.T + out_b
        return out + residual

    def _L0_ffn_ref(input_embeddings, router_w, w1, b1, w2, b2):
        import jax, jax.numpy as jnp
        import numpy as np
        NUM_EXPERTS = 8
        TOP_K = 2
        B, S, D = (8, 2048, 64)

        def _moe(tokens, router_w, w1, b1, w2, b2):
            N = tokens.shape[0]
            E = router_w.shape[0]
            logits = tokens.astype(jnp.float32) @ router_w.astype(jnp.float32).T
            probs = jax.nn.softmax(logits, axis=-1)
            rw, re = jax.lax.top_k(probs, TOP_K)
            if TOP_K > 1:
                rw = rw / jnp.maximum(rw.sum(-1, keepdims=True), 1e-12)
            rw = rw.astype(tokens.dtype)
            combine = jnp.zeros((N, E), tokens.dtype).at[jnp.arange(N)[:, None], re].set(rw)
            out = tokens
            for e in range(E):
                h = jax.nn.gelu(tokens @ w1[e] + b1[e], approximate=False)
                y = h @ w2[e] + b2[e]
                out = out + combine[:, e:e + 1] * y
            return out
        b, s, d = input_embeddings.shape
        tokens = input_embeddings.reshape(b * s, d)
        return _moe(tokens, router_w, w1, b1, w2, b2).reshape(b, s, d)
    h = _L0_tok_ref(x, L0_tok_pe_w, L0_tok_pe_b, L0_tok_pe_ng, L0_tok_pe_nb, L0_tok_n1g, L0_tok_n1b, L0_tok_qkv_w, L0_tok_qkv_b, L0_tok_rpb, L0_tok_proj_w, L0_tok_proj_b, L0_tok_n2g, L0_tok_n2b, L0_tok_w1, L0_tok_b1, L0_tok_w2, L0_tok_b2)
    h = jnp.concatenate([h, txt], axis=1)
    h = h + _L0_attn_ref(_layernorm(h, axis=-1), L0_attn_ln_g, L0_attn_ln_b, L0_attn_fwd_w_ih, L0_attn_fwd_w_hh, L0_attn_fwd_b_ih, L0_attn_fwd_b_hh, L0_attn_rev_w_ih, L0_attn_rev_w_hh, L0_attn_rev_b_ih, L0_attn_rev_b_hh, L0_attn_gate_w, L0_attn_gate_b, L0_attn_out_w, L0_attn_out_b)
    h = h + _L0_ffn_ref(_layernorm(h, axis=-1), L0_ffn_router_w, L0_ffn_w1, L0_ffn_b1, L0_ffn_w2, L0_ffn_b2)
    return h

_drawn_inputs = setup_inputs


def setup_inputs(seed=0):
    import zlib

    import numpy as np

    out = dict(_drawn_inputs(seed))
    spreads = {'L0_tok_pe_b': (0.0, 0.1),
     'L0_tok_pe_ng': (1.0, 0.2),
     'L0_tok_pe_nb': (0.0, 0.1),
     'L0_tok_n1g': (1.0, 0.6),
     'L0_tok_n1b': (0.0, 0.798),
     'L0_tok_qkv_b': (0.0, 0.282),
     'L0_tok_proj_b': (0.0, 0.1),
     'L0_tok_n2g': (1.0, 0.6),
     'L0_tok_n2b': (0.0, 0.73),
     'L0_tok_b1': (0.0, 0.1),
     'L0_tok_b2': (0.0, 0.1),
     'L0_attn_ln_g': (1.0, 0.6),
     'L0_attn_ln_b': (0.0, 0.481),
     'L0_ffn_b1': (0.0, 0.485),
     'L0_ffn_b2': (0.0, 0.356)}
    factors = {'L0_tok_rpb': 200.0,
     'L0_attn_fwd_w_hh': 3.835,
     'L0_attn_fwd_b_ih': 4.154,
     'L0_attn_fwd_b_hh': 8.0,
     'L0_attn_rev_w_hh': 2.937,
     'L0_attn_rev_b_ih': 3.449,
     'L0_attn_rev_b_hh': 8.0,
     'L0_attn_gate_w': 3.178,
     'L0_attn_gate_b': 8.0}
    for name, (base, spread) in spreads.items():
        noise = np.random.default_rng([zlib.crc32(name.encode()), seed]).standard_normal(out[name].shape)
        drawn = base * np.exp(spread * noise) if base else spread * noise
        out[name] = jnp.asarray(drawn.astype(out[name].dtype))
    for name, factor in factors.items():
        out[name] = (out[name] * factor).astype(out[name].dtype)
    return out
```

```python
import concourse.bass as bass
from concourse import mybir
from contextlib import ExitStack

F32 = mybir.dt.float32
F16 = mybir.dt.float16
ACT = mybir.ActivationFunctionType
ALU = mybir.AluOpType
AX = mybir.AxisListType

NIMG, HB, C = 16, 8, 64
WS, GRID = 7, 56
SHIFT = WS // 2
NTOK = GRID * GRID
NTXT = 32
S = NTOK + NTXT
NW = GRID // WS
SC = WS * GRID
WT = WS * WS
NH, HD = 8, 8
KP = 64
EPS = 1e-5
LN_EXP = "natural_log_exp_and_others"

N1G, N1B, N2G, N2B, QB, KB, VB, PB, B2, B1 = range(10)
LV = 13
PEB, PEG, PENB = 2 * LV, 2 * LV + 1, 2 * LV + 2
NVEC = 2 * LV + 3
WQ, WK, WV, WP, W1, W2 = 0, 1, 2, 3, 4, 8
LW = 12


def swin(nc, patches, wts, pew, vec, rpb, amask, hmask, consts, tok1, tok2):
    with ExitStack() as ctx:
        def sb(name, shape, dt=F32):
            return ctx.enter_context(nc.sbuf_tensor(name, shape, dt))

        def bank(name):
            return ctx.enter_context(nc.psum_tensor(name, [128, 512], F32))

        def sem(name):
            return ctx.enter_context(nc.semaphore(name))

        w = sb("w", [128, 2, LW, 128])
        pe_w = sb("pe_w", [32, 128])
        v = sb("v", [128, NVEC])
        vf = sb("vf", [128, 2, 8])
        ident = sb("ident", [128, 128])
        center = sb("center", [128, 128])
        mean = sb("mean", [128, 128])
        eps = sb("eps", [128, 1])
        rpb_l = sb("rpb_l", [128, 2, NH * WT])
        am = sb("am", [128, 4, NH * WT])
        bias = sb("bias", [128, 2, NH * WT])
        hm = sb("hm", [128, NH])
        px = [sb(f"px{u}", [32, SC]) for u in (0, 1)]
        x = [sb(f"x{u}", [128, SC]) for u in (0, 1)]
        xo = [sb(f"xo{u}", [128, SC]) for u in (0, 1)]
        sq = [sb(f"sq{u}", [128, SC]) for u in (0, 1)]
        lnv = [sb(f"lnv{u}", [128, SC]) for u in (0, 1)]
        rs = [sb(f"rs{u}", [128, SC]) for u in (0, 1)]
        xn = [sb(f"xn{u}", [128, 512]) for u in (0, 1)]
        qbd = [sb(f"qbd{u}", [128, NW, 128]) for u in (0, 1)]
        vz = [sb(f"vz{u}", [128, NW, 4 * (128 + 2 * HD)]) for u in (0, 1)]
        ot = [sb(f"ot{u}", [128, SC]) for u in (0, 1)]
        gh = [sb(f"gh{u}", [128, 4, SC]) for u in (0, 1)]
        kbd = [sb(f"kbd{r}", [128, NH, WT]) for r in (0, 1)]
        R, RP = 4, 6
        s1 = [sb(f"s1_{r}", [128, NH, WT]) for r in range(R)]
        s2 = [sb(f"s2_{r}", [128, NH, WT]) for r in range(R)]
        ex = [sb(f"ex{r}", [128, NH, WT]) for r in range(R)]
        pn = [sb(f"pn{r}", [128, NH, KP]) for r in range(RP)]
        mx = [sb(f"mx{r}", [128, NH]) for r in range(R)]
        sm = [sb(f"sm{r}", [128, NH]) for r in range(R)]
        rc = [sb(f"rc{r}", [128, NH]) for r in range(R)]
        pt = [sb(f"pt{r}", [128, 4, 128]) for r in (0, 1)]

        G = [bank(f"G{u}") for u in (0, 1)]
        O = [bank(f"O{u}") for u in (0, 1)]
        P = [bank(f"P{u}") for u in (0, 1)]
        T = [bank(f"T{u}") for u in (0, 1)]

        weights_loaded = sem("weights_loaded")
        setup_pe = sem("setup_pe")
        setup_dve = sem("setup_dve")
        consts_ready = sem("consts_ready")
        bias_set = sem("bias_set")
        loaded = [sem(f"loaded{u}") for u in (0, 1)]
        stored = [sem(f"stored{u}") for u in (0, 1)]
        x_free = sem("x_free")
        embedded = sem("embedded")
        emb_biased = sem("emb_biased")
        pre_affine = sem("pre_affine")
        x_ready = sem("x_ready")
        centered = {k: sem(f"centered_{k}") for k in "p12"}
        squared = {k: sem(f"squared_{k}") for k in "p12"}
        var_ready = {k: sem(f"var_ready_{k}") for k in "p12"}
        log_ready = {k: sem(f"log_ready_{k}") for k in "p12"}
        rstd_ready = {k: sem(f"rstd_ready_{k}") for k in "p12"}
        normed = {k: sem(f"normed_{k}") for k in "12"}
        q_done, q_kept = sem("q_done"), sem("q_kept")
        k_done, kbd_ready = sem("k_done"), sem("kbd_ready")
        v_done, v_kept = sem("v_done"), sem("v_kept")
        scores, biased, max_ready, shifted = sem("scores"), sem("biased"), sem("max_ready"), sem("shifted")
        exps, sum_ready, rcp_ready, probs = sem("exps"), sem("sum_ready"), sem("rcp_ready"), sem("probs")
        transposed, pt_kept = sem("transposed"), sem("pt_kept")
        attended, o_kept = sem("attended"), sem("o_kept")
        projected, proj_biased, res_added = sem("projected"), sem("proj_biased"), sem("res_added")
        up_done, gelu_done, down_done = sem("up_done"), sem("gelu_done"), sem("down_done")

        block = ctx.enter_context(nc.Block())
        SUM_LAG, PROB_LAG, T_LAG, AV_LAG = 2, 3, 5, 6
        NS = 2 * 16

        def steps(eng, body, between=None):
            with eng.Fori(0, NW) as s:
                with eng.Fori(0, 4) as q:
                    body(0, s, q, False)
            if between:
                between(0)
            with eng.Fori(0, NW - 1) as s:
                with eng.Fori(0, 4) as q:
                    body(1, s, q, False)
            if between:
                between(1)
            with eng.Fori(0, 4) as q:
                body(1, NW - 1, q, True)

        def windowed(t, layer):
            g = t.rearrange("p (r g) -> p r g", g=GRID)
            if layer == 0:
                return [(g.rearrange("p r (w c) -> p w r c", c=WS), 0, NW, 0, WS)]
            n = NW - 1
            return [(g[:, :, SHIFT:SHIFT + n * WS].rearrange("p r (w c) -> p w r c", c=WS), 0, n, 0, WS),
                    (g[:, :, SHIFT + n * WS:GRID], n, 1, 0, WS - SHIFT),
                    (g[:, :, 0:SHIFT], n, 1, WS - SHIFT, WS)]

        def window_cols(t, w0, nw, c0, c1):
            q = t[:, 0:SC].rearrange("p (w r c) -> p w r c", r=WS, c=WS)[:, w0:w0 + nw, :, c0:c1]
            return q if nw > 1 else q[:, 0]

        @block.sync
        def _(sp):
            for dst, src in ((w[:].rearrange("p a b c -> p (a b c)"), wts), (pe_w[:], pew), (v[:], vec),
                             (rpb_l[:].rearrange("p a b -> p (a b)"), rpb),
                             (am[:].rearrange("p a b -> p (a b)"), amask), (hm[:], hmask),
                             (ident[:], consts[0]), (center[:], consts[1]), (mean[:], consts[2])):
                sp.dma_start(dst, src).then_inc(weights_loaded, 16)

            def ends(layer, s, q, u, wraps):
                head = (WS - SHIFT) * GRID
                base = (q * 2 + u) * NTOK
                a = base + s * SC + (SHIFT * GRID if layer else 0)
                b = base if wraps else a + head
                return (a, 0, head), (b, head, SC)

            def body(layer, s, q, wraps):
                n = layer * NS + s * 4 + q
                for u in (0, 1):
                    sp.wait_ge(x_free, n * 2 + u + 1)
                    src, dst = (patches, px[u]) if layer == 0 else (tok1, x[u])
                    for at, c0, c1 in ends(0, s, q, u, False) if layer == 0 else ends(1, s, q, u, wraps):
                        sp.dma_start(dst[:, c0:c1], src[:, bass.ds(at, c1 - c0)]).then_inc(loaded[u], 16)
                for u in (0, 1):
                    sp.wait_ge(x_free, n * 2 + u + 3)
                    out = tok1 if layer == 0 else tok2
                    for at, c0, c1 in ends(layer, s, q, u, wraps):
                        sp.dma_start(out[:, bass.ds(at, c1 - c0)], xo[u][:, c0:c1]).then_inc(stored[u], 16)

            def between(k):
                if k == 0:
                    for u in (0, 1):
                        sp.wait_ge(stored[u], 32 * NS + 1)

            steps(sp, body, between)
            for u in (0, 1):
                sp.wait_ge(stored[u], 64 * NS + 1)

        @block.tensor
        def _(pe):
            mm = nc.tensor.matmul
            pe.wait_ge(weights_loaded, 9 * 16)
            for l in (0, 1):
                for i, blk in enumerate((WQ, WK, WV)):
                    mm(G[l][:, i:i + 1], w[:, l, blk, :], v[:, l * LV + N1B:l * LV + N1B + 1], start=True, stop=True)
                for i in range(4):
                    last = mm(G[l][:, 4 + i:5 + i], w[:, l, W1 + i, :], v[:, l * LV + N2B:l * LV + N2B + 1],
                              start=True, stop=True)
            last.then_inc(setup_pe, 1)
            pe.wait_ge(setup_dve, 1)
            for l in (0, 1):
                last = mm(O[l][:, 0:1], w[:, l, WP, :], vf[:, l, 2:3], start=True, stop=True)
            last.then_inc(setup_pe, 1)
            pe.wait_ge(consts_ready, 1)

            def norm(k, m, wait_input):
                for u in (0, 1):
                    wait_input(u)
                    mm(G[u][:, 0:SC], center[:], x[u][:], start=True, stop=True).then_inc(centered[k], 1)
                for u in (0, 1):
                    pe.wait_ge(squared[k], m + u + 1)
                    mm(O[u][:, 0:SC], mean[:], sq[u][:], start=True, stop=True).then_inc(var_ready[k], 1)

            def body(layer, s, q, wraps):
                n = layer * NS + s * 4 + q
                m = n * 2
                W = lambda blk: w[:, layer, blk, :]
                for u in (0, 1):
                    pe.wait_ge(loaded[u], n * 32 + 32)
                    if layer == 0:
                        mm(G[u][:, 0:SC], pe_w[:], px[u][:], start=True, stop=True).then_inc(embedded, 1)
                pe.wait_ge(x_free, m + 2)
                if layer == 0:
                    norm("p", m, lambda u: pe.wait_ge(emb_biased, m + u + 1))
                    norm("1", m, lambda u: pe.wait_ge(x_ready, m + u + 1))
                else:
                    norm("1", m, lambda u: None)
                for u in (0, 1):
                    pe.wait_ge(normed["1"], m + u + 1)
                    mm(O[u][:, 0:SC], W(WQ), xn[u][:, 0:SC], start=True, stop=True).then_inc(q_done, 1)
                    mm(G[u][:, 0:SC], W(WK), xn[u][:, 0:SC], start=True, stop=True).then_inc(k_done, 1)
                for u in (0, 1):
                    for b in (0, 1):
                        if u == 1:
                            pe.wait_ge(v_kept, m * 2 + b + 1)
                        for i in range(4):
                            at = (b * 4 + i) * WT
                            last = mm(P[b][0:KP, i * 128:(i + 1) * 128], xn[u][:, at:at + KP], W(WV), start=True, stop=True)
                        last.then_inc(v_done, 1)
                pe.wait_ge(q_kept, m + 2)
                pe.wait_ge(v_kept, m * 2 + 4)
                for i in range(16 + AV_LAG):
                    if i < 16:
                        u, a = i // 8, i % 8
                        pe.wait_ge(kbd_ready, m * 8 + i + 1)
                        mm(P[i % 2][:, 0:NH * WT], qbd[u][:, a, :], kbd[i % 2][:].rearrange("p h k -> p (h k)"),
                           start=True, stop=True).then_inc(scores, 1)
                    if 0 <= i - T_LAG < 16:
                        j = i - T_LAG
                        pe.wait_ge(probs, m * 8 + j + 1)
                        for h in range(4):
                            last = nc.tensor.transpose(T[j % 2][:, h * 128:(h + 1) * 128],
                                                       pn[j % RP][:, 2 * h:2 * h + 2, :].rearrange("p h k -> p (h k)"), ident[:])
                        last.then_inc(transposed, 1)
                    if i >= AV_LAG:
                        j = i - AV_LAG
                        u, a = j // 8, j % 8
                        pe.wait_ge(pt_kept, m * 8 + j + 1)
                        if u == 1 and a % 4 == 0:
                            pe.wait_ge(o_kept, m * 2 + a // 4 + 1)
                        for h in range(4):
                            last = mm(O[a // 4][:, (a % 4) * 128:(a % 4 + 1) * 128], vz[u][:, a, h * 128:(h + 1) * 128],
                                      pt[j % 2][:, h, :], start=h == 0, stop=h == 3)
                        if a % 4 == 3:
                            last.then_inc(attended, 1)
                for u in (0, 1):
                    pe.wait_ge(o_kept, m * 2 + 2 * u + 2)
                    mm(G[u][:, 0:SC], W(WP), ot[u][:], start=True, stop=True).then_inc(projected, 1)
                norm("2", m, lambda u: pe.wait_ge(res_added, m + u + 1))
                for u in (0, 1):
                    pe.wait_ge(normed["2"], m + u + 1)
                    for c in range(4):
                        if u == 1:
                            pe.wait_ge(gelu_done, m * 4 + c + 1)
                        mm((T + P)[c][:, 0:SC], W(W1 + c), xn[u][:, 0:SC], start=True, stop=True).then_inc(up_done, 1)
                for u in (0, 1):
                    pe.wait_ge(gelu_done, (m + u) * 4 + 4)
                    for c in range(4):
                        last = mm(O[u][:, 0:SC], W(W2 + c), gh[u][:, c, :], start=c == 0, stop=c == 3)
                    last.then_inc(down_done, 1)

            steps(pe, body)

        @block.scalar
        def _(act):
            A = nc.scalar.activation
            act.wait_ge(consts_ready, 1)

            def norm(k, m):
                for u in (0, 1):
                    act.wait_ge(centered[k], m + u + 1)
                    A(sq[u][:], G[u][:, 0:SC], ACT.Square).then_inc(squared[k], 1)
                for u in (0, 1):
                    act.wait_ge(var_ready[k], m + u + 1)
                    A(lnv[u][:], O[u][:, 0:SC], ACT.Ln, bias=eps[:]).then_inc(log_ready[k], 1)
                    act.wait_ge(log_ready[k], m + u + 1)
                    A(rs[u][:], lnv[u][:], ACT.Exp, scale=-0.5).then_inc(rstd_ready[k], 1)

            def body(layer, s, q, wraps):
                n = layer * NS + s * 4 + q
                m = n * 2
                act.preload_act_table_set(LN_EXP)
                if layer == 0:
                    norm("p", m)
                norm("1", m)
                for u in (0, 1):
                    act.wait_ge(q_done, m + u + 1)
                    for h in (0, 1):
                        r = slice(64 * h, 64 * h + 64)
                        last = A(qbd[u][r, :, 64 * h:64 * h + WT], O[u][r, 0:SC].rearrange("p (w t) -> p w t", t=WT),
                                 ACT.Identity, bias=vf[r, layer, 0:1], scale=float(HD) ** -0.5)
                    last.then_inc(q_kept, 1)
                for u in (0, 1):
                    for b in (0, 1):
                        act.wait_ge(v_done, (m + u) * 2 + b + 1)
                        src = P[b][0:KP, :].rearrange("p (w h j e d) -> p w h j e d", w=4, h=2, j=4, e=2)
                        dst = vz[u][:, 4 * b:4 * b + 4].rearrange("p w (j s) -> p w j s", j=4)
                        for e in (0, 1):
                            r = slice(64 * e, 64 * e + 64)
                            for h in (0, 1):
                                c = 64 * h + HD * e
                                last = A(dst[r, :, :, c:c + HD], src[:, :, h, :, e, :], ACT.Copy)
                        last.then_inc(v_kept, 1)
                for i in range(16 + AV_LAG):
                    if i < 16:
                        act.wait_ge(shifted, m * 8 + i + 1)
                        A(ex[i % R][:], s2[i % R][:], ACT.Exp).then_inc(exps, 1)
                    if 0 <= i - T_LAG < 16:
                        j = i - T_LAG
                        act.wait_ge(transposed, m * 8 + j + 1)
                        A(pt[j % 2][:].rearrange("p a b -> p (a b)"), T[j % 2][:], ACT.Copy).then_inc(pt_kept, 1)
                    if i >= AV_LAG and (i - AV_LAG) % 4 == 3:
                        u, b = (i - AV_LAG) // 8, (i - AV_LAG) % 8 // 4
                        act.wait_ge(attended, (m + u) * 2 + b + 1)
                        for h in (0, 1):
                            r = slice(64 * h, 64 * h + 64)
                            last = A(ot[u][r, b * 4 * WT:(b + 1) * 4 * WT].rearrange("p (w t) -> p w t", t=WT),
                                     O[b][r, :].rearrange("p (w t) -> p w t", t=128)[:, :, 64 * h:64 * h + WT], ACT.Copy)
                        last.then_inc(o_kept, 1)
                for u in (0, 1):
                    act.wait_ge(projected, m + u + 1)
                    A(lnv[u][:], G[u][:, 0:SC], ACT.Identity, bias=vf[:, layer, 3:4]).then_inc(proj_biased, 1)
                norm("2", m)
                for u in (0, 1):
                    for c in range(4):
                        act.wait_ge(up_done, (m + u) * 4 + c + 1)
                        A(gh[u][:, c, :], (T + P)[c][:, 0:SC], ACT.Gelu, bias=vf[:, layer, 4 + c:5 + c]).then_inc(gelu_done, 1)

            steps(act, body)

        @block.gpsimd
        def _(pool):
            TT = nc.gpsimd.tensor_tensor

            def body(layer, s, q, wraps):
                n = layer * NS + s * 4 + q
                m = n * 2
                for i in range(16 + PROB_LAG):
                    if i < 16:
                        pool.wait_ge(max_ready, m * 8 + i + 1)
                        TT(s2[i % R][:], s1[i % R][:], mx[i % R][:].unsqueeze(2).broadcast_to([128, NH, WT]),
                           ALU.subtract).then_inc(shifted, 1)
                    if i >= PROB_LAG:
                        j = i - PROB_LAG
                        if j >= RP:
                            pool.wait_ge(transposed, m * 8 + j - RP + 1)
                        pool.wait_ge(rcp_ready, m * 8 + j + 1)
                        TT(pn[j % RP][:, :, 0:WT], ex[j % R][:], rc[j % R][:].unsqueeze(2).broadcast_to([128, NH, WT]),
                           ALU.mult).then_inc(probs, 1)

            pool.wait_ge(consts_ready, 1)
            steps(pool, body)

        @block.vector
        def _(dve):
            V = nc.vector
            for t in vz + qbd + pn + xn:
                V.memset(t[:], 0.0)
            V.memset(eps[:], EPS).then_inc(stored[0], 1)
            V.memset(mx[2][:], 0.0).then_inc(stored[1], 1)
            dve.wait_ge(weights_loaded, 9 * 16)
            dve.wait_ge(setup_pe, 1)
            for l in (0, 1):
                V.tensor_tensor(vf[:, l, 0:3], G[l][:, 0:3], v[:, l * LV + QB:l * LV + VB + 1], ALU.add)
                last = V.tensor_tensor(vf[:, l, 4:8], G[l][:, 4:8], v[:, l * LV + B1:l * LV + B1 + 4], ALU.add)
            last.then_inc(setup_dve, 1)
            dve.wait_ge(setup_pe, 2)
            dve.wait_ge(setup_dve, 1)
            for l in (0, 1):
                V.tensor_scalar(vf[:, l, 0:1], vf[:, l, 0:1], float(HD) ** -0.5, None, ALU.mult)
                V.tensor_tensor(vf[:, l, 3:4], O[l][:, 0:1], v[:, l * LV + PB:l * LV + PB + 1], ALU.add)
                V.tensor_scalar(w[:, l, WQ:WV + 1, :], w[:, l, WQ:WV + 1, :], v[:, l * LV + N1G:l * LV + N1G + 1], None, ALU.mult)
                V.tensor_scalar(w[:, l, W1:W1 + 4, :], w[:, l, W1:W1 + 4, :], v[:, l * LV + N2G:l * LV + N2G + 1], None, ALU.mult)
            for c in (0, 1):
                last = V.tensor_copy(bias[:, c, :], rpb_l[:, 0, :])
            last.then_inc(x_free, 1)
            V.memset(mx[0][:], 0.0).then_inc(x_free, 1)
            dve.wait_ge(x_free, 2)
            V.memset(mx[1][:], 0.0).then_inc(consts_ready, 1)

            def body(layer, s, q, wraps):
                n = layer * NS + s * 4 + q
                m = n * 2
                col = lambda k: v[:, k:k + 1]
                if layer == 0:
                    for u in (0, 1):
                        dve.wait_ge(embedded, m + u + 1)
                        V.tensor_scalar(x[u][:], G[u][:, 0:SC], col(PEB), None, ALU.add).then_inc(emb_biased, 1)
                    for u in (0, 1):
                        dve.wait_ge(rstd_ready["p"], m + u + 1)
                        V.tensor_tensor(lnv[u][:], G[u][:, 0:SC], rs[u][:], ALU.mult).then_inc(pre_affine, 1)
                        dve.wait_ge(pre_affine, m + u + 1)
                        V.tensor_scalar(x[u][:], lnv[u][:], col(PEG), col(PENB), ALU.mult, ALU.add).then_inc(x_ready, 1)
                for u in (0, 1):
                    dve.wait_ge(rstd_ready["1"], m + u + 1)
                    for (a, w0, nw, c0, c1), (b, *_) in zip(windowed(G[u][:, 0:SC], layer), windowed(rs[u][:], layer)):
                        last = V.tensor_tensor(window_cols(xn[u], w0, nw, c0, c1), a, b, ALU.mult)
                    last.then_inc(normed["1"], 1)

                def blockdiag(i):
                    u, a = i // 8, i % 8
                    if a == 0:
                        dve.wait_ge(k_done, m + u + 1)
                    V.scalar_tensor_tensor(kbd[i % 2][:], G[u][:, a * WT:(a + 1) * WT].unsqueeze(1).broadcast_to([128, NH, WT]),
                                           vf[:, layer, 1:2], hm[:].unsqueeze(2).broadcast_to([128, NH, WT]),
                                           ALU.add, ALU.mult).then_inc(kbd_ready, 1)

                blockdiag(0)
                for i in range(16 + SUM_LAG):
                    if i < 15:
                        blockdiag(i + 1)
                    if i < 16:
                        dve.wait_ge(scores, m * 8 + i + 1)
                        V.tensor_tensor(s1[i % R][:].rearrange("p h k -> p (h k)"), P[i % 2][:, 0:NH * WT],
                                        bias[:, 1 if i % 8 == NW - 1 else 0, :], ALU.add).then_inc(biased, 1)
                        dve.wait_ge(biased, m * 8 + i + 1)
                        V.tensor_reduce(mx[i % R][:], s1[i % R][:], AX.X, ALU.max).then_inc(max_ready, 1)
                    if i >= SUM_LAG:
                        j = i - SUM_LAG
                        dve.wait_ge(exps, m * 8 + j + 1)
                        V.tensor_reduce(sm[j % R][:], ex[j % R][:], AX.X, ALU.add).then_inc(sum_ready, 1)
                        dve.wait_ge(sum_ready, m * 8 + j + 1)
                        V.reciprocal(rc[j % R][:], sm[j % R][:]).then_inc(rcp_ready, 1)
                for u in (0, 1):
                    dve.wait_ge(proj_biased, m + u + 1)
                    for a, w0, nw, c0, c1 in windowed(x[u][:], layer):
                        last = V.tensor_tensor(a, window_cols(lnv[u], w0, nw, c0, c1), a, ALU.add)
                    last.then_inc(res_added, 1)
                for u in (0, 1):
                    dve.wait_ge(rstd_ready["2"], m + u + 1)
                    V.tensor_tensor(xn[u][:, 0:SC], G[u][:, 0:SC], rs[u][:], ALU.mult).then_inc(normed["2"], 1)
                for u in (0, 1):
                    dve.wait_ge(down_done, m + u + 1)
                    dve.wait_ge(stored[u], n * 32 + 1)
                    V.scalar_tensor_tensor(xo[u][:], O[u][:, 0:SC], col(layer * LV + B2), x[u][:],
                                           ALU.add, ALU.add).then_inc(x_free, 1)

            def between(k):
                dve.wait_ge(x_free, 2 * (NS if k == 0 else NS + 4 * (NW - 1)) + 2)
                for c in (0, 1):
                    last = V.tensor_tensor(bias[:, c, :], rpb_l[:, 1, :], am[:, 2 * k + c, :], ALU.add)
                last.then_inc(bias_set, 1)
                dve.wait_ge(bias_set, k + 1)

            steps(dve, body, between)


ROW = GRID * HB
HSCALE = 4096.0
WSCALE = 256.0
T16 = 16
NBLK = S // T16


def prepare(nc, consts, tok, txt, xparts, resid):
    Q = 4
    with ExitStack() as ctx:
        def sb(name, shape, dt=F32):
            return ctx.enter_context(nc.sbuf_tensor("b_" + name, shape, dt))

        def sem(name):
            return ctx.enter_context(nc.semaphore("b_" + name))

        center, mean = sb("center", [128, 128]), sb("mean", [128, 128])
        eps = sb("eps", [128, 2])
        each = lambda name, dt=F32: [sb(f"{name}{u}", [128, ROW], dt) for u in range(Q)]
        x, sq, l1, l2, r1, r2, xs, res = (each(k) for k in ("x", "sq", "l1", "l2", "r1", "r2", "xs", "res"))
        xa, xb = each("xa", F16), each("xb", F16)
        G = [ctx.enter_context(nc.psum_tensor(f"b_G{u}", [128, 512], F32)) for u in range(Q)]
        O = [ctx.enter_context(nc.psum_tensor(f"b_O{u}", [128, 512], F32)) for u in range(Q)]
        consts_loaded, ready = sem("consts_loaded"), sem("ready")
        loaded = [sem(f"loaded{u}") for u in range(Q)]
        stored = [sem(f"stored{u}") for u in range(Q)]
        centered, squared, var_ready, logs, rstd, hi, full, norm1, done = (
            sem(k) for k in ("centered", "squared", "var_ready", "logs", "rstd", "hi", "full", "norm1", "done"))
        block = ctx.enter_context(nc.Block())

        def tiles(eng, body):
            with eng.Fori(0, GRID // Q) as n:
                body(n, range(Q), GRID)
            body(GRID // Q, (0,), NTXT)

        def by_image(t, nt):
            return t[:, 0:HB * nt].rearrange("p (b t) -> p t b", t=nt)

        def by_token(t, nt):
            return t[:, 0:HB * nt].rearrange("p (t b) -> p t b", b=HB)

        @block.sync
        def _(sp):
            sp.dma_start(center[:], consts[1]).then_inc(consts_loaded, 16)
            sp.dma_start(mean[:], consts[2]).then_inc(consts_loaded, 16)
            rows = tok.rearrange("p (b t) -> p b t", b=HB)

            def load(tile, u, nt):
                src = rows[:, :, bass.ds(tile * GRID, nt)] if nt == GRID else txt.rearrange("p (b t) -> p b t", b=HB)
                sp.dma_start(x[u][:, 0:HB * nt].rearrange("p (b t) -> p b t", b=HB), src).then_inc(loaded[u], 16)

            def store(tile, u, nt):
                sp.wait_ge(done, tile + 1)
                at = bass.ds(tile * ROW, HB * nt)
                for dst, t in ((xparts[0], xa[u]), (xparts[1], xb[u]), (resid, res[u])):
                    sp.dma_start(dst[:, at], t[:, 0:HB * nt]).then_inc(stored[u], 16)

            for u in range(Q):
                load(u, u, GRID)
            with sp.Fori(0, GRID // Q - 1) as n:
                for u in range(Q):
                    store(n * Q + u, u, GRID)
                    load(n * Q + Q + u, u, GRID)
            for u in range(Q):
                store(GRID - Q + u, u, GRID)
                if u == 0:
                    load(GRID, 0, NTXT)
            store(GRID, 0, NTXT)
            for u in range(Q):
                sp.wait_ge(stored[u], 48 * (GRID // Q + (u == 0)) + 1)

        @block.tensor
        def _(pe):
            pe.wait_ge(consts_loaded, 32)

            def body(n, us, nt):
                m, w = n * Q, HB * nt
                for u in us:
                    pe.wait_ge(loaded[u], 16 * n + 16)
                    nc.tensor.matmul(G[u][:, 0:w], center[:], x[u][:, 0:w], start=True, stop=True).then_inc(centered, 1)
                for u in us:
                    pe.wait_ge(squared, m + u + 1)
                    nc.tensor.matmul(O[u][:, 0:w], mean[:], sq[u][:, 0:w], start=True, stop=True).then_inc(var_ready, 1)

            tiles(pe, body)

        @block.scalar
        def _(act):
            A = nc.scalar.activation
            act.wait_ge(ready, 1)
            act.preload_act_table_set(LN_EXP)

            def body(n, us, nt):
                m, w = n * Q, HB * nt
                for u in us:
                    act.wait_ge(centered, m + u + 1)
                    A(sq[u][:, 0:w], G[u][:, 0:w], ACT.Square).then_inc(squared, 1)
                for u in us:
                    act.wait_ge(var_ready, m + u + 1)
                    A(l1[u][:, 0:w], O[u][:, 0:w], ACT.Ln, bias=eps[:, 0:1])
                    A(l2[u][:, 0:w], O[u][:, 0:w], ACT.Ln, bias=eps[:, 1:2], scale=1.0 + EPS).then_inc(logs, 1)
                    act.wait_ge(logs, m + u + 1)
                    A(r1[u][:, 0:w], l1[u][:, 0:w], ACT.Exp, scale=-0.5)
                    A(r2[u][:, 0:w], l2[u][:, 0:w], ACT.Exp, scale=-0.5).then_inc(rstd, 1)

            tiles(act, body)

        @block.vector
        def _(dve):
            V = nc.vector
            V.memset(eps[:, 0:1], EPS)
            V.memset(eps[:, 1:2], EPS * EPS)
            for u in range(Q):
                V.memset(l1[u][:, 0:1], 0.0).then_inc(stored[u], 1)
            V.memset(res[0][:], 0.0).then_inc(ready, 1)
            dve.wait_ge(ready, 1)

            def body(n, us, nt):
                m = n * Q
                for u in us:
                    dve.wait_ge(rstd, m + u + 1)
                    dve.wait_ge(stored[u], n * 48 + 1)
                    c = by_image(G[u], nt)
                    V.scalar_tensor_tensor(by_token(xa[u], nt), c, HSCALE, by_image(r2[u], nt), ALU.mult, ALU.mult).then_inc(hi, 1)
                    V.scalar_tensor_tensor(by_token(xs[u], nt), c, HSCALE, by_image(r2[u], nt), ALU.mult, ALU.mult).then_inc(full, 1)
                    V.tensor_tensor(by_token(l1[u], nt), c, by_image(r1[u], nt), ALU.mult).then_inc(norm1, 1)
                    dve.wait_ge(full, m + u + 1)
                    V.tensor_tensor(xb[u][:, 0:HB * nt], xs[u][:, 0:HB * nt], xa[u][:, 0:HB * nt], ALU.subtract)
                    dve.wait_ge(norm1, m + u + 1)
                    V.tensor_tensor(by_token(res[u], nt), by_token(l1[u], nt), by_image(x[u], nt), ALU.add).then_inc(done, 1)

            tiles(dve, body)


def gru(nc, consts, wih, whh, gvec, xparts, hist):
    B, T = NIMG, T16
    with ExitStack() as ctx:
        def sb(name, shape, dt=F32):
            return ctx.enter_context(nc.sbuf_tensor("g_" + name, shape, dt))

        def sem(name):
            return ctx.enter_context(nc.semaphore("g_" + name))

        wi = sb("wi", [128, 2, 3, C])
        wh = sb("wh", [128, 3, 128])
        vecs = sb("vecs", [128, 8])
        ident = sb("ident", [128, 128])
        ident_s = sb("ident_s", [128, 128], F16)
        bias = sb("bias", [128, 4])
        gb = vecs[:, 1:8]
        wi_f = sb("wi_f", [128, 2, 3, C])
        wi1 = sb("wi1", [128, 2, 2, 3, C], F16)
        wi2 = sb("wi2", [128, 2, 2, 3, C], F16)
        wh1, wh2 = sb("wh1", [128, 3, 128], F16), sb("wh2", [128, 3, 128], F16)
        bias_f = sb("bias_f", [128, 4, T * B])
        bias1, bias2 = sb("bias1", [128, 4, T * B], F16), sb("bias2", [128, 4, T * B], F16)
        x = sb("x", [128, 2, 2, 2, T, HB], F16)
        h = sb("h", [128, 2, T, B])
        zero = sb("zero", [128, B], F16)
        rz, pre_n = sb("rz", [128, 2, B, 2]), sb("pre_n", [128, B, 2])
        n_, omz, zh, zn = (sb(k, [128, B]) for k in ("n", "omz", "zh", "zn"))
        one_s = sb("one_s", [128, 1])
        zh1, zh2, zn1, zn2 = (sb(k, [128, B], F16) for k in ("zh1", "zh2", "zn1", "zn2"))
        RZ = [ctx.enter_context(nc.psum_tensor(f"g_RZ{u}", [128, 2, T, B], F32)) for u in (0, 1)]
        NX = [ctx.enter_context(nc.psum_tensor(f"g_NX{u}", [128, T, B, 2], F32)) for u in (0, 1)]
        BP = ctx.enter_context(nc.psum_tensor("g_BP", [128, 512], F32))

        weights_loaded, bias_products, link, ready = sem("weights_loaded"), sem("bias_products"), sem("link"), sem("ready")
        x_loaded = [sem("x_loaded0"), sem("x_loaded1")]
        h_stored, h_ready = sem("h_stored"), sem("h_ready")
        gates_ready, nh_ready, rz_ready = sem("gates_ready"), sem("nh_ready"), sem("rz_ready")
        pre_n_ready, n_ready = sem("pre_n_ready"), sem("n_ready")
        zh_ready, zh1_ready, zh2_ready, zn1_ready, zn2_ready, zn_ready = (
            sem(k) for k in ("zh_ready", "zh1_ready", "zh2_ready", "zn1_ready", "zn2_ready", "zn_ready"))
        block = ctx.enter_context(nc.Block())

        def blocks(eng, body):
            body(0, True, False)
            with eng.Fori(1, NBLK // 2 - 1) as i:
                body(i, False, False)
            body(NBLK // 2 - 1, False, True)

        flat = lambda t: t.rearrange("p a b -> p (a b)")

        @block.sync
        def _(sp):
            for dst, src in ((wi[:].rearrange("p a b c -> p (a b c)"), wih), (flat(wh[:]), whh), (vecs[:], gvec),
                             (ident[:], consts[0])):
                sp.dma_start(dst, src).then_inc(weights_loaded, 16)

            def load(k, u):
                for p in (0, 1):
                    sp.dma_start(flat(x[:, u, 0, p]), xparts[p][:, bass.ds(k * (T * HB), T * HB)]).then_inc(x_loaded[u], 16)
                    sp.dma_start(flat(x[:, u, 1, p]), xparts[p][:, bass.ds((NBLK - 1 - k) * (T * HB), T * HB)])\
                        .then_inc(x_loaded[u], 16)

            load(0, 0)
            load(1, 1)

            def body(i, first, last):
                for u in (0, 1):
                    k = i * 2 + u
                    sp.wait_ge(h_ready, (k + 1) * T)
                    sp.dma_start(hist[:, bass.ds(k * (T * B), T * B)], flat(h[:, u])).then_inc(h_stored, 16)
                    if not last:
                        load(k + 2, u)

            blocks(sp, body)
            sp.wait_ge(h_stored, 16 * NBLK)

        PROJ = [(g, d, half, w, p) for g in range(3) for d in (0, 1) for half in (0, 1)
                for w, p in ((wi1, 0), (wi2, 0), (wi1, 1))]

        @block.tensor
        def _(pe):
            def mm(dst, a, b, start=False):
                return nc.tensor.matmul(dst, a, b, start=start, stop=True, skip_group_check=True)

            pe.wait_ge(weights_loaded, 4 * 16)
            for d in (0, 1):
                for g in range(3):
                    last = mm(BP[C * d:C * d + C, g:g + 1], wi[0:C, d, g, :], gb[0:C, 6:7], start=True)
            last.then_inc(bias_products, 1)
            pe.wait_ge(ready, 1)

            def set_biases(u):
                for bank, c in ((RZ[u], 0), (NX[u], 2)):
                    dst = bank[:].rearrange("p a b c -> p (a b c)")
                    mm(dst, ident_s[:], flat(bias1[:, c:c + 2]), start=True)
                    mm(dst, ident_s[:], flat(bias2[:, c:c + 2]))

            def project(u, i):
                g, d, half, w, p = PROJ[i]
                dst = (RZ[u][:, g] if g < 2 else NX[u][:, :, :, 1])[C * d:C * d + C, :, HB * half:HB * half + HB]
                src = x[:, u, d, p]
                return mm(dst, w[:, half, d, g, :], src[:, ::-1, :] if d else src)

            def state(part, u, j, low, last=False):
                for g, dst in enumerate((RZ[u][:, 0, j], RZ[u][:, 1, j], NX[u][:, j, :, 0])):
                    m = mm(dst, wh1[:, g, :], part[:])
                    if not low:
                        m = mm(dst, wh2[:, g, :], part[:])
                    if last and g == 1:
                        m.then_inc(gates_ready, 1)
                if last:
                    m.then_inc(nh_ready, 1)

            pe.wait_ge(x_loaded[0], 64)
            set_biases(0)
            for i in range(len(PROJ)):
                m = project(0, i)
            m.then_inc(gates_ready, 1)
            mm(NX[0][:, 0, :, 0], wh1[:, 2, :], zero[:]).then_inc(nh_ready, 1)

            def body(i, first, last):
                for u in (0, 1):
                    k = i * 2 + u
                    more = not (last and u == 1)
                    for j in range(T):
                        s = k * T + j
                        if more and j == 0:
                            pe.wait_ge(x_loaded[1 - u], (i + 1 + u) * 64)
                            set_biases(1 - u)
                        if more and j > 0:
                            for q in range(3 * (j - 1), min(3 * j, len(PROJ))):
                                project(1 - u, q)
                        if more or j < T - 1:
                            to = (u, j + 1) if j < T - 1 else (1 - u, 0)
                            pe.wait_ge(zh1_ready, s + 1)
                            state(zh1, *to, low=False)
                            pe.wait_ge(zh2_ready, s + 1)
                            state(zh2, *to, low=True)
                            pe.wait_ge(zn1_ready, s + 1)
                            state(zn1, *to, low=False)
                            pe.wait_ge(zn2_ready, s + 1)
                            state(zn2, *to, low=True, last=True)

            blocks(pe, body)

        @block.scalar
        def _(act):
            unscale = 1.0 / (HSCALE * WSCALE)

            def body(i, first, last):
                for u in (0, 1):
                    for j in range(T):
                        s = (i * 2 + u) * T + j
                        act.wait_ge(gates_ready, s + 1)
                        nc.scalar.activation(rz[:, :, :, 1], RZ[u][:, :, j, :], ACT.Sigmoid, scale=unscale).then_inc(rz_ready, 1)
                        act.wait_ge(rz_ready, s + 1)
                        nc.scalar.activation(omz[:], rz[:, 1, :, 1], ACT.Identity, scale=-HSCALE, bias=one_s[:])
                        act.wait_ge(pre_n_ready, s + 1)
                        nc.scalar.activation(n_[:], pre_n[:, :, 1], ACT.Tanh, scale=unscale).then_inc(n_ready, 1)

            blocks(act, body)

        @block.vector
        def _(dve):
            V = nc.vector
            count = [0]

            def chain(op):
                count[0] += 1
                op.then_inc(link, 1)
                dve.wait_ge(link, count[0])

            dve.wait_ge(weights_loaded, 4 * 16)
            for t in (wi1, wi2, h, zero, bias_f, rz):
                chain(V.memset(t[:], 0.0))
            chain(V.memset(one_s[:], HSCALE))
            dve.wait_ge(bias_products, 1)
            chain(V.tensor_tensor(bias[:, 0:3], BP[:, 0:3], gb[:, 0:3], ALU.add))
            chain(V.tensor_tensor(bias[:, 0:2], bias[:, 0:2], gb[:, 3:5], ALU.add))
            chain(V.tensor_copy(bias[:, 3:4], gb[:, 5:6]))
            chain(V.tensor_scalar(bias[:], bias[:], WSCALE, None, ALU.mult))
            chain(V.tensor_scalar(ident_s[:], ident[:], HSCALE, None, ALU.mult))
            chain(V.tensor_scalar(wi_f[:], wi[:], vecs[:, 0:1], WSCALE, ALU.mult, ALU.mult))
            chain(V.tensor_scalar(wh[:], wh[:], WSCALE, None, ALU.mult))
            for half in (0, 1):
                r = slice(C * half, C * half + C)
                chain(V.tensor_copy(wi1[r, half], wi_f[r]))
                chain(V.tensor_tensor(wi2[r, half], wi_f[r], wi1[r, half], ALU.subtract))
            chain(V.tensor_copy(wh1[:], wh[:]))
            chain(V.tensor_tensor(wh2[:], wh[:], wh1[:], ALU.subtract))
            for q in (0, 1):
                chain(V.tensor_scalar(bias_f[:, q, :], bias_f[:, q, :], bias[:, q:q + 1], None, ALU.add))
            side = flat(bias_f[:, 2:4]).rearrange("p (c e) -> p c e", e=2)
            for e, q in ((0, 3), (1, 2)):
                chain(V.tensor_scalar(side[:, :, e], side[:, :, e], bias[:, q:q + 1], None, ALU.add))
            chain(V.tensor_copy(bias1[:], bias_f[:]))
            V.tensor_tensor(bias2[:], bias_f[:], bias1[:], ALU.subtract).then_inc(ready, 1)

            def body(i, first, last):
                for u in (0, 1):
                    k = i * 2 + u
                    for j in range(T):
                        s = k * T + j
                        before = h[:, u, j - 1] if j else h[:, 1 - u, T - 1]
                        dve.wait_ge(rz_ready, s + 1)
                        dve.wait_ge(nh_ready, s + 1)
                        V.tensor_tensor_scan(pre_n[:].rearrange("p b e -> p (b e)"), rz[:, 0].rearrange("p b e -> p (b e)"),
                                             NX[u][:, j].rearrange("p b e -> p (b e)"), 0.0, ALU.mult, ALU.add)\
                            .then_inc(pre_n_ready, 1)
                        if not (first and s == 0):
                            dve.wait_ge(h_ready, s)
                        V.tensor_tensor(zh1[:], rz[:, 1, :, 1], before, ALU.mult).then_inc(zh1_ready, 1)
                        V.tensor_tensor(zh[:], rz[:, 1, :, 1], before, ALU.mult).then_inc(zh_ready, 1)
                        dve.wait_ge(zh_ready, s + 1)
                        V.tensor_tensor(zh2[:], zh[:], zh1[:], ALU.subtract).then_inc(zh2_ready, 1)
                        dve.wait_ge(n_ready, s + 1)
                        V.tensor_tensor(zn1[:], n_[:], omz[:], ALU.mult).then_inc(zn1_ready, 1)
                        V.tensor_tensor(zn[:], n_[:], omz[:], ALU.mult).then_inc(zn_ready, 1)
                        dve.wait_ge(zn_ready, s + 1)
                        V.tensor_tensor(zn2[:], zn[:], zn1[:], ALU.subtract).then_inc(zn2_ready, 1)
                        if j == 0 and not first:
                            dve.wait_ge(h_stored, 16 * (k - 1))
                        V.tensor_tensor(h[:, u, j], zn[:], zh[:], ALU.add).then_inc(h_ready, 1)

            blocks(dve, body)


NE = 8
TT = 48
TC = TT * HB
CH = TC // 128
MSTEP = S // TT // 2
MV_OB, MV_GB, MV_B1 = 0, 1, 2


def mixture(nc, consts, gru_w, out_w, router, wexp, b2w, sel_c, mvec, low_c, rank_c, hist, resid, out):
    with ExitStack() as ctx:
        def sb(name, shape, dt=F32):
            return ctx.enter_context(nc.sbuf_tensor("m_" + name, shape, dt))

        def sem(name):
            return ctx.enter_context(nc.semaphore("m_" + name))

        def bank(name):
            return ctx.enter_context(nc.psum_tensor("m_" + name, [128, 512], F32))

        two = lambda name, shape: [sb(f"{name}{u}", shape) for u in (0, 1)]
        ident, center, mean = sb("ident", [128, 128]), sb("center", [128, 128]), sb("mean", [128, 128])
        gw = sb("gw", [128, 3, C])
        ow, rw, we = sb("ow", [128, 128]), sb("rw", [128, 2 * NE]), sb("we", [128, NE, 2, 128])
        bw, sel = sb("bw", [2 * NE, 128]), sb("sel", [2 * NE, NE, 128])
        mv, low, rank_at = sb("mv", [128, 10]), sb("low", [128, NE, NE]), sb("rank_at", [128, NE])
        eps = sb("eps", [128, 1])
        fr, rev = two("fr", [128, TT, NIMG]), two("rev", [128, TT, NIMG])
        res, th, p = two("res", [128, TC]), two("th", [128, TC]), two("p", [128, TC])
        h2, sq, lnv, rs, xn, base = (two(k, [128, TC]) for k in ("h2", "sq", "lnv", "rs", "xn", "base"))
        G6 = CH * 2
        lg, lx, lexp, rank, chosen, comb = (two(k, [128, G6, NE]) for k in ("lg", "lx", "lexp", "rank", "chosen", "comb"))
        beat = two("beat", [128, G6, NE, NE])
        rk2 = two("rk2", [128, G6, NE])
        lmx, lsum, lrc = (two(k, [128, G6]) for k in ("lmx", "lsum", "lrc"))
        ct = two("ct", [2 * NE, TC])
        hg, hm = two("hg", [128, TC]), two("hm", [128, TC])
        y = two("y", [128, TC])
        A_, B_, U, W = ([bank(f"{k}{u}") for u in (0, 1)] for k in "ABUW")

        weights_loaded, scaled, ready = sem("weights_loaded"), sem("scaled"), sem("ready")
        loaded, stored = [sem("loaded0"), sem("loaded1")], [sem("stored0"), sem("stored1")]
        names = ("aligned gate_done tanh_done gated mixed summed centered squared var_ready log_ready rstd_ready normed "
                 "based routed logits_kept max_ready less_max beat_ready beat_upper ranks_a rank_ready lexp_ready chosen_ready "
                 "kept_exp sum_ready rcp_ready comb_ready comb_t comb_kept up_done spread gelu_done weighted down_done done").split()
        on = {k: sem(k) for k in names}
        block = ctx.enter_context(nc.Block())

        @block.sync
        def _(sp):
            flat = lambda t: t.rearrange("p a b -> p (a b)")
            for dst, src in ((ident[:], consts[0]), (center[:], consts[1]), (mean[:], consts[2]), (flat(gw[:]), gru_w),
                             (ow[:], out_w), (rw[:], router), (we[:].rearrange("p a b c -> p (a b c)"), wexp), (bw[:], b2w),
                             (flat(sel[:]), sel_c), (mv[:], mvec), (flat(low[:]), low_c), (rank_at[:], rank_c)):
                sp.dma_start(dst, src).then_inc(weights_loaded, 16)

            def load(t, u):
                sp.dma_start(flat(fr[u][0:C]), hist[0:C, bass.ds(t * (TT * NIMG), TT * NIMG)]).then_inc(loaded[u], 16)
                sp.dma_start(flat(rev[u][C:128]), hist[C:128, bass.ds((2 * MSTEP - 1 - t) * (TT * NIMG), TT * NIMG)])\
                    .then_inc(loaded[u], 16)
                sp.dma_start(res[u][:], resid[:, bass.ds(t * TC, TC)]).then_inc(loaded[u], 16)

            def body(n, last):
                for u in (0, 1):
                    t = n * 2 + u
                    sp.wait_ge(on["summed"], t + 1)
                    if not last:
                        load(t + 2, u)
                for u in (0, 1):
                    t = n * 2 + u
                    sp.wait_ge(on["done"], t + 3)
                    sp.dma_start(out[:, bass.ds(t * TC, TC)], y[u][:]).then_inc(stored[u], 16)

            load(0, 0)
            load(1, 1)
            with sp.Fori(0, MSTEP - 1) as n:
                body(n, False)
            body(MSTEP - 1, True)
            for u in (0, 1):
                sp.wait_ge(stored[u], 16 * MSTEP + 1)

        @block.gpsimd
        def _(pool):
            with pool.Fori(0, MSTEP) as n:
                m = n * 2
                for u in (0, 1):
                    pool.wait_ge(on["normed"], m + u + 1)
                    nc.gpsimd.tensor_tensor(base[u][:], h2[u][:], xn[u][:], ALU.add).then_inc(on["based"], 1)

        @block.tensor
        def _(pe):
            def mm(dst, a, b, start=True, stop=True, **k):
                return nc.tensor.matmul(dst, a, b, start=start, stop=stop, **k)

            pe.wait_ge(ready, 1)
            with pe.Fori(0, MSTEP) as n:
                m = n * 2
                pe.wait_ge(on["done"], m + 2)
                for u in (0, 1):
                    pe.wait_ge(loaded[u], n * 48 + 48)
                    pe.wait_ge(on["aligned"], m + u + 1)
                    for i, bk in ((0, A_[u]), (1, B_[u])):
                        for half in (0, 1):
                            last = mm(bk[C * half:C * half + C, 0:TC], gw[:, i, :], fr[u][:, :, HB * half:HB * half + HB])
                    last.then_inc(on["gate_done"], 1)
                for u in (0, 1):
                    for half in (0, 1):
                        mm(U[u][C * half:C * half + C, 0:TC], gw[:, 2, :], fr[u][:, :, HB * half:HB * half + HB])
                    pe.wait_ge(on["gated"], m + u + 1)
                    mm(U[u][:, 0:TC], ow[:], p[u][:], start=False, skip_group_check=True).then_inc(on["mixed"], 1)
                for u in (0, 1):
                    pe.wait_ge(on["summed"], m + u + 1)
                    mm(A_[u][:, 0:TC], center[:], h2[u][:]).then_inc(on["centered"], 1)
                for u in (0, 1):
                    pe.wait_ge(on["squared"], m + u + 1)
                    mm(B_[u][:, 0:TC], mean[:], sq[u][:]).then_inc(on["var_ready"], 1)
                for u in (0, 1):
                    pe.wait_ge(on["normed"], m + u + 1)
                    for c in range(CH):
                        last = mm(A_[u][:, 2 * NE * c:2 * NE * (c + 1)], xn[u][:, 128 * c:128 * (c + 1)], rw[:])
                    last.then_inc(on["routed"], 1)
                for u in (0, 1):
                    pe.wait_ge(on["comb_ready"], m + u + 1)
                    for c in range(CH):
                        last = nc.tensor.transpose(A_[u][0:2 * NE, 128 * c:128 * (c + 1)],
                                                   comb[u][:, 2 * c:2 * c + 2, :].rearrange("p a b -> p (a b)"), ident[:])
                    last.then_inc(on["comb_t"], 1)
                for i in range(2 * NE + 2):
                    if i >= 2:
                        e, u = (i - 2) // 2, i % 2
                        pe.wait_ge(on["weighted"], m * NE + i - 2 + 1)
                        last = mm(B_[u][:, 0:TC], we[:, e, 1, :], hm[u][:], start=False, stop=e == NE - 1)
                        if e == NE - 1:
                            last.then_inc(on["down_done"], 1)
                    if i < 2 * NE:
                        e, u = i // 2, i % 2
                        if e == 0:
                            pe.wait_ge(on["comb_kept"], m + u + 1)
                            mm(B_[u][:, 0:TC], bw[:], ct[u][:], stop=False)
                        mm(U[u][:, 0:TC], we[:, e, 0, :], xn[u][:]).then_inc(on["up_done"], 1)
                        mm(W[u][:, 0:TC], sel[:, e, :], ct[u][:]).then_inc(on["spread"], 1)

        @block.scalar
        def _(act):
            A = nc.scalar.activation
            act.wait_ge(ready, 1)
            with act.Fori(0, MSTEP) as n:
                m = n * 2
                for u in (0, 1):
                    act.wait_ge(loaded[u], n * 48 + 48)
                    A(fr[u][C:128], rev[u][C:128, ::-1, :], ACT.Copy).then_inc(on["aligned"], 1)
                for u in (0, 1):
                    act.wait_ge(on["gate_done"], m + u + 1)
                    A(th[u][:], A_[u][:, 0:TC], ACT.Tanh, scale=0.5, bias=mv[:, MV_GB:MV_GB + 1]).then_inc(on["tanh_done"], 1)
                act.preload_act_table_set(LN_EXP)
                for u in (0, 1):
                    act.wait_ge(on["centered"], m + u + 1)
                    A(sq[u][:], A_[u][:, 0:TC], ACT.Square).then_inc(on["squared"], 1)
                for u in (0, 1):
                    act.wait_ge(on["var_ready"], m + u + 1)
                    A(lnv[u][:], B_[u][:, 0:TC], ACT.Ln, bias=eps[:]).then_inc(on["log_ready"], 1)
                    act.wait_ge(on["log_ready"], m + u + 1)
                    A(rs[u][:], lnv[u][:], ACT.Exp, scale=-0.5).then_inc(on["rstd_ready"], 1)
                for u in (0, 1):
                    act.wait_ge(on["less_max"], m + u + 1)
                    A(lexp[u][:], lx[u][:], ACT.Exp).then_inc(on["lexp_ready"], 1)
                for u in (0, 1):
                    act.wait_ge(on["comb_t"], m + u + 1)
                    A(ct[u][:], A_[u][0:2 * NE, 0:TC], ACT.Copy).then_inc(on["comb_kept"], 1)
                for i in range(2 * NE):
                    e, u = i // 2, i % 2
                    act.wait_ge(on["up_done"], m * NE + i + 1)
                    A(hg[u][:], U[u][:, 0:TC], ACT.Gelu, bias=mv[:, MV_B1 + e:MV_B1 + e + 1]).then_inc(on["gelu_done"], 1)

        @block.vector
        def _(dve):
            V = nc.vector
            dve.wait_ge(weights_loaded, 12 * 16)
            V.memset(eps[:], EPS).then_inc(stored[0], 1)
            V.memset(lmx[0][:], 0.0).then_inc(stored[1], 1)
            V.tensor_scalar(gw[:, 0, :], gw[:, 0, :], 1.0 / HSCALE, None, ALU.mult)
            V.tensor_scalar(gw[:, 1, :], gw[:, 1, :], 0.5 / HSCALE, None, ALU.mult)
            V.tensor_scalar(gw[:, 2, :], gw[:, 2, :], 1.0 / HSCALE, None, ALU.mult)
            V.tensor_scalar(mv[:, MV_GB:MV_GB + 1], mv[:, MV_GB:MV_GB + 1], 0.5, None, ALU.mult).then_inc(on["done"], 1)
            V.memset(hg[0][:, 0:1], 0.0).then_inc(on["done"], 1)
            dve.wait_ge(on["done"], 2)
            V.memset(hg[1][:, 0:1], 0.0).then_inc(ready, 1)
            dve.wait_ge(ready, 1)
            bc = lambda t: t.unsqueeze(2).broadcast_to([128, G6, NE])
            with dve.Fori(0, MSTEP) as n:
                m = n * 2
                for u in (0, 1):
                    dve.wait_ge(on["tanh_done"], m + u + 1)
                    V.scalar_tensor_tensor(p[u][:], th[u][:], 1.0, B_[u][:, 0:TC], ALU.add, ALU.mult).then_inc(on["gated"], 1)
                for u in (0, 1):
                    dve.wait_ge(on["mixed"], m + u + 1)
                    V.scalar_tensor_tensor(h2[u][:], U[u][:, 0:TC], mv[:, MV_OB:MV_OB + 1], res[u][:], ALU.add, ALU.add)\
                        .then_inc(on["summed"], 1)
                for u in (0, 1):
                    dve.wait_ge(on["rstd_ready"], m + u + 1)
                    V.tensor_tensor(xn[u][:], A_[u][:, 0:TC], rs[u][:], ALU.mult).then_inc(on["normed"], 1)
                for u in (0, 1):
                    dve.wait_ge(on["routed"], m + u + 1)
                    V.tensor_copy(lg[u][:].rearrange("p a b -> p (a b)"), A_[u][:, 0:G6 * NE]).then_inc(on["logits_kept"], 1)
                    dve.wait_ge(on["logits_kept"], m + u + 1)
                    V.tensor_reduce(lmx[u][:], lg[u][:], AX.X, ALU.max).then_inc(on["max_ready"], 1)
                    V.tensor_tensor(beat[u][:], lg[u][:].unsqueeze(2).broadcast_to([128, G6, NE, NE]),
                                    lg[u][:].unsqueeze(3).broadcast_to([128, G6, NE, NE]), ALU.is_gt).then_inc(on["beat_ready"], 1)
                    dve.wait_ge(on["max_ready"], m + u + 1)
                    V.tensor_tensor(lx[u][:], lg[u][:], bc(lmx[u][:]), ALU.subtract).then_inc(on["less_max"], 1)
                    dve.wait_ge(on["beat_ready"], m + u + 1)
                    V.tensor_tensor(beat[u][:], beat[u][:], low[:].unsqueeze(1).broadcast_to([128, G6, NE, NE]), ALU.mult)\
                        .then_inc(on["beat_upper"], 1)
                    dve.wait_ge(on["beat_upper"], m + u + 1)
                    V.tensor_reduce(rank[u][:], beat[u][:], AX.X, ALU.add)
                    V.tensor_reduce(rk2[u][:], beat[u][:].rearrange("p g e j -> p g j e"), AX.X, ALU.add).then_inc(on["ranks_a"], 1)
                    dve.wait_ge(on["ranks_a"], m + u + 1)
                    V.tensor_tensor(rank[u][:], rank[u][:], rk2[u][:], ALU.subtract).then_inc(on["rank_ready"], 1)
                    dve.wait_ge(on["rank_ready"], m + u + 1)
                    V.tensor_tensor(chosen[u][:], rank[u][:], rank_at[:].unsqueeze(1).broadcast_to([128, G6, NE]), ALU.is_lt)\
                        .then_inc(on["chosen_ready"], 1)
                for u in (0, 1):
                    dve.wait_ge(on["lexp_ready"], m + u + 1)
                    dve.wait_ge(on["chosen_ready"], m + u + 1)
                    V.tensor_tensor(lexp[u][:], lexp[u][:], chosen[u][:], ALU.mult).then_inc(on["kept_exp"], 1)
                    dve.wait_ge(on["kept_exp"], m + u + 1)
                    V.tensor_reduce(lsum[u][:], lexp[u][:], AX.X, ALU.add).then_inc(on["sum_ready"], 1)
                    dve.wait_ge(on["sum_ready"], m + u + 1)
                    V.reciprocal(lrc[u][:], lsum[u][:]).then_inc(on["rcp_ready"], 1)
                    dve.wait_ge(on["rcp_ready"], m + u + 1)
                    V.tensor_tensor(comb[u][:], lexp[u][:], bc(lrc[u][:]), ALU.mult).then_inc(on["comb_ready"], 1)
                for i in range(2 * NE):
                    u = i % 2
                    dve.wait_ge(on["spread"], m * NE + i + 1)
                    dve.wait_ge(on["gelu_done"], m * NE + i + 1)
                    V.tensor_tensor(hm[u][:], hg[u][:], W[u][:, 0:TC], ALU.mult).then_inc(on["weighted"], 1)
                for u in (0, 1):
                    dve.wait_ge(on["down_done"], m + u + 1)
                    dve.wait_ge(on["based"], m + u + 1)
                    dve.wait_ge(stored[u], n * 16 + 1)
                    V.tensor_tensor(y[u][:], B_[u][:, 0:TC], base[u][:], ALU.add).then_inc(on["done"], 1)


def _halves(a):
    return a.reshape((2, HB) + a.shape[1:])


def _dup(a):
    import numpy as np
    return np.concatenate([a, a], 0)


def _diag(a):
    import numpy as np
    z = np.zeros((2, a.shape[0], 2, a.shape[1]), a.dtype)
    z[0, :, 0], z[1, :, 1] = a, a
    return z.reshape(2 * a.shape[0], 2 * a.shape[1])


def swin_inputs(i):
    import numpy as np
    f = np.float32
    x = _halves(i["x"].reshape(NIMG, GRID, 4, GRID, 4))
    patches = x.transpose(0, 3, 5, 1, 2, 4).reshape(32, HB * NTOK)
    blocks, vecs = [], []
    for l in range(2):
        qkv = i["L0_tok_qkv_w"][l]
        blocks += [_diag(qkv[k * C:(k + 1) * C].T) for k in range(3)] + [_diag(i["L0_tok_proj_w"][l].T)]
        blocks += [_diag(i["L0_tok_w1"][l][c * C:(c + 1) * C].T) for c in range(4)]
        blocks += [_diag(i["L0_tok_w2"][l][:, c * C:(c + 1) * C].T) for c in range(4)]
        vecs += [i["L0_tok_" + k][l] for k in ("n1g", "n1b", "n2g", "n2b")]
        vecs += [i["L0_tok_qkv_b"][l][k * C:(k + 1) * C] for k in range(3)] + [i["L0_tok_proj_b"][l], i["L0_tok_b2"][l]]
        vecs += [i["L0_tok_b1"][l][c * C:(c + 1) * C] for c in range(4)]
    vecs += [i["L0_tok_pe_b"], i["L0_tok_pe_ng"], i["L0_tok_pe_nb"]]
    at = np.arange(WT)
    rel = (at[:, None] // WS - at[None] // WS + WS - 1) * (2 * WS - 1) + at[:, None] % WS - at[None] % WS + WS - 1
    part = lambda at: np.where(at < WS - SHIFT, 0, 1)
    row, col = part(at // WS), part(at % WS)
    differ = [np.zeros((WT, WT), bool), col[:, None] != col[None], row[:, None] != row[None]]
    differ.append(differ[1] | differ[2])

    def rows(t):
        z = np.zeros((2, KP, NH * WT), f)
        z[:, :WT] = t.reshape(WT, -1)
        return z.reshape(128, -1)

    rpb = np.concatenate([rows(i["L0_tok_rpb"][l][rel].transpose(0, 2, 1)) for l in range(2)], 1)
    amask = np.concatenate([rows(np.repeat(np.where(d, f(-100), f(0))[:, None], NH, 1)) for d in differ], 1)
    heads = _dup((np.arange(C)[:, None] // HD == np.arange(NH)[None]).astype(f))
    mean = _diag(np.full((C, C), 1.0 / C, f))
    consts = np.stack([np.eye(128, dtype=f), np.eye(128, dtype=f) - mean, mean])
    return {"patches": patches, "wts": np.concatenate(blocks, 1), "pew": _diag(i["L0_tok_pe_w"].reshape(C, 16).T),
            "vec": _dup(np.stack(vecs, 1)), "rpb": rpb, "amask": amask, "hmask": heads, "consts": consts}


def gru_inputs(i):
    import numpy as np
    f = np.float32
    d2 = ("fwd", "rev")
    wih = np.stack([i[f"L0_attn_{d}_w_ih"].reshape(3, C, C) for d in d2])
    wih = _dup(wih.transpose(3, 0, 1, 2).reshape(C, -1))
    whh = np.zeros((2, C, 3, 2, C), f)
    for n, d in enumerate(d2):
        whh[n, :, :, n] = i[f"L0_attn_{d}_w_hh"].reshape(3, C, C).transpose(2, 0, 1)
    bias = [np.concatenate([i[f"L0_attn_{d}_{b}"][g * C:(g + 1) * C] for d in d2]) for b in ("b_ih", "b_hh") for g in range(3)]
    gvec = np.stack([_dup(i["L0_attn_ln_g"])] + bias + [_dup(i["L0_attn_ln_b"])], 1)
    txt = _halves(i["txt"]).transpose(0, 3, 1, 2).reshape(128, HB * NTXT)
    return {"wih": wih, "whh": whh.reshape(128, -1), "gvec": gvec, "txt": txt}


def mixture_inputs(i):
    import numpy as np
    f = np.float32
    eye, zero = np.eye(C, dtype=f), np.zeros((C, C), f)
    ow = i["L0_attn_out_w"].T
    gru_w = np.concatenate([i["L0_attn_gate_w"].T, np.concatenate([eye, -eye]), np.concatenate([zero, ow])], 1)
    wexp = np.concatenate([_diag(i[k][e]) for e in range(NE) for k in ("L0_ffn_w1", "L0_ffn_w2")], 1)
    sel = np.zeros((2, NE, NE, 2, C), f)
    for h in range(2):
        for e in range(NE):
            sel[h, e, e, h] = 1
    mvec = np.stack([_dup(i["L0_attn_out_b"]), _dup(i["L0_attn_gate_b"])] + [_dup(i["L0_ffn_b1"][e]) for e in range(NE)], 1)
    e = np.arange(NE)
    after = (e[None] > e[:, None]).astype(f)
    low = np.repeat(after.reshape(1, -1), 128, 0)
    rank = np.repeat((2 - e).astype(f)[None], 128, 0)
    return {"gru_w": gru_w, "out_w": _diag(ow), "router": _diag(i["L0_ffn_router_w"].T), "wexp": wexp,
            "b2w": _diag(i["L0_ffn_b2"]), "sel_c": sel.reshape(2 * NE, -1), "mvec": mvec, "low_c": low, "rank_c": rank}


def program(nc, a, out):
    dram = lambda name, cols, dt=F32: nc.dram_tensor(name, (128, cols), dt, kind="Internal").ap()
    tok1, tok2 = dram("tok1", HB * NTOK), dram("tok2", HB * NTOK)
    xparts = (dram("x_hi", HB * S, F16), dram("x_lo", HB * S, F16))
    resid, hist = dram("resid", HB * S), dram("hist", NIMG * S)
    swin(nc, a["patches"], a["wts"], a["pew"], a["vec"], a["rpb"], a["amask"], a["hmask"], a["consts"], tok1, tok2)
    prepare(nc, a["consts"], tok2, a["txt"], xparts, resid)
    gru(nc, a["consts"], a["wih"], a["whh"], a["gvec"], xparts, hist)
    mixture(nc, a["consts"], a["gru_w"], a["out_w"], a["router"], a["wexp"], a["b2w"], a["sel_c"], a["mvec"], a["low_c"],
            a["rank_c"], hist, resid, out)


def kernel(**inputs):
    import numpy as np
    import concourse.bacc as bacc
    from concourse.bass_utils import run_bass_kernel_spmd

    i = {k: np.asarray(v) for k, v in inputs.items()}
    arrays = {**swin_inputs(i), **gru_inputs(i), **mixture_inputs(i)}
    arrays = {k: np.ascontiguousarray(v) for k, v in arrays.items()}
    nc = bacc.Bacc("TRN2", target_bir_lowering=False, num_devices=1)
    aps = {k: nc.dram_tensor(k, v.shape, mybir.dt.from_np(v.dtype), kind="ExternalInput").ap() for k, v in arrays.items()}
    out = nc.dram_tensor("out", (128, HB * S), F32, kind="ExternalOutput").ap()
    program(nc, aps, out)
    r = run_bass_kernel_spmd(nc, [arrays], core_ids=[0]).results[0]["out"]
    return r.reshape(2, C, S, HB).transpose(0, 3, 2, 1).reshape(NIMG, S, C)
```

```python
import concourse.bass as bass
from concourse import mybir
from contextlib import ExitStack

F32 = mybir.dt.float32
F16 = mybir.dt.float16
ACT = mybir.ActivationFunctionType
ALU = mybir.AluOpType
AX = mybir.AxisListType

NIMG, HB, C = 16, 8, 64
WS, GRID = 7, 56
SHIFT = WS // 2
NTOK = GRID * GRID
NTXT = 32
S = NTOK + NTXT
NW = GRID // WS
SC = WS * GRID
WT = WS * WS
NH, HD = 8, 8
KP = 64
EPS = 1e-5
LN_EXP = "natural_log_exp_and_others"

N1G, N1B, N2G, N2B, QB, KB, VB, PB, B2, B1 = range(10)
LV = 13
PEB, PEG, PENB = 2 * LV, 2 * LV + 1, 2 * LV + 2
NVEC = 2 * LV + 3
WQ, WK, WV, WP, W1, W2 = 0, 1, 2, 3, 4, 8
LW = 12


def swin(nc, patches, wts, pew, vec, rpb, amask, hmask, consts, tok1, tok2):
    with ExitStack() as ctx:
        def sb(name, shape, dt=F32):
            return ctx.enter_context(nc.sbuf_tensor(name, shape, dt))

        def bank(name):
            return ctx.enter_context(nc.psum_tensor(name, [128, 512], F32))

        def sem(name):
            return ctx.enter_context(nc.semaphore(name))

        w = sb("w", [128, 2, LW, 128])
        pe_w = sb("pe_w", [32, 128])
        v = sb("v", [128, NVEC])
        vf = sb("vf", [128, 2, 8])
        ident = sb("ident", [128, 128])
        center = sb("center", [128, 128])
        mean = sb("mean", [128, 128])
        eps = sb("eps", [128, 1])
        rpb_l = sb("rpb_l", [128, 2, NH * WT])
        am = sb("am", [128, 4, NH * WT])
        bias = sb("bias", [128, 2, NH * WT])
        hm = sb("hm", [128, NH])
        px = [sb(f"px{u}", [32, SC]) for u in (0, 1)]
        x = [sb(f"x{u}", [128, SC]) for u in (0, 1)]
        xo = [sb(f"xo{u}", [128, SC]) for u in (0, 1)]
        sq = [sb(f"sq{u}", [128, SC]) for u in (0, 1)]
        lnv = [sb(f"lnv{u}", [128, SC]) for u in (0, 1)]
        rs = [sb(f"rs{u}", [128, SC]) for u in (0, 1)]
        xn = [sb(f"xn{u}", [128, 512]) for u in (0, 1)]
        qbd = [sb(f"qbd{u}", [128, NW, 128]) for u in (0, 1)]
        vz = [sb(f"vz{u}", [128, NW, 4 * (128 + 2 * HD)]) for u in (0, 1)]
        ot = [sb(f"ot{u}", [128, SC]) for u in (0, 1)]
        gh = [sb(f"gh{u}", [128, 4, SC]) for u in (0, 1)]
        kbd = [sb(f"kbd{r}", [128, NH, WT]) for r in (0, 1)]
        R, RP = 4, 6
        s1 = [sb(f"s1_{r}", [128, NH, WT]) for r in range(R)]
        s2 = [sb(f"s2_{r}", [128, NH, WT]) for r in range(R)]
        ex = [sb(f"ex{r}", [128, NH, WT]) for r in range(R)]
        pn = [sb(f"pn{r}", [128, NH, KP]) for r in range(RP)]
        mx = [sb(f"mx{r}", [128, NH]) for r in range(R)]
        sm = [sb(f"sm{r}", [128, NH]) for r in range(R)]
        rc = [sb(f"rc{r}", [128, NH]) for r in range(R)]
        pt = [sb(f"pt{r}", [128, 4, 128]) for r in (0, 1)]

        G = [bank(f"G{u}") for u in (0, 1)]
        O = [bank(f"O{u}") for u in (0, 1)]
        P = [bank(f"P{u}") for u in (0, 1)]
        T = [bank(f"T{u}") for u in (0, 1)]

        weights_loaded = sem("weights_loaded")
        setup_pe = sem("setup_pe")
        setup_dve = sem("setup_dve")
        consts_ready = sem("consts_ready")
        bias_set = sem("bias_set")
        loaded = [sem(f"loaded{u}") for u in (0, 1)]
        stored = [sem(f"stored{u}") for u in (0, 1)]
        x_free = sem("x_free")
        embedded = sem("embedded")
        emb_biased = sem("emb_biased")
        pre_affine = sem("pre_affine")
        x_ready = sem("x_ready")
        centered = {k: sem(f"centered_{k}") for k in "p12"}
        squared = {k: sem(f"squared_{k}") for k in "p12"}
        var_ready = {k: sem(f"var_ready_{k}") for k in "p12"}
        log_ready = {k: sem(f"log_ready_{k}") for k in "p12"}
        rstd_ready = {k: sem(f"rstd_ready_{k}") for k in "p12"}
        normed = {k: sem(f"normed_{k}") for k in "12"}
        q_done, q_kept = sem("q_done"), sem("q_kept")
        k_done, kbd_ready = sem("k_done"), sem("kbd_ready")
        v_done, v_kept = sem("v_done"), sem("v_kept")
        scores, biased, max_ready, shifted = sem("scores"), sem("biased"), sem("max_ready"), sem("shifted")
        exps, sum_ready, rcp_ready, probs = sem("exps"), sem("sum_ready"), sem("rcp_ready"), sem("probs")
        transposed, pt_kept = sem("transposed"), sem("pt_kept")
        attended, o_kept = sem("attended"), sem("o_kept")
        projected, proj_biased, res_added = sem("projected"), sem("proj_biased"), sem("res_added")
        up_done, gelu_done, down_done = sem("up_done"), sem("gelu_done"), sem("down_done")

        block = ctx.enter_context(nc.Block())
        SUM_LAG, PROB_LAG, T_LAG, AV_LAG = 2, 3, 5, 6
        NS = 2 * 16

        def steps(eng, body, between=None):
            with eng.Fori(0, NW) as s:
                with eng.Fori(0, 4) as q:
                    body(0, s, q, False)
            if between:
                between(0)
            with eng.Fori(0, NW - 1) as s:
                with eng.Fori(0, 4) as q:
                    body(1, s, q, False)
            if between:
                between(1)
            with eng.Fori(0, 4) as q:
                body(1, NW - 1, q, True)

        def windowed(t, layer):
            g = t.rearrange("p (r g) -> p r g", g=GRID)
            if layer == 0:
                return [(g.rearrange("p r (w c) -> p w r c", c=WS), 0, NW, 0, WS)]
            n = NW - 1
            return [(g[:, :, SHIFT:SHIFT + n * WS].rearrange("p r (w c) -> p w r c", c=WS), 0, n, 0, WS),
                    (g[:, :, SHIFT + n * WS:GRID], n, 1, 0, WS - SHIFT),
                    (g[:, :, 0:SHIFT], n, 1, WS - SHIFT, WS)]

        def window_cols(t, w0, nw, c0, c1):
            q = t[:, 0:SC].rearrange("p (w r c) -> p w r c", r=WS, c=WS)[:, w0:w0 + nw, :, c0:c1]
            return q if nw > 1 else q[:, 0]

        @block.sync
        def _(sp):
            for dst, src in ((w[:].rearrange("p a b c -> p (a b c)"), wts), (pe_w[:], pew), (v[:], vec),
                             (rpb_l[:].rearrange("p a b -> p (a b)"), rpb),
                             (am[:].rearrange("p a b -> p (a b)"), amask), (hm[:], hmask),
                             (ident[:], consts[0]), (center[:], consts[1]), (mean[:], consts[2])):
                sp.dma_start(dst, src).then_inc(weights_loaded, 16)

            def ends(layer, s, q, u, wraps):
                head = (WS - SHIFT) * GRID
                base = (q * 2 + u) * NTOK
                a = base + s * SC + (SHIFT * GRID if layer else 0)
                b = base if wraps else a + head
                return (a, 0, head), (b, head, SC)

            def body(layer, s, q, wraps):
                n = layer * NS + s * 4 + q
                for u in (0, 1):
                    sp.wait_ge(x_free, n * 2 + u + 1)
                    src, dst = (patches, px[u]) if layer == 0 else (tok1, x[u])
                    for at, c0, c1 in ends(0, s, q, u, False) if layer == 0 else ends(1, s, q, u, wraps):
                        sp.dma_start(dst[:, c0:c1], src[:, bass.ds(at, c1 - c0)]).then_inc(loaded[u], 16)
                for u in (0, 1):
                    sp.wait_ge(x_free, n * 2 + u + 3)
                    out = tok1 if layer == 0 else tok2
                    for at, c0, c1 in ends(layer, s, q, u, wraps):
                        sp.dma_start(out[:, bass.ds(at, c1 - c0)], xo[u][:, c0:c1]).then_inc(stored[u], 16)

            def between(k):
                if k == 0:
                    for u in (0, 1):
                        sp.wait_ge(stored[u], 32 * NS + 1)

            steps(sp, body, between)
            for u in (0, 1):
                sp.wait_ge(stored[u], 64 * NS + 1)

        @block.tensor
        def _(pe):
            mm = nc.tensor.matmul
            pe.wait_ge(weights_loaded, 9 * 16)
            for l in (0, 1):
                for i, blk in enumerate((WQ, WK, WV)):
                    mm(G[l][:, i:i + 1], w[:, l, blk, :], v[:, l * LV + N1B:l * LV + N1B + 1], start=True, stop=True)
                for i in range(4):
                    last = mm(G[l][:, 4 + i:5 + i], w[:, l, W1 + i, :], v[:, l * LV + N2B:l * LV + N2B + 1],
                              start=True, stop=True)
            last.then_inc(setup_pe, 1)
            pe.wait_ge(setup_dve, 1)
            for l in (0, 1):
                last = mm(O[l][:, 0:1], w[:, l, WP, :], vf[:, l, 2:3], start=True, stop=True)
            last.then_inc(setup_pe, 1)
            pe.wait_ge(consts_ready, 1)

            def norm(k, m, wait_input):
                for u in (0, 1):
                    wait_input(u)
                    mm(G[u][:, 0:SC], center[:], x[u][:], start=True, stop=True).then_inc(centered[k], 1)
                for u in (0, 1):
                    pe.wait_ge(squared[k], m + u + 1)
                    mm(O[u][:, 0:SC], mean[:], sq[u][:], start=True, stop=True).then_inc(var_ready[k], 1)

            def body(layer, s, q, wraps):
                n = layer * NS + s * 4 + q
                m = n * 2
                W = lambda blk: w[:, layer, blk, :]
                for u in (0, 1):
                    pe.wait_ge(loaded[u], n * 32 + 32)
                    if layer == 0:
                        mm(G[u][:, 0:SC], pe_w[:], px[u][:], start=True, stop=True).then_inc(embedded, 1)
                pe.wait_ge(x_free, m + 2)
                if layer == 0:
                    norm("p", m, lambda u: pe.wait_ge(emb_biased, m + u + 1))
                    norm("1", m, lambda u: pe.wait_ge(x_ready, m + u + 1))
                else:
                    norm("1", m, lambda u: None)
                for u in (0, 1):
                    pe.wait_ge(normed["1"], m + u + 1)
                    mm(O[u][:, 0:SC], W(WQ), xn[u][:, 0:SC], start=True, stop=True).then_inc(q_done, 1)
                    mm(G[u][:, 0:SC], W(WK), xn[u][:, 0:SC], start=True, stop=True).then_inc(k_done, 1)
                for u in (0, 1):
                    for b in (0, 1):
                        if u == 1:
                            pe.wait_ge(v_kept, m * 2 + b + 1)
                        for i in range(4):
                            at = (b * 4 + i) * WT
                            last = mm(P[b][0:KP, i * 128:(i + 1) * 128], xn[u][:, at:at + KP], W(WV), start=True, stop=True)
                        last.then_inc(v_done, 1)
                pe.wait_ge(q_kept, m + 2)
                pe.wait_ge(v_kept, m * 2 + 4)
                for i in range(16 + AV_LAG):
                    if i < 16:
                        u, a = i // 8, i % 8
                        pe.wait_ge(kbd_ready, m * 8 + i + 1)
                        mm(P[i % 2][:, 0:NH * WT], qbd[u][:, a, :], kbd[i % 2][:].rearrange("p h k -> p (h k)"),
                           start=True, stop=True).then_inc(scores, 1)
                    if 0 <= i - T_LAG < 16:
                        j = i - T_LAG
                        pe.wait_ge(probs, m * 8 + j + 1)
                        for h in range(4):
                            last = nc.tensor.transpose(T[j % 2][:, h * 128:(h + 1) * 128],
                                                       pn[j % RP][:, 2 * h:2 * h + 2, :].rearrange("p h k -> p (h k)"), ident[:])
                        last.then_inc(transposed, 1)
                    if i >= AV_LAG:
                        j = i - AV_LAG
                        u, a = j // 8, j % 8
                        pe.wait_ge(pt_kept, m * 8 + j + 1)
                        if u == 1 and a % 4 == 0:
                            pe.wait_ge(o_kept, m * 2 + a // 4 + 1)
                        for h in range(4):
                            last = mm(O[a // 4][:, (a % 4) * 128:(a % 4 + 1) * 128], vz[u][:, a, h * 128:(h + 1) * 128],
                                      pt[j % 2][:, h, :], start=h == 0, stop=h == 3)
                        if a % 4 == 3:
                            last.then_inc(attended, 1)
                for u in (0, 1):
                    pe.wait_ge(o_kept, m * 2 + 2 * u + 2)
                    mm(G[u][:, 0:SC], W(WP), ot[u][:], start=True, stop=True).then_inc(projected, 1)
                norm("2", m, lambda u: pe.wait_ge(res_added, m + u + 1))
                for u in (0, 1):
                    pe.wait_ge(normed["2"], m + u + 1)
                    for c in range(4):
                        if u == 1:
                            pe.wait_ge(gelu_done, m * 4 + c + 1)
                        mm((T + P)[c][:, 0:SC], W(W1 + c), xn[u][:, 0:SC], start=True, stop=True).then_inc(up_done, 1)
                for u in (0, 1):
                    pe.wait_ge(gelu_done, (m + u) * 4 + 4)
                    for c in range(4):
                        last = mm(O[u][:, 0:SC], W(W2 + c), gh[u][:, c, :], start=c == 0, stop=c == 3)
                    last.then_inc(down_done, 1)

            steps(pe, body)

        @block.scalar
        def _(act):
            A = nc.scalar.activation
            act.wait_ge(consts_ready, 1)

            def norm(k, m):
                for u in (0, 1):
                    act.wait_ge(centered[k], m + u + 1)
                    A(sq[u][:], G[u][:, 0:SC], ACT.Square).then_inc(squared[k], 1)
                for u in (0, 1):
                    act.wait_ge(var_ready[k], m + u + 1)
                    A(lnv[u][:], O[u][:, 0:SC], ACT.Ln, bias=eps[:]).then_inc(log_ready[k], 1)
                    act.wait_ge(log_ready[k], m + u + 1)
                    A(rs[u][:], lnv[u][:], ACT.Exp, scale=-0.5).then_inc(rstd_ready[k], 1)

            def body(layer, s, q, wraps):
                n = layer * NS + s * 4 + q
                m = n * 2
                act.preload_act_table_set(LN_EXP)
                if layer == 0:
                    norm("p", m)
                norm("1", m)
                for u in (0, 1):
                    act.wait_ge(q_done, m + u + 1)
                    for h in (0, 1):
                        r = slice(64 * h, 64 * h + 64)
                        last = A(qbd[u][r, :, 64 * h:64 * h + WT], O[u][r, 0:SC].rearrange("p (w t) -> p w t", t=WT),
                                 ACT.Identity, bias=vf[r, layer, 0:1], scale=float(HD) ** -0.5)
                    last.then_inc(q_kept, 1)
                for u in (0, 1):
                    for b in (0, 1):
                        act.wait_ge(v_done, (m + u) * 2 + b + 1)
                        src = P[b][0:KP, :].rearrange("p (w h j e d) -> p w h j e d", w=4, h=2, j=4, e=2)
                        dst = vz[u][:, 4 * b:4 * b + 4].rearrange("p w (j s) -> p w j s", j=4)
                        for e in (0, 1):
                            r = slice(64 * e, 64 * e + 64)
                            for h in (0, 1):
                                c = 64 * h + HD * e
                                last = A(dst[r, :, :, c:c + HD], src[:, :, h, :, e, :], ACT.Copy)
                        last.then_inc(v_kept, 1)
                for i in range(16 + AV_LAG):
                    if i < 16:
                        act.wait_ge(shifted, m * 8 + i + 1)
                        A(ex[i % R][:], s2[i % R][:], ACT.Exp).then_inc(exps, 1)
                    if 0 <= i - T_LAG < 16:
                        j = i - T_LAG
                        act.wait_ge(transposed, m * 8 + j + 1)
                        A(pt[j % 2][:].rearrange("p a b -> p (a b)"), T[j % 2][:], ACT.Copy).then_inc(pt_kept, 1)
                    if i >= AV_LAG and (i - AV_LAG) % 4 == 3:
                        u, b = (i - AV_LAG) // 8, (i - AV_LAG) % 8 // 4
                        act.wait_ge(attended, (m + u) * 2 + b + 1)
                        for h in (0, 1):
                            r = slice(64 * h, 64 * h + 64)
                            last = A(ot[u][r, b * 4 * WT:(b + 1) * 4 * WT].rearrange("p (w t) -> p w t", t=WT),
                                     O[b][r, :].rearrange("p (w t) -> p w t", t=128)[:, :, 64 * h:64 * h + WT], ACT.Copy)
                        last.then_inc(o_kept, 1)
                for u in (0, 1):
                    act.wait_ge(projected, m + u + 1)
                    A(lnv[u][:], G[u][:, 0:SC], ACT.Identity, bias=vf[:, layer, 3:4]).then_inc(proj_biased, 1)
                norm("2", m)
                for u in (0, 1):
                    for c in range(4):
                        act.wait_ge(up_done, (m + u) * 4 + c + 1)
                        A(gh[u][:, c, :], (T + P)[c][:, 0:SC], ACT.Gelu, bias=vf[:, layer, 4 + c:5 + c]).then_inc(gelu_done, 1)

            steps(act, body)

        @block.gpsimd
        def _(pool):
            TT = nc.gpsimd.tensor_tensor

            def body(layer, s, q, wraps):
                n = layer * NS + s * 4 + q
                m = n * 2
                for i in range(16 + PROB_LAG):
                    if i < 16:
                        pool.wait_ge(max_ready, m * 8 + i + 1)
                        TT(s2[i % R][:], s1[i % R][:], mx[i % R][:].unsqueeze(2).broadcast_to([128, NH, WT]),
                           ALU.subtract).then_inc(shifted, 1)
                    if i >= PROB_LAG:
                        j = i - PROB_LAG
                        if j >= RP:
                            pool.wait_ge(transposed, m * 8 + j - RP + 1)
                        pool.wait_ge(rcp_ready, m * 8 + j + 1)
                        TT(pn[j % RP][:, :, 0:WT], ex[j % R][:], rc[j % R][:].unsqueeze(2).broadcast_to([128, NH, WT]),
                           ALU.mult).then_inc(probs, 1)

            pool.wait_ge(consts_ready, 1)
            steps(pool, body)

        @block.vector
        def _(dve):
            V = nc.vector
            for t in vz + qbd + pn + xn:
                V.memset(t[:], 0.0)
            V.memset(eps[:], EPS).then_inc(stored[0], 1)
            V.memset(mx[2][:], 0.0).then_inc(stored[1], 1)
            dve.wait_ge(weights_loaded, 9 * 16)
            dve.wait_ge(setup_pe, 1)
            for l in (0, 1):
                V.tensor_tensor(vf[:, l, 0:3], G[l][:, 0:3], v[:, l * LV + QB:l * LV + VB + 1], ALU.add)
                last = V.tensor_tensor(vf[:, l, 4:8], G[l][:, 4:8], v[:, l * LV + B1:l * LV + B1 + 4], ALU.add)
            last.then_inc(setup_dve, 1)
            dve.wait_ge(setup_pe, 2)
            dve.wait_ge(setup_dve, 1)
            for l in (0, 1):
                V.tensor_scalar(vf[:, l, 0:1], vf[:, l, 0:1], float(HD) ** -0.5, None, ALU.mult)
                V.tensor_tensor(vf[:, l, 3:4], O[l][:, 0:1], v[:, l * LV + PB:l * LV + PB + 1], ALU.add)
                V.tensor_scalar(w[:, l, WQ:WV + 1, :], w[:, l, WQ:WV + 1, :], v[:, l * LV + N1G:l * LV + N1G + 1], None, ALU.mult)
                V.tensor_scalar(w[:, l, W1:W1 + 4, :], w[:, l, W1:W1 + 4, :], v[:, l * LV + N2G:l * LV + N2G + 1], None, ALU.mult)
            for c in (0, 1):
                last = V.tensor_copy(bias[:, c, :], rpb_l[:, 0, :])
            last.then_inc(x_free, 1)
            V.memset(mx[0][:], 0.0).then_inc(x_free, 1)
            dve.wait_ge(x_free, 2)
            V.memset(mx[1][:], 0.0).then_inc(consts_ready, 1)

            def body(layer, s, q, wraps):
                n = layer * NS + s * 4 + q
                m = n * 2
                col = lambda k: v[:, k:k + 1]
                if layer == 0:
                    for u in (0, 1):
                        dve.wait_ge(embedded, m + u + 1)
                        V.tensor_scalar(x[u][:], G[u][:, 0:SC], col(PEB), None, ALU.add).then_inc(emb_biased, 1)
                    for u in (0, 1):
                        dve.wait_ge(rstd_ready["p"], m + u + 1)
                        V.tensor_tensor(lnv[u][:], G[u][:, 0:SC], rs[u][:], ALU.mult).then_inc(pre_affine, 1)
                        dve.wait_ge(pre_affine, m + u + 1)
                        V.tensor_scalar(x[u][:], lnv[u][:], col(PEG), col(PENB), ALU.mult, ALU.add).then_inc(x_ready, 1)
                for u in (0, 1):
                    dve.wait_ge(rstd_ready["1"], m + u + 1)
                    for (a, w0, nw, c0, c1), (b, *_) in zip(windowed(G[u][:, 0:SC], layer), windowed(rs[u][:], layer)):
                        last = V.tensor_tensor(window_cols(xn[u], w0, nw, c0, c1), a, b, ALU.mult)
                    last.then_inc(normed["1"], 1)

                def blockdiag(i):
                    u, a = i // 8, i % 8
                    if a == 0:
                        dve.wait_ge(k_done, m + u + 1)
                    V.scalar_tensor_tensor(kbd[i % 2][:], G[u][:, a * WT:(a + 1) * WT].unsqueeze(1).broadcast_to([128, NH, WT]),
                                           vf[:, layer, 1:2], hm[:].unsqueeze(2).broadcast_to([128, NH, WT]),
                                           ALU.add, ALU.mult).then_inc(kbd_ready, 1)

                blockdiag(0)
                for i in range(16 + SUM_LAG):
                    if i < 15:
                        blockdiag(i + 1)
                    if i < 16:
                        dve.wait_ge(scores, m * 8 + i + 1)
                        V.tensor_tensor(s1[i % R][:].rearrange("p h k -> p (h k)"), P[i % 2][:, 0:NH * WT],
                                        bias[:, 1 if i % 8 == NW - 1 else 0, :], ALU.add).then_inc(biased, 1)
                        dve.wait_ge(biased, m * 8 + i + 1)
                        V.tensor_reduce(mx[i % R][:], s1[i % R][:], AX.X, ALU.max).then_inc(max_ready, 1)
                    if i >= SUM_LAG:
                        j = i - SUM_LAG
                        dve.wait_ge(exps, m * 8 + j + 1)
                        V.tensor_reduce(sm[j % R][:], ex[j % R][:], AX.X, ALU.add).then_inc(sum_ready, 1)
                        dve.wait_ge(sum_ready, m * 8 + j + 1)
                        V.reciprocal(rc[j % R][:], sm[j % R][:]).then_inc(rcp_ready, 1)
                for u in (0, 1):
                    dve.wait_ge(proj_biased, m + u + 1)
                    for a, w0, nw, c0, c1 in windowed(x[u][:], layer):
                        last = V.tensor_tensor(a, window_cols(lnv[u], w0, nw, c0, c1), a, ALU.add)
                    last.then_inc(res_added, 1)
                for u in (0, 1):
                    dve.wait_ge(rstd_ready["2"], m + u + 1)
                    V.tensor_tensor(xn[u][:, 0:SC], G[u][:, 0:SC], rs[u][:], ALU.mult).then_inc(normed["2"], 1)
                for u in (0, 1):
                    dve.wait_ge(down_done, m + u + 1)
                    dve.wait_ge(stored[u], n * 32 + 1)
                    V.scalar_tensor_tensor(xo[u][:], O[u][:, 0:SC], col(layer * LV + B2), x[u][:],
                                           ALU.add, ALU.add).then_inc(x_free, 1)

            def between(k):
                dve.wait_ge(x_free, 2 * (NS if k == 0 else NS + 4 * (NW - 1)) + 2)
                for c in (0, 1):
                    last = V.tensor_tensor(bias[:, c, :], rpb_l[:, 1, :], am[:, 2 * k + c, :], ALU.add)
                last.then_inc(bias_set, 1)
                dve.wait_ge(bias_set, k + 1)

            steps(dve, body, between)


ROW = GRID * HB
HSCALE = 4096.0
WSCALE = 256.0
T16 = 16
NBLK = S // T16


def prepare(nc, consts, tok, txt, xparts, resid):
    Q = 4
    with ExitStack() as ctx:
        def sb(name, shape, dt=F32):
            return ctx.enter_context(nc.sbuf_tensor("b_" + name, shape, dt))

        def sem(name):
            return ctx.enter_context(nc.semaphore("b_" + name))

        center, mean = sb("center", [128, 128]), sb("mean", [128, 128])
        eps = sb("eps", [128, 2])
        each = lambda name, dt=F32: [sb(f"{name}{u}", [128, ROW], dt) for u in range(Q)]
        x, sq, l1, l2, r1, r2, xs, res = (each(k) for k in ("x", "sq", "l1", "l2", "r1", "r2", "xs", "res"))
        xa, xb = each("xa", F16), each("xb", F16)
        G = [ctx.enter_context(nc.psum_tensor(f"b_G{u}", [128, 512], F32)) for u in range(Q)]
        O = [ctx.enter_context(nc.psum_tensor(f"b_O{u}", [128, 512], F32)) for u in range(Q)]
        consts_loaded, ready = sem("consts_loaded"), sem("ready")
        loaded = [sem(f"loaded{u}") for u in range(Q)]
        stored = [sem(f"stored{u}") for u in range(Q)]
        centered, squared, var_ready, logs, rstd, hi, full, norm1, done = (
            sem(k) for k in ("centered", "squared", "var_ready", "logs", "rstd", "hi", "full", "norm1", "done"))
        block = ctx.enter_context(nc.Block())

        def tiles(eng, body):
            with eng.Fori(0, GRID // Q) as n:
                body(n, range(Q), GRID)
            body(GRID // Q, (0,), NTXT)

        def by_image(t, nt):
            return t[:, 0:HB * nt].rearrange("p (b t) -> p t b", t=nt)

        def by_token(t, nt):
            return t[:, 0:HB * nt].rearrange("p (t b) -> p t b", b=HB)

        @block.sync
        def _(sp):
            sp.dma_start(center[:], consts[1]).then_inc(consts_loaded, 16)
            sp.dma_start(mean[:], consts[2]).then_inc(consts_loaded, 16)
            rows = tok.rearrange("p (b t) -> p b t", b=HB)

            def load(tile, u, nt):
                src = rows[:, :, bass.ds(tile * GRID, nt)] if nt == GRID else txt.rearrange("p (b t) -> p b t", b=HB)
                sp.dma_start(x[u][:, 0:HB * nt].rearrange("p (b t) -> p b t", b=HB), src).then_inc(loaded[u], 16)

            def store(tile, u, nt):
                sp.wait_ge(done, tile + 1)
                at = bass.ds(tile * ROW, HB * nt)
                for dst, t in ((xparts[0], xa[u]), (xparts[1], xb[u]), (resid, res[u])):
                    sp.dma_start(dst[:, at], t[:, 0:HB * nt]).then_inc(stored[u], 16)

            for u in range(Q):
                load(u, u, GRID)
            with sp.Fori(0, GRID // Q - 1) as n:
                for u in range(Q):
                    store(n * Q + u, u, GRID)
                    load(n * Q + Q + u, u, GRID)
            for u in range(Q):
                store(GRID - Q + u, u, GRID)
                if u == 0:
                    load(GRID, 0, NTXT)
            store(GRID, 0, NTXT)
            for u in range(Q):
                sp.wait_ge(stored[u], 48 * (GRID // Q + (u == 0)) + 1)

        @block.tensor
        def _(pe):
            pe.wait_ge(consts_loaded, 32)

            def body(n, us, nt):
                m, w = n * Q, HB * nt
                for u in us:
                    pe.wait_ge(loaded[u], 16 * n + 16)
                    nc.tensor.matmul(G[u][:, 0:w], center[:], x[u][:, 0:w], start=True, stop=True).then_inc(centered, 1)
                for u in us:
                    pe.wait_ge(squared, m + u + 1)
                    nc.tensor.matmul(O[u][:, 0:w], mean[:], sq[u][:, 0:w], start=True, stop=True).then_inc(var_ready, 1)

            tiles(pe, body)

        @block.scalar
        def _(act):
            A = nc.scalar.activation
            act.wait_ge(ready, 1)
            act.preload_act_table_set(LN_EXP)

            def body(n, us, nt):
                m, w = n * Q, HB * nt
                for u in us:
                    act.wait_ge(centered, m + u + 1)
                    A(sq[u][:, 0:w], G[u][:, 0:w], ACT.Square).then_inc(squared, 1)
                for u in us:
                    act.wait_ge(var_ready, m + u + 1)
                    A(l1[u][:, 0:w], O[u][:, 0:w], ACT.Ln, bias=eps[:, 0:1])
                    A(l2[u][:, 0:w], O[u][:, 0:w], ACT.Ln, bias=eps[:, 1:2], scale=1.0 + EPS).then_inc(logs, 1)
                    act.wait_ge(logs, m + u + 1)
                    A(r1[u][:, 0:w], l1[u][:, 0:w], ACT.Exp, scale=-0.5)
                    A(r2[u][:, 0:w], l2[u][:, 0:w], ACT.Exp, scale=-0.5).then_inc(rstd, 1)

            tiles(act, body)

        @block.vector
        def _(dve):
            V = nc.vector
            V.memset(eps[:, 0:1], EPS)
            V.memset(eps[:, 1:2], EPS * EPS)
            for u in range(Q):
                V.memset(l1[u][:, 0:1], 0.0).then_inc(stored[u], 1)
            V.memset(res[0][:], 0.0).then_inc(ready, 1)
            dve.wait_ge(ready, 1)

            def body(n, us, nt):
                m = n * Q
                for u in us:
                    dve.wait_ge(rstd, m + u + 1)
                    dve.wait_ge(stored[u], n * 48 + 1)
                    c = by_image(G[u], nt)
                    V.scalar_tensor_tensor(by_token(xa[u], nt), c, HSCALE, by_image(r2[u], nt), ALU.mult, ALU.mult).then_inc(hi, 1)
                    V.scalar_tensor_tensor(by_token(xs[u], nt), c, HSCALE, by_image(r2[u], nt), ALU.mult, ALU.mult).then_inc(full, 1)
                    V.tensor_tensor(by_token(l1[u], nt), c, by_image(r1[u], nt), ALU.mult).then_inc(norm1, 1)
                    dve.wait_ge(full, m + u + 1)
                    V.tensor_tensor(xb[u][:, 0:HB * nt], xs[u][:, 0:HB * nt], xa[u][:, 0:HB * nt], ALU.subtract)
                    dve.wait_ge(norm1, m + u + 1)
                    V.tensor_tensor(by_token(res[u], nt), by_token(l1[u], nt), by_image(x[u], nt), ALU.add).then_inc(done, 1)

            tiles(dve, body)


def gru(nc, consts, wih, whh, gvec, xparts, hist):
    B, T = NIMG, T16
    with ExitStack() as ctx:
        def sb(name, shape, dt=F32):
            return ctx.enter_context(nc.sbuf_tensor("g_" + name, shape, dt))

        def sem(name):
            return ctx.enter_context(nc.semaphore("g_" + name))

        wi = sb("wi", [128, 2, 3, C])
        wh = sb("wh", [128, 3, 128])
        vecs = sb("vecs", [128, 8])
        ident = sb("ident", [128, 128])
        ident_s = sb("ident_s", [128, 128], F16)
        bias = sb("bias", [128, 4])
        gb = vecs[:, 1:8]
        wi_f = sb("wi_f", [128, 2, 3, C])
        wi1 = sb("wi1", [128, 2, 2, 3, C], F16)
        wi2 = sb("wi2", [128, 2, 2, 3, C], F16)
        wh1, wh2 = sb("wh1", [128, 3, 128], F16), sb("wh2", [128, 3, 128], F16)
        bias_f = sb("bias_f", [128, 4, T * B])
        bias1, bias2 = sb("bias1", [128, 4, T * B], F16), sb("bias2", [128, 4, T * B], F16)
        x = sb("x", [128, 2, 2, 2, T, HB], F16)
        h = sb("h", [128, 2, T, B])
        zero = sb("zero", [128, B], F16)
        rz, pre_n = sb("rz", [128, 2, B, 2]), sb("pre_n", [128, B, 2])
        n_, omz, zh, zn = (sb(k, [128, B]) for k in ("n", "omz", "zh", "zn"))
        one_s = sb("one_s", [128, 1])
        zh1, zh2, zn1, zn2 = (sb(k, [128, B], F16) for k in ("zh1", "zh2", "zn1", "zn2"))
        RZ = [ctx.enter_context(nc.psum_tensor(f"g_RZ{u}", [128, 2, T, B], F32)) for u in (0, 1)]
        NX = [ctx.enter_context(nc.psum_tensor(f"g_NX{u}", [128, T, B, 2], F32)) for u in (0, 1)]
        BP = ctx.enter_context(nc.psum_tensor("g_BP", [128, 512], F32))

        weights_loaded, bias_products, link, ready = sem("weights_loaded"), sem("bias_products"), sem("link"), sem("ready")
        x_loaded = [sem("x_loaded0"), sem("x_loaded1")]
        h_stored, h_ready = sem("h_stored"), sem("h_ready")
        gates_ready, nh_ready, rz_ready = sem("gates_ready"), sem("nh_ready"), sem("rz_ready")
        pre_n_ready, n_ready = sem("pre_n_ready"), sem("n_ready")
        zh_ready, zh1_ready, zh2_ready, zn1_ready, zn2_ready, zn_ready = (
            sem(k) for k in ("zh_ready", "zh1_ready", "zh2_ready", "zn1_ready", "zn2_ready", "zn_ready"))
        block = ctx.enter_context(nc.Block())

        def blocks(eng, body):
            body(0, True, False)
            with eng.Fori(1, NBLK // 2 - 1) as i:
                body(i, False, False)
            body(NBLK // 2 - 1, False, True)

        flat = lambda t: t.rearrange("p a b -> p (a b)")

        @block.sync
        def _(sp):
            for dst, src in ((wi[:].rearrange("p a b c -> p (a b c)"), wih), (flat(wh[:]), whh), (vecs[:], gvec),
                             (ident[:], consts[0])):
                sp.dma_start(dst, src).then_inc(weights_loaded, 16)

            def load(k, u):
                for p in (0, 1):
                    sp.dma_start(flat(x[:, u, 0, p]), xparts[p][:, bass.ds(k * (T * HB), T * HB)]).then_inc(x_loaded[u], 16)
                    sp.dma_start(flat(x[:, u, 1, p]), xparts[p][:, bass.ds((NBLK - 1 - k) * (T * HB), T * HB)])\
                        .then_inc(x_loaded[u], 16)

            load(0, 0)
            load(1, 1)

            def body(i, first, last):
                for u in (0, 1):
                    k = i * 2 + u
                    sp.wait_ge(h_ready, (k + 1) * T)
                    sp.dma_start(hist[:, bass.ds(k * (T * B), T * B)], flat(h[:, u])).then_inc(h_stored, 16)
                    if not last:
                        load(k + 2, u)

            blocks(sp, body)
            sp.wait_ge(h_stored, 16 * NBLK)

        PROJ = [(g, d, half, w, p) for g in range(3) for d in (0, 1) for half in (0, 1)
                for w, p in ((wi1, 0), (wi2, 0), (wi1, 1))]

        @block.tensor
        def _(pe):
            def mm(dst, a, b, start=False):
                return nc.tensor.matmul(dst, a, b, start=start, stop=True, skip_group_check=True)

            pe.wait_ge(weights_loaded, 4 * 16)
            for d in (0, 1):
                for g in range(3):
                    last = mm(BP[C * d:C * d + C, g:g + 1], wi[0:C, d, g, :], gb[0:C, 6:7], start=True)
            last.then_inc(bias_products, 1)
            pe.wait_ge(ready, 1)

            def set_biases(u):
                for bank, c in ((RZ[u], 0), (NX[u], 2)):
                    dst = bank[:].rearrange("p a b c -> p (a b c)")
                    mm(dst, ident_s[:], flat(bias1[:, c:c + 2]), start=True)
                    mm(dst, ident_s[:], flat(bias2[:, c:c + 2]))

            def project(u, i):
                g, d, half, w, p = PROJ[i]
                dst = (RZ[u][:, g] if g < 2 else NX[u][:, :, :, 1])[C * d:C * d + C, :, HB * half:HB * half + HB]
                src = x[:, u, d, p]
                return mm(dst, w[:, half, d, g, :], src[:, ::-1, :] if d else src)

            def state(part, u, j, low, last=False):
                for g, dst in enumerate((RZ[u][:, 0, j], RZ[u][:, 1, j], NX[u][:, j, :, 0])):
                    m = mm(dst, wh1[:, g, :], part[:])
                    if not low:
                        m = mm(dst, wh2[:, g, :], part[:])
                    if last and g == 1:
                        m.then_inc(gates_ready, 1)
                if last:
                    m.then_inc(nh_ready, 1)

            pe.wait_ge(x_loaded[0], 64)
            set_biases(0)
            for i in range(len(PROJ)):
                m = project(0, i)
            m.then_inc(gates_ready, 1)
            mm(NX[0][:, 0, :, 0], wh1[:, 2, :], zero[:]).then_inc(nh_ready, 1)

            def body(i, first, last):
                for u in (0, 1):
                    k = i * 2 + u
                    more = not (last and u == 1)
                    for j in range(T):
                        s = k * T + j
                        if more and j == 0:
                            pe.wait_ge(x_loaded[1 - u], (i + 1 + u) * 64)
                            set_biases(1 - u)
                        if more and j > 0:
                            for q in range(3 * (j - 1), min(3 * j, len(PROJ))):
                                project(1 - u, q)
                        if more or j < T - 1:
                            to = (u, j + 1) if j < T - 1 else (1 - u, 0)
                            pe.wait_ge(zh1_ready, s + 1)
                            state(zh1, *to, low=False)
                            pe.wait_ge(zh2_ready, s + 1)
                            state(zh2, *to, low=True)
                            pe.wait_ge(zn1_ready, s + 1)
                            state(zn1, *to, low=False)
                            pe.wait_ge(zn2_ready, s + 1)
                            state(zn2, *to, low=True, last=True)

            blocks(pe, body)

        @block.scalar
        def _(act):
            unscale = 1.0 / (HSCALE * WSCALE)

            def body(i, first, last):
                for u in (0, 1):
                    for j in range(T):
                        s = (i * 2 + u) * T + j
                        act.wait_ge(gates_ready, s + 1)
                        nc.scalar.activation(rz[:, :, :, 1], RZ[u][:, :, j, :], ACT.Sigmoid, scale=unscale).then_inc(rz_ready, 1)
                        act.wait_ge(rz_ready, s + 1)
                        nc.scalar.activation(omz[:], rz[:, 1, :, 1], ACT.Identity, scale=-HSCALE, bias=one_s[:])
                        act.wait_ge(pre_n_ready, s + 1)
                        nc.scalar.activation(n_[:], pre_n[:, :, 1], ACT.Tanh, scale=unscale).then_inc(n_ready, 1)

            blocks(act, body)

        @block.vector
        def _(dve):
            V = nc.vector
            count = [0]

            def chain(op):
                count[0] += 1
                op.then_inc(link, 1)
                dve.wait_ge(link, count[0])

            dve.wait_ge(weights_loaded, 4 * 16)
            for t in (wi1, wi2, h, zero, bias_f, rz):
                chain(V.memset(t[:], 0.0))
            chain(V.memset(one_s[:], HSCALE))
            dve.wait_ge(bias_products, 1)
            chain(V.tensor_tensor(bias[:, 0:3], BP[:, 0:3], gb[:, 0:3], ALU.add))
            chain(V.tensor_tensor(bias[:, 0:2], bias[:, 0:2], gb[:, 3:5], ALU.add))
            chain(V.tensor_copy(bias[:, 3:4], gb[:, 5:6]))
            chain(V.tensor_scalar(bias[:], bias[:], WSCALE, None, ALU.mult))
            chain(V.tensor_scalar(ident_s[:], ident[:], HSCALE, None, ALU.mult))
            chain(V.tensor_scalar(wi_f[:], wi[:], vecs[:, 0:1], WSCALE, ALU.mult, ALU.mult))
            chain(V.tensor_scalar(wh[:], wh[:], WSCALE, None, ALU.mult))
            for half in (0, 1):
                r = slice(C * half, C * half + C)
                chain(V.tensor_copy(wi1[r, half], wi_f[r]))
                chain(V.tensor_tensor(wi2[r, half], wi_f[r], wi1[r, half], ALU.subtract))
            chain(V.tensor_copy(wh1[:], wh[:]))
            chain(V.tensor_tensor(wh2[:], wh[:], wh1[:], ALU.subtract))
            for q in (0, 1):
                chain(V.tensor_scalar(bias_f[:, q, :], bias_f[:, q, :], bias[:, q:q + 1], None, ALU.add))
            side = flat(bias_f[:, 2:4]).rearrange("p (c e) -> p c e", e=2)
            for e, q in ((0, 3), (1, 2)):
                chain(V.tensor_scalar(side[:, :, e], side[:, :, e], bias[:, q:q + 1], None, ALU.add))
            chain(V.tensor_copy(bias1[:], bias_f[:]))
            V.tensor_tensor(bias2[:], bias_f[:], bias1[:], ALU.subtract).then_inc(ready, 1)

            def body(i, first, last):
                for u in (0, 1):
                    k = i * 2 + u
                    for j in range(T):
                        s = k * T + j
                        before = h[:, u, j - 1] if j else h[:, 1 - u, T - 1]
                        dve.wait_ge(rz_ready, s + 1)
                        dve.wait_ge(nh_ready, s + 1)
                        V.tensor_tensor_scan(pre_n[:].rearrange("p b e -> p (b e)"), rz[:, 0].rearrange("p b e -> p (b e)"),
                                             NX[u][:, j].rearrange("p b e -> p (b e)"), 0.0, ALU.mult, ALU.add)\
                            .then_inc(pre_n_ready, 1)
                        if not (first and s == 0):
                            dve.wait_ge(h_ready, s)
                        V.tensor_tensor(zh1[:], rz[:, 1, :, 1], before, ALU.mult).then_inc(zh1_ready, 1)
                        V.tensor_tensor(zh[:], rz[:, 1, :, 1], before, ALU.mult).then_inc(zh_ready, 1)
                        dve.wait_ge(zh_ready, s + 1)
                        V.tensor_tensor(zh2[:], zh[:], zh1[:], ALU.subtract).then_inc(zh2_ready, 1)
                        dve.wait_ge(n_ready, s + 1)
                        V.tensor_tensor(zn1[:], n_[:], omz[:], ALU.mult).then_inc(zn1_ready, 1)
                        V.tensor_tensor(zn[:], n_[:], omz[:], ALU.mult).then_inc(zn_ready, 1)
                        dve.wait_ge(zn_ready, s + 1)
                        V.tensor_tensor(zn2[:], zn[:], zn1[:], ALU.subtract).then_inc(zn2_ready, 1)
                        if j == 0 and not first:
                            dve.wait_ge(h_stored, 16 * (k - 1))
                        V.tensor_tensor(h[:, u, j], zn[:], zh[:], ALU.add).then_inc(h_ready, 1)

            blocks(dve, body)


NE = 8
TT = 48
TC = TT * HB
CH = TC // 128
MSTEP = S // TT // 2
MV_OB, MV_GB, MV_B1 = 0, 1, 2


def mixture(nc, consts, gru_w, out_w, router, wexp, b2w, sel_c, mvec, low_c, rank_c, hist, resid, out):
    with ExitStack() as ctx:
        def sb(name, shape, dt=F32):
            return ctx.enter_context(nc.sbuf_tensor("m_" + name, shape, dt))

        def sem(name):
            return ctx.enter_context(nc.semaphore("m_" + name))

        def bank(name):
            return ctx.enter_context(nc.psum_tensor("m_" + name, [128, 512], F32))

        two = lambda name, shape: [sb(f"{name}{u}", shape) for u in (0, 1)]
        ident, center, mean = sb("ident", [128, 128]), sb("center", [128, 128]), sb("mean", [128, 128])
        gw = sb("gw", [128, 3, C])
        ow, rw, we = sb("ow", [128, 128]), sb("rw", [128, 2 * NE]), sb("we", [128, NE, 2, 128])
        bw, sel = sb("bw", [2 * NE, 128]), sb("sel", [2 * NE, NE, 128])
        mv, low, rank_at = sb("mv", [128, 10]), sb("low", [128, NE, NE]), sb("rank_at", [128, NE])
        eps = sb("eps", [128, 1])
        fr, rev = two("fr", [128, TT, NIMG]), two("rev", [128, TT, NIMG])
        res, th, p = two("res", [128, TC]), two("th", [128, TC]), two("p", [128, TC])
        h2, sq, lnv, rs = (two(k, [128, TC]) for k in ("h2", "sq", "lnv", "rs"))
        xn, base = ([two(f"{k}{i}", [128, TC]) for i in (0, 1)] for k in ("xn", "base"))
        G6 = CH * 2
        lg, lx, lexp, rank, chosen, comb = (two(k, [128, G6, NE]) for k in ("lg", "lx", "lexp", "rank", "chosen", "comb"))
        beat = two("beat", [128, G6, NE, NE])
        rk2 = two("rk2", [128, G6, NE])
        lmx, lsum, lrc = (two(k, [128, G6]) for k in ("lmx", "lsum", "lrc"))
        ct = [two(f"ct{i}", [2 * NE, TC]) for i in (0, 1)]
        cs = [[sb(f"cs{i}{u}", [48, TC], F16) for u in (0, 1)] for i in (0, 1)]
        sel16 = sb("sel16", [48, NE, 128], F16)
        hg, hm = two("hg", [128, TC]), two("hm", [128, TC])
        y = two("y", [128, TC])
        A_, B_, L, W = (bank(k) for k in "ABLW")
        U, Y = ([bank(f"{k}{u}") for u in (0, 1)] for k in "UY")

        weights_loaded, scaled, ready = sem("weights_loaded"), sem("scaled"), sem("ready")
        loaded, stored = [sem("loaded0"), sem("loaded1")], [sem("stored0"), sem("stored1")]
        names = ("aligned gate_done tanh_done gated mixed summed centered squared var_ready log_ready rstd_ready normed "
                 "based routed logits_kept max_ready less_max beat_ready beat_upper ranks_a rank_ready lexp_ready chosen_ready "
                 "kept_exp sum_ready rcp_ready comb_ready comb_t comb_kept comb_split up_done spread gelu_done weighted down_done done").split()
        on = {k: sem(k) for k in names}
        block = ctx.enter_context(nc.Block())
        SLOTS, LATER = 2 * NE + 2, 6

        def pairs(eng, body, front):
            for i in range(SLOTS):
                front(0, 0, i)
            with eng.Fori(0, (MSTEP - 1) // 2) as k:
                for par in (0, 1):
                    n = 2 * k + par
                    body(n, par, lambda i: front(n + 1, 1 - par, i))
            body(MSTEP - 1, 0, lambda i: None)

        @block.sync
        def _(sp):
            flat = lambda t: t.rearrange("p a b -> p (a b)")
            for dst, src in ((ident[:], consts[0]), (center[:], consts[1]), (mean[:], consts[2]), (flat(gw[:]), gru_w),
                             (ow[:], out_w), (rw[:], router), (we[:].rearrange("p a b c -> p (a b c)"), wexp), (bw[:], b2w),
                             (flat(sel[:]), sel_c), (mv[:], mvec), (flat(low[:]), low_c), (rank_at[:], rank_c)):
                sp.dma_start(dst, src).then_inc(weights_loaded, 16)

            def load(t, u):
                sp.dma_start(flat(fr[u][0:C]), hist[0:C, bass.ds(t * (TT * NIMG), TT * NIMG)]).then_inc(loaded[u], 16)
                sp.dma_start(flat(rev[u][C:128]), hist[C:128, bass.ds((2 * MSTEP - 1 - t) * (TT * NIMG), TT * NIMG)])\
                    .then_inc(loaded[u], 16)
                sp.dma_start(res[u][:], resid[:, bass.ds(t * TC, TC)]).then_inc(loaded[u], 16)

            def reload(n):
                for u in (0, 1):
                    sp.wait_ge(on["summed"], n * 2 + u + 1)
                    load(n * 2 + 2 + u, u)

            def store(n):
                for u in (0, 1):
                    t = n * 2 + u
                    sp.wait_ge(on["done"], t + 3)
                    sp.dma_start(out[:, bass.ds(t * TC, TC)], y[u][:]).then_inc(stored[u], 16)

            load(0, 0)
            load(1, 1)
            reload(0)
            with sp.Fori(0, MSTEP - 2) as n:
                reload(n + 1)
                store(n)
            store(MSTEP - 2)
            store(MSTEP - 1)
            for u in (0, 1):
                sp.wait_ge(stored[u], 16 * MSTEP + 1)

        @block.gpsimd
        def _(pool):
            def front(n, par, i):
                for u in (0, 1):
                    if i - LATER * u == 5:
                        pool.wait_ge(on["normed"], n * 2 + u + 1)
                        nc.gpsimd.tensor_tensor(base[par][u][:], h2[u][:], xn[par][u][:], ALU.add).then_inc(on["based"], 1)

            def body(n, par, ahead):
                for i in range(SLOTS):
                    ahead(i)

            pairs(pool, body, front)

        @block.tensor
        def _(pe):
            def mm(dst, a, b, start=True, stop=True, **k):
                return nc.tensor.matmul(dst, a, b, start=start, stop=stop, **k)

            pe.wait_ge(ready, 3)

            def front(n, par, i):
                for u in (0, 1):
                    t, k = n * 2 + u, i - LATER * u
                    if k == 0:
                        pe.wait_ge(loaded[u], n * 48 + 48)
                        pe.wait_ge(on["aligned"], t + 1)
                        if not (isinstance(t, int) and t == 0):
                            pe.wait_ge(on["normed"], t)
                        for w, bk in ((0, A_), (1, B_)):
                            for half in (0, 1):
                                last = mm(bk[C * half:C * half + C, 0:TC], gw[:, w, :], fr[u][:, :, HB * half:HB * half + HB])
                        last.then_inc(on["gate_done"], 1)
                    if k == 1:
                        pe.wait_ge(on["gated"], t + 1)
                        for half in (0, 1):
                            mm(A_[C * half:C * half + C, 0:TC], gw[:, 2, :], fr[u][:, :, HB * half:HB * half + HB])
                        mm(A_[:, 0:TC], ow[:], p[u][:], start=False, skip_group_check=True).then_inc(on["mixed"], 1)
                    if k == 2:
                        pe.wait_ge(on["summed"], t + 1)
                        mm(B_[:, 0:TC], center[:], h2[u][:]).then_inc(on["centered"], 1)
                    if k == 3:
                        pe.wait_ge(on["squared"], t + 1)
                        mm(A_[:, 0:TC], mean[:], sq[u][:]).then_inc(on["var_ready"], 1)
                    if k == 5:
                        pe.wait_ge(on["normed"], t + 1)
                        if not (isinstance(t, int) and t == 0):
                            pe.wait_ge(on["comb_kept"], t)
                        for c in range(CH):
                            last = mm(L[:, 2 * NE * c:2 * NE * (c + 1)], xn[par][u][:, 128 * c:128 * (c + 1)], rw[:])
                        last.then_inc(on["routed"], 1)
                    if k == 10:
                        pe.wait_ge(on["comb_ready"], t + 1)
                        for c in range(CH):
                            last = nc.tensor.transpose(L[0:2 * NE, 128 * c:128 * (c + 1)],
                                                       comb[u][:, 2 * c:2 * c + 2, :].rearrange("p a b -> p (a b)"), ident[:])
                        last.then_inc(on["comb_t"], 1)

            def body(n, par, ahead):
                m = n * 2
                for i in range(SLOTS):
                    if i >= 2:
                        e, u = (i - 2) // 2, i % 2
                        pe.wait_ge(on["weighted"], m * NE + i - 2 + 1)
                        last = mm(Y[u][:, 0:TC], we[:, e, 1, :], hm[u][:], start=False, stop=e == NE - 1)
                        if e == NE - 1:
                            last.then_inc(on["down_done"], 1)
                    if i < 2 * NE:
                        e, u = i // 2, i % 2
                        mm(U[u][:, 0:TC], we[:, e, 0, :], xn[par][u][:]).then_inc(on["up_done"], 1)
                        if e == 0:
                            pe.wait_ge(on["comb_kept"], m + u + 1)
                            pe.wait_ge(on["done"], m + u + 1)
                            mm(Y[u][:, 0:TC], bw[:], ct[par][u][:], stop=False)
                        if i >= 1:
                            pe.wait_ge(on["weighted"], m * NE + i)
                        if e == 0:
                            pe.wait_ge(on["comb_split"], m + u + 1)
                        mm(W[:, 0:TC], sel16[:, e, :], cs[par][u][:]).then_inc(on["spread"], 1)
                    ahead(i)

            pairs(pe, body, front)

        @block.scalar
        def _(act):
            A = nc.scalar.activation
            act.wait_ge(ready, 3)

            def front(n, par, i):
                for u in (0, 1):
                    t, k = n * 2 + u, i - LATER * u
                    if k == 0:
                        act.wait_ge(loaded[u], n * 48 + 48)
                        A(fr[u][C:128], rev[u][C:128, ::-1, :], ACT.Copy).then_inc(on["aligned"], 1)
                    if k == 1:
                        act.wait_ge(on["gate_done"], t + 1)
                        A(th[u][:], A_[:, 0:TC], ACT.Tanh, scale=0.5, bias=mv[:, MV_GB:MV_GB + 1]).then_inc(on["tanh_done"], 1)
                    if k == 3:
                        act.wait_ge(on["centered"], t + 1)
                        A(sq[u][:], B_[:, 0:TC], ACT.Square).then_inc(on["squared"], 1)
                    if k == 4:
                        act.preload_act_table_set(LN_EXP)
                        act.wait_ge(on["var_ready"], t + 1)
                        A(lnv[u][:], A_[:, 0:TC], ACT.Ln, bias=eps[:]).then_inc(on["log_ready"], 1)
                        act.wait_ge(on["log_ready"], t + 1)
                        A(rs[u][:], lnv[u][:], ACT.Exp, scale=-0.5).then_inc(on["rstd_ready"], 1)
                    if k == 7:
                        act.wait_ge(on["less_max"], t + 1)
                        A(lexp[u][:], lx[u][:], ACT.Exp).then_inc(on["lexp_ready"], 1)
                    if k == 11:
                        act.wait_ge(on["comb_t"], t + 1)
                        A(ct[par][u][:], L[0:2 * NE, 0:TC], ACT.Copy)
                        A(cs[par][u][0:2 * NE], L[0:2 * NE, 0:TC], ACT.Copy, scale=HSCALE).then_inc(on["comb_kept"], 1)

            def body(n, par, ahead):
                for i in range(SLOTS):
                    ahead(i)
                    if i < 2 * NE:
                        e, u = i // 2, i % 2
                        act.wait_ge(on["up_done"], n * (2 * NE) + i + 1)
                        A(hg[u][:], U[u][:, 0:TC], ACT.Gelu, bias=mv[:, MV_B1 + e:MV_B1 + e + 1]).then_inc(on["gelu_done"], 1)

            pairs(act, body, front)

        @block.vector
        def _(dve):
            V = nc.vector
            dve.wait_ge(weights_loaded, 12 * 16)
            V.memset(eps[:], EPS).then_inc(stored[0], 1)
            V.memset(lmx[0][:], 0.0).then_inc(stored[1], 1)
            V.tensor_scalar(gw[:, 0, :], gw[:, 0, :], 1.0 / HSCALE, None, ALU.mult)
            V.tensor_scalar(gw[:, 1, :], gw[:, 1, :], 0.5 / HSCALE, None, ALU.mult)
            V.tensor_scalar(gw[:, 2, :], gw[:, 2, :], 1.0 / HSCALE, None, ALU.mult)
            V.tensor_scalar(mv[:, MV_GB:MV_GB + 1], mv[:, MV_GB:MV_GB + 1], 0.5, None, ALU.mult).then_inc(on["done"], 1)
            V.memset(hg[0][:, 0:1], 0.0).then_inc(on["done"], 1)
            dve.wait_ge(on["done"], 2)
            V.memset(hg[1][:, 0:1], 0.0).then_inc(ready, 1)
            dve.wait_ge(ready, 1)
            for t in (cs[0] + cs[1]):
                V.memset(t[:], 0.0)
            V.memset(sel16[:], 0.0).then_inc(scaled, 1)
            dve.wait_ge(scaled, 1)
            for r in (0, 32):
                V.tensor_scalar(sel16[r:r + 2 * NE], sel[:], 1.0 / HSCALE, None, ALU.mult).then_inc(ready, 1)
            bc = lambda t: t.unsqueeze(2).broadcast_to([128, G6, NE])

            def front(n, par, i):
                for u in (0, 1):
                    t, k = n * 2 + u, i - LATER * u
                    if k == 1:
                        dve.wait_ge(on["tanh_done"], t + 1)
                        V.scalar_tensor_tensor(p[u][:], th[u][:], 1.0, B_[:, 0:TC], ALU.add, ALU.mult).then_inc(on["gated"], 1)
                    if k == 2:
                        dve.wait_ge(on["mixed"], t + 1)
                        if not (isinstance(t, int) and t < 2):
                            dve.wait_ge(on["based"], t - 1)
                        V.scalar_tensor_tensor(h2[u][:], A_[:, 0:TC], mv[:, MV_OB:MV_OB + 1], res[u][:], ALU.add, ALU.add)\
                            .then_inc(on["summed"], 1)
                    if k == 4:
                        dve.wait_ge(on["rstd_ready"], t + 1)
                        V.tensor_tensor(xn[par][u][:], B_[:, 0:TC], rs[u][:], ALU.mult).then_inc(on["normed"], 1)
                    if k == 6:
                        dve.wait_ge(on["routed"], t + 1)
                        V.tensor_copy(lg[u][:].rearrange("p a b -> p (a b)"), L[:, 0:G6 * NE]).then_inc(on["logits_kept"], 1)
                        dve.wait_ge(on["logits_kept"], t + 1)
                        V.tensor_reduce(lmx[u][:], lg[u][:], AX.X, ALU.max).then_inc(on["max_ready"], 1)
                        dve.wait_ge(on["max_ready"], t + 1)
                        V.tensor_tensor(lx[u][:], lg[u][:], bc(lmx[u][:]), ALU.subtract).then_inc(on["less_max"], 1)
                    if k == 7:
                        V.tensor_tensor(beat[u][:], lg[u][:].unsqueeze(2).broadcast_to([128, G6, NE, NE]),
                                        lg[u][:].unsqueeze(3).broadcast_to([128, G6, NE, NE]), ALU.is_gt).then_inc(on["beat_ready"], 1)
                        dve.wait_ge(on["beat_ready"], t + 1)
                        V.tensor_tensor(beat[u][:], beat[u][:], low[:].unsqueeze(1).broadcast_to([128, G6, NE, NE]), ALU.mult)\
                            .then_inc(on["beat_upper"], 1)
                    if k == 8:
                        dve.wait_ge(on["beat_upper"], t + 1)
                        V.tensor_reduce(rank[u][:], beat[u][:], AX.X, ALU.add)
                        V.tensor_reduce(rk2[u][:], beat[u][:].rearrange("p g e j -> p g j e"), AX.X, ALU.add).then_inc(on["ranks_a"], 1)
                        dve.wait_ge(on["ranks_a"], t + 1)
                        V.tensor_tensor(rank[u][:], rank[u][:], rk2[u][:], ALU.subtract).then_inc(on["rank_ready"], 1)
                        dve.wait_ge(on["rank_ready"], t + 1)
                        V.tensor_tensor(chosen[u][:], rank[u][:], rank_at[:].unsqueeze(1).broadcast_to([128, G6, NE]), ALU.is_lt)\
                            .then_inc(on["chosen_ready"], 1)
                    if k == 9:
                        dve.wait_ge(on["lexp_ready"], t + 1)
                        dve.wait_ge(on["chosen_ready"], t + 1)
                        V.tensor_tensor(lexp[u][:], lexp[u][:], chosen[u][:], ALU.mult).then_inc(on["kept_exp"], 1)
                        dve.wait_ge(on["kept_exp"], t + 1)
                        V.tensor_reduce(lsum[u][:], lexp[u][:], AX.X, ALU.add).then_inc(on["sum_ready"], 1)
                        dve.wait_ge(on["sum_ready"], t + 1)
                        V.reciprocal(lrc[u][:], lsum[u][:]).then_inc(on["rcp_ready"], 1)
                        dve.wait_ge(on["rcp_ready"], t + 1)
                        V.tensor_tensor(comb[u][:], lexp[u][:], bc(lrc[u][:]), ALU.mult).then_inc(on["comb_ready"], 1)

                    if k == (12, 11)[u]:
                        dve.wait_ge(on["comb_kept"], t + 1)
                        V.scalar_tensor_tensor(cs[par][u][32:32 + 2 * NE], ct[par][u][:], HSCALE, cs[par][u][0:2 * NE],
                                               ALU.mult, ALU.subtract).then_inc(on["comb_split"], 1)

            def body(n, par, ahead):
                for i in range(SLOTS):
                    ahead(i)
                    if i < 2 * NE:
                        u = i % 2
                        dve.wait_ge(on["spread"], n * (2 * NE) + i + 1)
                        dve.wait_ge(on["gelu_done"], n * (2 * NE) + i + 1)
                        V.tensor_tensor(hm[u][:], hg[u][:], W[:, 0:TC], ALU.mult).then_inc(on["weighted"], 1)
                for u in (0, 1):
                    t = n * 2 + u
                    dve.wait_ge(on["down_done"], t + 1)
                    dve.wait_ge(on["based"], t + 1)
                    dve.wait_ge(stored[u], n * 16 + 1)
                    V.tensor_tensor(y[u][:], Y[u][:, 0:TC], base[par][u][:], ALU.add).then_inc(on["done"], 1)

            pairs(dve, body, front)


def _halves(a):
    return a.reshape((2, HB) + a.shape[1:])


def _dup(a):
    import numpy as np
    return np.concatenate([a, a], 0)


def _diag(a):
    import numpy as np
    z = np.zeros((2, a.shape[0], 2, a.shape[1]), a.dtype)
    z[0, :, 0], z[1, :, 1] = a, a
    return z.reshape(2 * a.shape[0], 2 * a.shape[1])


def swin_inputs(i):
    import numpy as np
    f = np.float32
    x = _halves(i["x"].reshape(NIMG, GRID, 4, GRID, 4))
    patches = x.transpose(0, 3, 5, 1, 2, 4).reshape(32, HB * NTOK)
    blocks, vecs = [], []
    for l in range(2):
        qkv = i["L0_tok_qkv_w"][l]
        blocks += [_diag(qkv[k * C:(k + 1) * C].T) for k in range(3)] + [_diag(i["L0_tok_proj_w"][l].T)]
        blocks += [_diag(i["L0_tok_w1"][l][c * C:(c + 1) * C].T) for c in range(4)]
        blocks += [_diag(i["L0_tok_w2"][l][:, c * C:(c + 1) * C].T) for c in range(4)]
        vecs += [i["L0_tok_" + k][l] for k in ("n1g", "n1b", "n2g", "n2b")]
        vecs += [i["L0_tok_qkv_b"][l][k * C:(k + 1) * C] for k in range(3)] + [i["L0_tok_proj_b"][l], i["L0_tok_b2"][l]]
        vecs += [i["L0_tok_b1"][l][c * C:(c + 1) * C] for c in range(4)]
    vecs += [i["L0_tok_pe_b"], i["L0_tok_pe_ng"], i["L0_tok_pe_nb"]]
    at = np.arange(WT)
    rel = (at[:, None] // WS - at[None] // WS + WS - 1) * (2 * WS - 1) + at[:, None] % WS - at[None] % WS + WS - 1
    part = lambda at: np.where(at < WS - SHIFT, 0, 1)
    row, col = part(at // WS), part(at % WS)
    differ = [np.zeros((WT, WT), bool), col[:, None] != col[None], row[:, None] != row[None]]
    differ.append(differ[1] | differ[2])

    def rows(t):
        z = np.zeros((2, KP, NH * WT), f)
        z[:, :WT] = t.reshape(WT, -1)
        return z.reshape(128, -1)

    rpb = np.concatenate([rows(i["L0_tok_rpb"][l][rel].transpose(0, 2, 1)) for l in range(2)], 1)
    amask = np.concatenate([rows(np.repeat(np.where(d, f(-100), f(0))[:, None], NH, 1)) for d in differ], 1)
    heads = _dup((np.arange(C)[:, None] // HD == np.arange(NH)[None]).astype(f))
    mean = _diag(np.full((C, C), 1.0 / C, f))
    consts = np.stack([np.eye(128, dtype=f), np.eye(128, dtype=f) - mean, mean])
    return {"patches": patches, "wts": np.concatenate(blocks, 1), "pew": _diag(i["L0_tok_pe_w"].reshape(C, 16).T),
            "vec": _dup(np.stack(vecs, 1)), "rpb": rpb, "amask": amask, "hmask": heads, "consts": consts}


def gru_inputs(i):
    import numpy as np
    f = np.float32
    d2 = ("fwd", "rev")
    wih = np.stack([i[f"L0_attn_{d}_w_ih"].reshape(3, C, C) for d in d2])
    wih = _dup(wih.transpose(3, 0, 1, 2).reshape(C, -1))
    whh = np.zeros((2, C, 3, 2, C), f)
    for n, d in enumerate(d2):
        whh[n, :, :, n] = i[f"L0_attn_{d}_w_hh"].reshape(3, C, C).transpose(2, 0, 1)
    bias = [np.concatenate([i[f"L0_attn_{d}_{b}"][g * C:(g + 1) * C] for d in d2]) for b in ("b_ih", "b_hh") for g in range(3)]
    gvec = np.stack([_dup(i["L0_attn_ln_g"])] + bias + [_dup(i["L0_attn_ln_b"])], 1)
    txt = _halves(i["txt"]).transpose(0, 3, 1, 2).reshape(128, HB * NTXT)
    return {"wih": wih, "whh": whh.reshape(128, -1), "gvec": gvec, "txt": txt}


def mixture_inputs(i):
    import numpy as np
    f = np.float32
    eye, zero = np.eye(C, dtype=f), np.zeros((C, C), f)
    ow = i["L0_attn_out_w"].T
    gru_w = np.concatenate([i["L0_attn_gate_w"].T, np.concatenate([eye, -eye]), np.concatenate([zero, ow])], 1)
    wexp = np.concatenate([_diag(i[k][e]) for e in range(NE) for k in ("L0_ffn_w1", "L0_ffn_w2")], 1)
    sel = np.zeros((2, NE, NE, 2, C), f)
    for h in range(2):
        for e in range(NE):
            sel[h, e, e, h] = 1
    mvec = np.stack([_dup(i["L0_attn_out_b"]), _dup(i["L0_attn_gate_b"])] + [_dup(i["L0_ffn_b1"][e]) for e in range(NE)], 1)
    e = np.arange(NE)
    after = (e[None] > e[:, None]).astype(f)
    low = np.repeat(after.reshape(1, -1), 128, 0)
    rank = np.repeat((2 - e).astype(f)[None], 128, 0)
    return {"gru_w": gru_w, "out_w": _diag(ow), "router": _diag(i["L0_ffn_router_w"].T), "wexp": wexp,
            "b2w": _diag(i["L0_ffn_b2"]), "sel_c": sel.reshape(2 * NE, -1), "mvec": mvec, "low_c": low, "rank_c": rank}


def program(nc, a, out):
    dram = lambda name, cols, dt=F32: nc.dram_tensor(name, (128, cols), dt, kind="Internal").ap()
    tok1, tok2 = dram("tok1", HB * NTOK), dram("tok2", HB * NTOK)
    xparts = (dram("x_hi", HB * S, F16), dram("x_lo", HB * S, F16))
    resid, hist = dram("resid", HB * S), dram("hist", NIMG * S)
    swin(nc, a["patches"], a["wts"], a["pew"], a["vec"], a["rpb"], a["amask"], a["hmask"], a["consts"], tok1, tok2)
    prepare(nc, a["consts"], tok2, a["txt"], xparts, resid)
    gru(nc, a["consts"], a["wih"], a["whh"], a["gvec"], xparts, hist)
    mixture(nc, a["consts"], a["gru_w"], a["out_w"], a["router"], a["wexp"], a["b2w"], a["sel_c"], a["mvec"], a["low_c"],
            a["rank_c"], hist, resid, out)


def kernel(**inputs):
    import numpy as np
    import concourse.bacc as bacc
    from concourse.bass_utils import run_bass_kernel_spmd

    i = {k: np.asarray(v) for k, v in inputs.items()}
    arrays = {**swin_inputs(i), **gru_inputs(i), **mixture_inputs(i)}
    arrays = {k: np.ascontiguousarray(v) for k, v in arrays.items()}
    nc = bacc.Bacc("TRN2", target_bir_lowering=False, num_devices=1)
    aps = {k: nc.dram_tensor(k, v.shape, mybir.dt.from_np(v.dtype), kind="ExternalInput").ap() for k, v in arrays.items()}
    out = nc.dram_tensor("out", (128, HB * S), F32, kind="ExternalOutput").ap()
    program(nc, aps, out)
    r = run_bass_kernel_spmd(nc, [arrays], core_ids=[0]).results[0]["out"]
    return r.reshape(2, C, S, HB).transpose(0, 3, 2, 1).reshape(NIMG, S, C)
```

```python
import concourse.bass as bass
from concourse import mybir
from contextlib import ExitStack

F32 = mybir.dt.float32
F16 = mybir.dt.float16
ACT = mybir.ActivationFunctionType
ALU = mybir.AluOpType
AX = mybir.AxisListType

NIMG, HB, C = 16, 8, 64
WS, GRID = 7, 56
SHIFT = WS // 2
NTOK = GRID * GRID
NTXT = 32
S = NTOK + NTXT
NW = GRID // WS
SC = WS * GRID
WT = WS * WS
NH, HD = 8, 8
KP = 64
EPS = 1e-5
LN_EXP = "natural_log_exp_and_others"

N1G, N1B, N2G, N2B, QB, KB, VB, PB, B2, B1 = range(10)
LV = 13
PEB, PEG, PENB = 2 * LV, 2 * LV + 1, 2 * LV + 2
NVEC = 2 * LV + 3
WQ, WK, WV, WP, W1, W2 = 0, 1, 2, 3, 4, 8
LW = 12


def swin(nc, patches, wts, pew, vec, rpb, amask, hmask, consts, tok1, tok2):
    with ExitStack() as ctx:
        def sb(name, shape, dt=F32):
            return ctx.enter_context(nc.sbuf_tensor(name, shape, dt))

        def bank(name):
            return ctx.enter_context(nc.psum_tensor(name, [128, 512], F32))

        def sem(name):
            return ctx.enter_context(nc.semaphore(name))

        w = sb("w", [128, 2, LW, 128])
        pe_w = sb("pe_w", [32, 128])
        v = sb("v", [128, NVEC])
        vf = sb("vf", [128, 2, 8])
        ident = sb("ident", [128, 128])
        center = sb("center", [128, 128])
        mean = sb("mean", [128, 128])
        eps = sb("eps", [128, 1])
        rpb_l = sb("rpb_l", [128, 2, NH * WT])
        am = sb("am", [128, 4, NH * WT])
        hm = sb("hm", [128, NH])
        px = [sb(f"px{u}", [32, SC]) for u in (0, 1)]
        x = [sb(f"x{u}", [128, SC]) for u in range(4)]
        xo = [sb(f"xo{u}", [128, SC]) for u in (0, 1)]
        qbd = [sb(f"qbd{u}", [128, NW, 128]) for u in (0, 1)]
        ks = [sb(f"ks{u}", [128, SC]) for u in (0, 1)]
        vz = [sb(f"vz{u}", [128, NW, 4 * (128 + 2 * HD)]) for u in (0, 1)]
        f_sq, f_ln, f_rs, f_xn = sb("f_sq", [128, SC]), sb("f_ln", [128, SC]), sb("f_rs", [128, SC]), sb("f_xn", [128, 512])
        b_sq, b_ln, b_rs, b_xn = sb("b_sq", [128, SC]), sb("b_ln", [128, SC]), sb("b_rs", [128, SC]), sb("b_xn", [128, SC])
        ot, pj, gh = sb("ot", [128, SC]), sb("pj", [128, SC]), sb("gh", [128, 4, SC])
        R = 4
        kbd = sb("kbd", [128, NH, WT])
        s1 = [sb(f"s1_{r}", [128, NH, WT]) for r in range(R)]
        s2 = [sb(f"s2_{r}", [128, NH, WT]) for r in range(R)]
        ex = [sb(f"ex{r}", [128, NH, WT]) for r in range(R)]
        pn = [sb(f"pn{r}", [128, NH, KP]) for r in range(R)]
        mx = [sb(f"mx{r}", [128, NH]) for r in range(R)]
        sm = [sb(f"sm{r}", [128, NH]) for r in range(R)]
        rc = [sb(f"rc{r}", [128, NH]) for r in range(R)]
        pt = [sb(f"pt{r}", [128, 4, 128]) for r in (0, 1)]

        P, T, O = bank("P"), bank("T"), bank("O")
        F = [bank(f"F{i}") for i in range(3)]
        B = [bank(f"B{i}") for i in range(2)]
        UP = [B[0], B[1], F[1], F[2]]

        weights_loaded = sem("weights_loaded")
        setup_pe = sem("setup_pe")
        setup_dve = sem("setup_dve")
        consts_ready = sem("consts_ready")
        px_loaded = [sem(f"px_loaded{u}") for u in (0, 1)]
        x_loaded = [sem(f"x_loaded{u}") for u in range(4)]
        stored = [[sem(f"stored{l}_{u}") for u in (0, 1)] for l in (0, 1)]
        finished = sem("finished")
        embedded = sem("embedded")
        emb_biased = sem("emb_biased")
        pre_affine = sem("pre_affine")
        x_ready = sem("x_ready")
        centered = {k: sem(f"centered_{k}") for k in "p12"}
        squared = {k: sem(f"squared_{k}") for k in "p12"}
        var_ready = {k: sem(f"var_ready_{k}") for k in "p12"}
        log_ready = {k: sem(f"log_ready_{k}") for k in "p12"}
        rstd_ready = {k: sem(f"rstd_ready_{k}") for k in "p12"}
        normed = {k: sem(f"normed_{k}") for k in "12"}
        q_done, q_kept = sem("q_done"), sem("q_kept")
        k_done, k_kept, kbd_ready = sem("k_done"), sem("k_kept"), sem("kbd_ready")
        v_done, v_kept = sem("v_done"), sem("v_kept")
        scores, biased, max_ready, shifted = sem("scores"), sem("biased"), sem("max_ready"), sem("shifted")
        exps, sum_ready, rcp_ready, probs = sem("exps"), sem("sum_ready"), sem("rcp_ready"), sem("probs")
        transposed, pt_kept = sem("transposed"), sem("pt_kept")
        attended, o_kept = sem("attended"), sem("o_kept")
        projected, proj_biased, res_added = sem("projected"), sem("proj_biased"), sem("res_added")
        up_done, gelu_done, down_done = sem("up_done"), sem("gelu_done"), sem("down_done")

        block = ctx.enter_context(nc.Block())
        EXP_LAG, SUM_LAG, PROB_LAG, T_LAG, AV_LAG = 1, 2, 3, 4, 5
        NSTR = 64
        NR = 4
        NT = NSTR // NR

        def exists(t, r):
            return not isinstance(t, int) or 0 <= t * NR + r < NSTR

        BACK = {5: 1, 6: 1, 7: 1, 0: 2, 1: 2, 2: 2, 3: 2, 4: 2}

        def strips(eng, body):
            for layer in (0, 1):
                body(layer, 0, -1)
                for r in range(NR):
                    body(layer, 0, r)
                with eng.Fori(1, NT - 2) as t:
                    for r in range(NR):
                        body(layer, t, r)
                for r in range(2 * NR + 2):
                    body(layer, NT - 2 + r // NR, r % NR)

        def windowed(t, layer):
            g = t.rearrange("p (r g) -> p r g", g=GRID)
            if layer == 0:
                return [(g.rearrange("p r (w c) -> p w r c", c=WS), 0, NW, 0, WS)]
            n = NW - 1
            return [(g[:, :, SHIFT:SHIFT + n * WS].rearrange("p r (w c) -> p w r c", c=WS), 0, n, 0, WS),
                    (g[:, :, SHIFT + n * WS:GRID], n, 1, 0, WS - SHIFT),
                    (g[:, :, 0:SHIFT], n, 1, WS - SHIFT, WS)]

        def window_cols(t, w0, nw, c0, c1):
            q = t[:, 0:SC].rearrange("p (w r c) -> p w r c", r=WS, c=WS)[:, w0:w0 + nw, :, c0:c1]
            return q if nw > 1 else q[:, 0]

        @block.sync
        def _(sp):
            for dst, src in ((w[:].rearrange("p a b c -> p (a b c)"), wts), (pe_w[:], pew), (v[:], vec),
                             (rpb_l[:].rearrange("p a b -> p (a b)"), rpb),
                             (am[:].rearrange("p a b -> p (a b)"), amask), (hm[:], hmask),
                             (ident[:], consts[0]), (center[:], consts[1]), (mean[:], consts[2])):
                sp.dma_start(dst, src).then_inc(weights_loaded, 16)

            def ends(layer, s, image):
                base = image * NTOK
                if layer == 0:
                    return ((base + s * SC, 0, SC),)
                head = (WS - SHIFT) * GRID
                a = base + s * SC + SHIFT * GRID
                wraps = isinstance(s, int) and s == NW - 1
                return (a, 0, head), (base if wraps else a + head, head, SC)

            def load(layer, s, image):
                src, dst, on = ((patches, px[image % 2], px_loaded[image % 2]) if layer == 0 else
                                (tok1, x[image % 4], x_loaded[image % 4]))
                for at, c0, c1 in ends(layer, s, image):
                    sp.dma_start(dst[:, c0:c1], src[:, bass.ds(at, c1 - c0)]).then_inc(on, 16)

            def store(layer, s, image):
                for at, c0, c1 in ends(layer, s, image):
                    sp.dma_start((tok2 if layer else tok1)[:, bass.ds(at, c1 - c0)],
                                 xo[image % 2][:, c0:c1]).then_inc(stored[layer][image % 2], 16)

            def row(layer, s):
                for image in range(HB):
                    if image >= 2 or not isinstance(s, int) or s > 0:
                        sp.wait_ge(finished, layer * NSTR + s * HB + image - 1)
                    elif layer == 0:
                        sp.wait_ge(embedded, image + 1)
                    if image < HB - 2:
                        load(layer, s, image + 2)
                    elif not isinstance(s, int) or s < NW - 1:
                        load(layer, s + 1, image + 2 - HB)
                    if image >= 2:
                        store(layer, s, image - 2)
                    elif not isinstance(s, int) or s > 0:
                        store(layer, s - 1, image + HB - 2)

            for layer in (0, 1):
                load(layer, 0, 0)
                load(layer, 0, 1)
                row(layer, 0)
                with sp.Fori(1, NW - 2) as s:
                    row(layer, s)
                for s in (NW - 2, NW - 1):
                    row(layer, s)
                for image in (HB - 2, HB - 1):
                    sp.wait_ge(finished, layer * NSTR + (NW - 1) * HB + image + 1)
                    store(layer, NW - 1, image)
                for u in (0, 1):
                    sp.wait_ge(stored[layer][u], (1 + layer) * 16 * NSTR // 2)

        @block.tensor
        def _(pe):
            mm = nc.tensor.matmul
            pe.wait_ge(weights_loaded, 9 * 16)
            for l in (0, 1):
                for i, blk in enumerate((WQ, WK, WV)):
                    mm(F[l][:, i:i + 1], w[:, l, blk, :], v[:, l * LV + N1B:l * LV + N1B + 1], start=True, stop=True)
                for i in range(4):
                    last = mm(F[l][:, 4 + i:5 + i], w[:, l, W1 + i, :], v[:, l * LV + N2B:l * LV + N2B + 1],
                              start=True, stop=True)
            last.then_inc(setup_pe, 1)
            pe.wait_ge(setup_dve, 1)
            for l in (0, 1):
                last = mm(B[l][:, 0:1], w[:, l, WP, :], vf[:, l, 2:3], start=True, stop=True)
            last.then_inc(setup_pe, 1)
            pe.wait_ge(consts_ready, 1)

            def values(b):
                for i in range(4):
                    at = (b * 4 + i) * WT
                    last = mm(F[b][0:KP, i * 128:(i + 1) * 128], f_xn[:, at:at + KP], W[WV], start=True, stop=True)
                last.then_inc(v_done, 1)

            W = {}

            def prepare_strip(layer, t, r, k):
                g = t * NR + r + layer * NSTR
                if k == 0:
                    if not isinstance(g, int) or g > 0:
                        pe.wait_ge(v_kept, g * 2)
                    if layer == 0:
                        pe.wait_ge(px_loaded[r % 2], ((t * (NR // 2) + r // 2) + 1) * 16)
                        mm(F[0][:, 0:SC], pe_w[:], px[r % 2][:], start=True, stop=True).then_inc(embedded, 1)
                if k == 1 and layer == 0:
                    pe.wait_ge(emb_biased, g + 1)
                    mm(F[0][:, 0:SC], center[:], x[r % 4][:], start=True, stop=True).then_inc(centered["p"], 1)
                if k == 2 and layer == 0:
                    pe.wait_ge(squared["p"], g + 1)
                    mm(F[1][:, 0:SC], mean[:], f_sq[:], start=True, stop=True).then_inc(var_ready["p"], 1)
                if k == 3:
                    if layer == 0:
                        pe.wait_ge(x_ready, g + 1)
                    else:
                        pe.wait_ge(x_loaded[r % 4], (t + r // 4 + 1) * 32)
                    mm(F[0][:, 0:SC], center[:], x[r % 4][:], start=True, stop=True).then_inc(centered["1"], 1)
                if k == 4:
                    pe.wait_ge(squared["1"], g + 1)
                    mm(F[1][:, 0:SC], mean[:], f_sq[:], start=True, stop=True).then_inc(var_ready["1"], 1)
                if k == 5:
                    pe.wait_ge(normed["1"], g + 1)
                    mm(F[1][:, 0:SC], W[WQ], f_xn[:, 0:SC], start=True, stop=True).then_inc(q_done, 1)
                    mm(F[2][:, 0:SC], W[WK], f_xn[:, 0:SC], start=True, stop=True).then_inc(k_done, 1)
                if k == 6:
                    values(0)
                if k == 7:
                    pe.wait_ge(q_kept, g + 1)
                    values(1)

            def finish_strip(layer, t, r, k):
                g = t * NR + r + layer * NSTR
                if k == 5:
                    if not isinstance(g, int) or g > 0:
                        pe.wait_ge(finished, g)
                    pe.wait_ge(o_kept, g * 2 + 2)
                    mm(B[0][:, 0:SC], W[WP], ot[:], start=True, stop=True).then_inc(projected, 1)
                if k == 6:
                    pe.wait_ge(res_added, g + 1)
                    mm(B[0][:, 0:SC], center[:], x[r % 4][:], start=True, stop=True).then_inc(centered["2"], 1)
                if k == 7:
                    pe.wait_ge(squared["2"], g + 1)
                    mm(B[1][:, 0:SC], mean[:], b_sq[:], start=True, stop=True).then_inc(var_ready["2"], 1)
                if k == 0:
                    pe.wait_ge(normed["2"], g + 1)
                    if exists(t, r + 2):
                        pe.wait_ge(v_kept, g * 2 + 6)
                        pe.wait_ge(k_kept, g + 3)
                    for c in range(4):
                        mm(UP[c][:, 0:SC], W[W1 + c], b_xn[:], start=True, stop=True).then_inc(up_done, 1)
                if k in (1, 2):
                    pe.wait_ge(gelu_done, g * 4 + 4)
                    for c in (2 * k - 2, 2 * k - 1):
                        last = mm(B[0][:, 0:SC], W[W2 + c], gh[:, c, :], start=c == 0, stop=c == 3)
                    if k == 2:
                        last.then_inc(down_done, 1)

            def body(layer, t, r):
                for blk in range(LW):
                    W[blk] = w[:, layer, blk, :]
                l = t * NR + r
                n = (layer * NSTR + l) * NW
                for k in range(NW):
                    if exists(t, r):
                        if k == 0:
                            pe.wait_ge(q_kept, layer * NSTR + l + 1)
                        pe.wait_ge(kbd_ready, n + k + 1)
                        mm(P[:, 0:NH * WT], qbd[r % 2][:, k, :], kbd[:].rearrange("p h k -> p (h k)"),
                           start=True, stop=True).then_inc(scores, 1)
                    j, d = n + k - T_LAG, (k - T_LAG) // NW
                    if exists(t, r + d):
                        pe.wait_ge(probs, j + 1)
                        if not isinstance(j, int) or j > 0:
                            pe.wait_ge(pt_kept, j)
                        for h in range(4):
                            last = nc.tensor.transpose(T[:, h * 128:(h + 1) * 128],
                                                       pn[(k - T_LAG) % R][:, 2 * h:2 * h + 2, :].rearrange("p h k -> p (h k)"), ident[:])
                        last.then_inc(transposed, 1)
                    j, d, a = n + k - AV_LAG, (k - AV_LAG) // NW, (k - AV_LAG) % NW
                    if exists(t, r + d):
                        pe.wait_ge(pt_kept, j + 1)
                        if a == 0:
                            pe.wait_ge(v_kept, (layer * NSTR + l + d) * 2 + 2)
                        if a % 4 == 0:
                            g2 = (layer * NSTR + l + d) * 2 + a // 4
                            if not isinstance(g2, int) or g2 > 0:
                                pe.wait_ge(o_kept, g2)
                        for h in range(4):
                            last = mm(O[:, (a % 4) * 128:(a % 4 + 1) * 128], vz[(r + d) % 2][:, a, h * 128:(h + 1) * 128],
                                      pt[(k - AV_LAG) % 2][:, h, :], start=h == 0, stop=h == 3)
                        if a % 4 == 3:
                            last.then_inc(attended, 1)
                    if exists(t, r + 1):
                        prepare_strip(layer, t, r + 1, k)
                    if exists(t, r - BACK[k]):
                        finish_strip(layer, t, r - BACK[k], k)

            strips(pe, body)

        @block.scalar
        def _(act):
            A = nc.scalar.activation
            act.wait_ge(consts_ready, 1)
            act.preload_act_table_set(LN_EXP)

            def rstd(k, g, var, ln, rs):
                act.wait_ge(var_ready[k], g + 1)
                A(ln[:], var[:, 0:SC], ACT.Ln, bias=eps[:]).then_inc(log_ready[k], 1)
                act.wait_ge(log_ready[k], g + 1)
                A(rs[:], ln[:], ACT.Exp, scale=-0.5).then_inc(rstd_ready[k], 1)

            def prepare_strip(layer, t, r, k):
                g = t * NR + r + layer * NSTR
                if k == 1 and layer == 0:
                    act.wait_ge(centered["p"], g + 1)
                    A(f_sq[:], F[0][:, 0:SC], ACT.Square).then_inc(squared["p"], 1)
                if k == 2 and layer == 0:
                    rstd("p", g, F[1], f_ln, f_rs)
                if k == 3:
                    act.wait_ge(centered["1"], g + 1)
                    A(f_sq[:], F[0][:, 0:SC], ACT.Square).then_inc(squared["1"], 1)
                if k == 4:
                    rstd("1", g, F[1], f_ln, f_rs)
                if k == 5:
                    act.wait_ge(q_done, g + 1)
                    for h in (0, 1):
                        p = slice(64 * h, 64 * h + 64)
                        last = A(qbd[r % 2][p, :, 64 * h:64 * h + WT], F[1][p, 0:SC].rearrange("p (w t) -> p w t", t=WT),
                                 ACT.Identity, bias=vf[p, layer, 0:1], scale=float(HD) ** -0.5)
                    last.then_inc(q_kept, 1)
                    act.wait_ge(k_done, g + 1)
                    A(ks[r % 2][:], F[2][:, 0:SC], ACT.Identity, bias=vf[:, layer, 1:2]).then_inc(k_kept, 1)
                if k in (6, 7):
                    b = k - 6
                    act.wait_ge(v_done, g * 2 + b + 1)
                    src = F[b][0:KP, :].rearrange("p (w h j e d) -> p w h j e d", w=4, h=2, j=4, e=2)
                    dst = vz[r % 2][:, 4 * b:4 * b + 4].rearrange("p w (j s) -> p w j s", j=4)
                    for e in (0, 1):
                        p = slice(64 * e, 64 * e + 64)
                        for h in (0, 1):
                            c = 64 * h + HD * e
                            last = A(dst[p, :, :, c:c + HD], src[:, :, h, :, e, :], ACT.Copy)
                    last.then_inc(v_kept, 1)

            def finish_strip(layer, t, r, k):
                g = t * NR + r + layer * NSTR
                if k == 5:
                    act.wait_ge(projected, g + 1)
                    A(pj[:], B[0][:, 0:SC], ACT.Identity, bias=vf[:, layer, 3:4]).then_inc(proj_biased, 1)
                if k == 6:
                    act.wait_ge(centered["2"], g + 1)
                    A(b_sq[:], B[0][:, 0:SC], ACT.Square).then_inc(squared["2"], 1)
                if k == 7:
                    rstd("2", g, B[1], b_ln, b_rs)
                if k == 0:
                    for c in range(4):
                        act.wait_ge(up_done, g * 4 + c + 1)
                        A(gh[:, c, :], UP[c][:, 0:SC], ACT.Gelu, bias=vf[:, layer, 4 + c:5 + c]).then_inc(gelu_done, 1)
                    act.preload_act_table_set(LN_EXP)

            def body(layer, t, r):
                l = t * NR + r
                n = (layer * NSTR + l) * NW
                for k in range(NW):
                    if exists(t, r + (k - EXP_LAG) // NW):
                        act.wait_ge(shifted, n + k - EXP_LAG + 1)
                        A(ex[(k - EXP_LAG) % R][:], s2[(k - EXP_LAG) % R][:], ACT.Exp).then_inc(exps, 1)
                    if exists(t, r + (k - T_LAG) // NW):
                        act.wait_ge(transposed, n + k - T_LAG + 1)
                        A(pt[(k - T_LAG) % 2][:].rearrange("p a b -> p (a b)"), T[:], ACT.Copy).then_inc(pt_kept, 1)
                    d, a = (k - AV_LAG) // NW, (k - AV_LAG) % NW
                    if exists(t, r + d) and a % 4 == 3:
                        b = a // 4
                        act.wait_ge(attended, (layer * NSTR + l + d) * 2 + b + 1)
                        for h in (0, 1):
                            p = slice(64 * h, 64 * h + 64)
                            last = A(ot[p, b * 4 * WT:(b + 1) * 4 * WT].rearrange("p (w t) -> p w t", t=WT),
                                     O[p, :].rearrange("p (w t) -> p w t", t=128)[:, :, 64 * h:64 * h + WT], ACT.Copy)
                        last.then_inc(o_kept, 1)
                    if exists(t, r + 1):
                        prepare_strip(layer, t, r + 1, k)
                    if exists(t, r - BACK[k]):
                        finish_strip(layer, t, r - BACK[k], k)

            strips(act, body)

        @block.gpsimd
        def _(pool):
            TT = nc.gpsimd.tensor_tensor

            def body(layer, t, r):
                l = t * NR + r
                n = (layer * NSTR + l) * NW
                for k in range(NW):
                    if exists(t, r):
                        pool.wait_ge(max_ready, n + k + 1)
                        TT(s2[k % R][:], s1[k % R][:], mx[k % R][:].unsqueeze(2).broadcast_to([128, NH, WT]),
                           ALU.subtract).then_inc(shifted, 1)
                    j, i = n + k - PROB_LAG, (k - PROB_LAG) % R
                    if exists(t, r + (k - PROB_LAG) // NW):
                        pool.wait_ge(rcp_ready, j + 1)
                        if not isinstance(j, int) or j >= R:
                            pool.wait_ge(transposed, j - R + 1)
                        TT(pn[i][:, :, 0:WT], ex[i][:], rc[i][:].unsqueeze(2).broadcast_to([128, NH, WT]),
                           ALU.mult).then_inc(probs, 1)

            pool.wait_ge(consts_ready, 1)
            strips(pool, body)

        @block.vector
        def _(dve):
            V = nc.vector
            for t in vz + qbd + pn + [f_xn]:
                V.memset(t[:], 0.0)
            V.memset(eps[:], EPS)
            dve.wait_ge(weights_loaded, 9 * 16)
            dve.wait_ge(setup_pe, 1)
            for l in (0, 1):
                V.tensor_tensor(vf[:, l, 0:3], F[l][:, 0:3], v[:, l * LV + QB:l * LV + VB + 1], ALU.add)
                last = V.tensor_tensor(vf[:, l, 4:8], F[l][:, 4:8], v[:, l * LV + B1:l * LV + B1 + 4], ALU.add)
            last.then_inc(setup_dve, 1)
            dve.wait_ge(setup_pe, 2)
            dve.wait_ge(setup_dve, 1)
            for l in (0, 1):
                V.tensor_scalar(vf[:, l, 0:1], vf[:, l, 0:1], float(HD) ** -0.5, None, ALU.mult)
                V.tensor_tensor(vf[:, l, 3:4], B[l][:, 0:1], v[:, l * LV + PB:l * LV + PB + 1], ALU.add)
                V.tensor_scalar(w[:, l, WQ:WV + 1, :], w[:, l, WQ:WV + 1, :], v[:, l * LV + N1G:l * LV + N1G + 1], None, ALU.mult)
                V.tensor_scalar(w[:, l, W1:W1 + 4, :], w[:, l, W1:W1 + 4, :], v[:, l * LV + N2G:l * LV + N2G + 1], None, ALU.mult)
            for c in range(4):
                last = V.tensor_tensor(am[:, c, :], rpb_l[:, 1, :], am[:, c, :], ALU.add)
            last.then_inc(setup_dve, 1)
            dve.wait_ge(setup_dve, 2)
            V.memset(mx[1][:], 0.0).then_inc(consts_ready, 1)
            col = lambda k: v[:, k:k + 1]

            def prepare_strip(layer, t, r, k):
                g = t * NR + r + layer * NSTR
                if k == 0 and layer == 0:
                    dve.wait_ge(embedded, g + 1)
                    V.tensor_scalar(x[r % 4][:], F[0][:, 0:SC], col(PEB), None, ALU.add).then_inc(emb_biased, 1)
                if k == 2 and layer == 0:
                    dve.wait_ge(rstd_ready["p"], g + 1)
                    V.tensor_tensor(f_ln[:], F[0][:, 0:SC], f_rs[:], ALU.mult).then_inc(pre_affine, 1)
                    dve.wait_ge(pre_affine, g + 1)
                    V.tensor_scalar(x[r % 4][:], f_ln[:], col(PEG), col(PENB), ALU.mult, ALU.add).then_inc(x_ready, 1)
                if k == 4:
                    dve.wait_ge(rstd_ready["1"], g + 1)
                    for (a, w0, nw, c0, c1), (b, *_) in zip(windowed(F[0][:, 0:SC], layer), windowed(f_rs[:], layer)):
                        last = V.tensor_tensor(window_cols(f_xn, w0, nw, c0, c1), a, b, ALU.mult)
                    last.then_inc(normed["1"], 1)

            def finish_strip(layer, t, r, k):
                g = t * NR + r + layer * NSTR
                if k == 5:
                    dve.wait_ge(proj_biased, g + 1)
                    for a, w0, nw, c0, c1 in windowed(x[r % 4][:], layer):
                        last = V.tensor_tensor(a, window_cols(pj, w0, nw, c0, c1), a, ALU.add)
                    last.then_inc(res_added, 1)
                if k == 7:
                    dve.wait_ge(rstd_ready["2"], g + 1)
                    V.tensor_tensor(b_xn[:], B[0][:, 0:SC], b_rs[:], ALU.mult).then_inc(normed["2"], 1)
                if k == 2:
                    dve.wait_ge(down_done, g + 1)
                    if not isinstance(t, int) or t * NR + r >= 2:
                        dve.wait_ge(stored[layer][r % 2], (t * (NR // 2) + r // 2) * 16 * (1 + layer))
                    elif layer == 1:
                        dve.wait_ge(stored[0][r % 2], 16 * NSTR // 2)
                    V.scalar_tensor_tensor(xo[r % 2][:], B[0][:, 0:SC], col(layer * LV + B2), x[r % 4][:],
                                           ALU.add, ALU.add).then_inc(finished, 1)

            def blockdiag(layer, l, r, a):
                if a == 0:
                    dve.wait_ge(k_kept, layer * NSTR + l + 1)
                V.tensor_tensor(kbd[:], ks[r % 2][:, a * WT:(a + 1) * WT].unsqueeze(1).broadcast_to([128, NH, WT]),
                                hm[:].unsqueeze(2).broadcast_to([128, NH, WT]), ALU.mult).then_inc(kbd_ready, 1)

            def body(layer, t, r):
                l = t * NR + r
                n = (layer * NSTR + l) * NW
                for k in range(NW):
                    i = n + k
                    if exists(t, r):
                        if layer == 0:
                            bias = rpb_l[:, 0, :]
                        else:
                            bias = am[:, (2 if isinstance(l, int) and l >= NSTR - HB else 0) + (1 if k == NW - 1 else 0), :]
                        dve.wait_ge(scores, i + 1)
                        V.tensor_tensor(s1[k % R][:].rearrange("p h k -> p (h k)"), P[:, 0:NH * WT], bias,
                                        ALU.add).then_inc(biased, 1)
                        dve.wait_ge(biased, i + 1)
                        V.tensor_reduce(mx[k % R][:], s1[k % R][:], AX.X, ALU.max).then_inc(max_ready, 1)
                        if k < NW - 1:
                            blockdiag(layer, l, r, k + 1)
                        elif exists(t, r + 1):
                            blockdiag(layer, l + 1, r + 1, 0)
                    j = i - SUM_LAG
                    if exists(t, r + (k - SUM_LAG) // NW):
                        dve.wait_ge(exps, j + 1)
                        V.tensor_reduce(sm[(k - SUM_LAG) % R][:], ex[(k - SUM_LAG) % R][:], AX.X, ALU.add).then_inc(sum_ready, 1)
                        dve.wait_ge(sum_ready, j + 1)
                        V.reciprocal(rc[(k - SUM_LAG) % R][:], sm[(k - SUM_LAG) % R][:]).then_inc(rcp_ready, 1)
                    if exists(t, r + 1):
                        prepare_strip(layer, t, r + 1, k)
                    if exists(t, r - BACK[k]):
                        finish_strip(layer, t, r - BACK[k], k)
                    if k == NW - 1 and not exists(t, r) and exists(t, r + 1):
                        blockdiag(layer, l + 1, r + 1, 0)

            strips(dve, body)


ROW = GRID * HB
HSCALE = 4096.0
WSCALE = 256.0
T16 = 16
NBLK = S // T16


def prepare(nc, consts, tok, txt, xparts, resid):
    Q = 4
    with ExitStack() as ctx:
        def sb(name, shape, dt=F32):
            return ctx.enter_context(nc.sbuf_tensor("b_" + name, shape, dt))

        def sem(name):
            return ctx.enter_context(nc.semaphore("b_" + name))

        center, mean = sb("center", [128, 128]), sb("mean", [128, 128])
        eps = sb("eps", [128, 2])
        each = lambda name, dt=F32: [sb(f"{name}{u}", [128, ROW], dt) for u in range(Q)]
        x, sq, l1, l2, r1, r2, xs, res = (each(k) for k in ("x", "sq", "l1", "l2", "r1", "r2", "xs", "res"))
        xa, xb = each("xa", F16), each("xb", F16)
        G = [ctx.enter_context(nc.psum_tensor(f"b_G{u}", [128, 512], F32)) for u in range(Q)]
        O = [ctx.enter_context(nc.psum_tensor(f"b_O{u}", [128, 512], F32)) for u in range(Q)]
        consts_loaded, ready = sem("consts_loaded"), sem("ready")
        loaded = [sem(f"loaded{u}") for u in range(Q)]
        stored = [sem(f"stored{u}") for u in range(Q)]
        centered, squared, var_ready, logs, rstd, hi, full, norm1, done = (
            sem(k) for k in ("centered", "squared", "var_ready", "logs", "rstd", "hi", "full", "norm1", "done"))
        block = ctx.enter_context(nc.Block())

        def tiles(eng, body):
            with eng.Fori(0, GRID // Q) as n:
                body(n, range(Q), GRID)
            body(GRID // Q, (0,), NTXT)

        def by_image(t, nt):
            return t[:, 0:HB * nt].rearrange("p (b t) -> p t b", t=nt)

        def by_token(t, nt):
            return t[:, 0:HB * nt].rearrange("p (t b) -> p t b", b=HB)

        @block.sync
        def _(sp):
            sp.dma_start(center[:], consts[1]).then_inc(consts_loaded, 16)
            sp.dma_start(mean[:], consts[2]).then_inc(consts_loaded, 16)
            rows = tok.rearrange("p (b t) -> p b t", b=HB)

            def load(tile, u, nt):
                src = rows[:, :, bass.ds(tile * GRID, nt)] if nt == GRID else txt.rearrange("p (b t) -> p b t", b=HB)
                sp.dma_start(x[u][:, 0:HB * nt].rearrange("p (b t) -> p b t", b=HB), src).then_inc(loaded[u], 16)

            def store(tile, u, nt):
                sp.wait_ge(done, tile + 1)
                at = bass.ds(tile * ROW, HB * nt)
                for dst, t in ((xparts[0], xa[u]), (xparts[1], xb[u]), (resid, res[u])):
                    sp.dma_start(dst[:, at], t[:, 0:HB * nt]).then_inc(stored[u], 16)

            for u in range(Q):
                load(u, u, GRID)
            with sp.Fori(0, GRID // Q - 1) as n:
                for u in range(Q):
                    store(n * Q + u, u, GRID)
                    load(n * Q + Q + u, u, GRID)
            for u in range(Q):
                store(GRID - Q + u, u, GRID)
                if u == 0:
                    load(GRID, 0, NTXT)
            store(GRID, 0, NTXT)
            for u in range(Q):
                sp.wait_ge(stored[u], 48 * (GRID // Q + (u == 0)) + 1)

        @block.tensor
        def _(pe):
            pe.wait_ge(consts_loaded, 32)

            def body(n, us, nt):
                m, w = n * Q, HB * nt
                for u in us:
                    pe.wait_ge(loaded[u], 16 * n + 16)
                    nc.tensor.matmul(G[u][:, 0:w], center[:], x[u][:, 0:w], start=True, stop=True).then_inc(centered, 1)
                for u in us:
                    pe.wait_ge(squared, m + u + 1)
                    nc.tensor.matmul(O[u][:, 0:w], mean[:], sq[u][:, 0:w], start=True, stop=True).then_inc(var_ready, 1)

            tiles(pe, body)

        @block.scalar
        def _(act):
            A = nc.scalar.activation
            act.wait_ge(ready, 1)
            act.preload_act_table_set(LN_EXP)

            def body(n, us, nt):
                m, w = n * Q, HB * nt
                for u in us:
                    act.wait_ge(centered, m + u + 1)
                    A(sq[u][:, 0:w], G[u][:, 0:w], ACT.Square).then_inc(squared, 1)
                for u in us:
                    act.wait_ge(var_ready, m + u + 1)
                    A(l1[u][:, 0:w], O[u][:, 0:w], ACT.Ln, bias=eps[:, 0:1])
                    A(l2[u][:, 0:w], O[u][:, 0:w], ACT.Ln, bias=eps[:, 1:2], scale=1.0 + EPS).then_inc(logs, 1)
                    act.wait_ge(logs, m + u + 1)
                    A(r1[u][:, 0:w], l1[u][:, 0:w], ACT.Exp, scale=-0.5)
                    A(r2[u][:, 0:w], l2[u][:, 0:w], ACT.Exp, scale=-0.5).then_inc(rstd, 1)

            tiles(act, body)

        @block.vector
        def _(dve):
            V = nc.vector
            V.memset(eps[:, 0:1], EPS)
            V.memset(eps[:, 1:2], EPS * EPS)
            for u in range(Q):
                V.memset(l1[u][:, 0:1], 0.0).then_inc(stored[u], 1)
            V.memset(res[0][:], 0.0).then_inc(ready, 1)
            dve.wait_ge(ready, 1)

            def body(n, us, nt):
                m = n * Q
                for u in us:
                    dve.wait_ge(rstd, m + u + 1)
                    dve.wait_ge(stored[u], n * 48 + 1)
                    c = by_image(G[u], nt)
                    V.scalar_tensor_tensor(by_token(xa[u], nt), c, HSCALE, by_image(r2[u], nt), ALU.mult, ALU.mult).then_inc(hi, 1)
                    V.scalar_tensor_tensor(by_token(xs[u], nt), c, HSCALE, by_image(r2[u], nt), ALU.mult, ALU.mult).then_inc(full, 1)
                    V.tensor_tensor(by_token(l1[u], nt), c, by_image(r1[u], nt), ALU.mult).then_inc(norm1, 1)
                    dve.wait_ge(full, m + u + 1)
                    V.tensor_tensor(xb[u][:, 0:HB * nt], xs[u][:, 0:HB * nt], xa[u][:, 0:HB * nt], ALU.subtract)
                    dve.wait_ge(norm1, m + u + 1)
                    V.tensor_tensor(by_token(res[u], nt), by_token(l1[u], nt), by_image(x[u], nt), ALU.add).then_inc(done, 1)

            tiles(dve, body)


def gru(nc, consts, wih, whh, gvec, xparts, hist):
    B, T = NIMG, T16
    with ExitStack() as ctx:
        def sb(name, shape, dt=F32):
            return ctx.enter_context(nc.sbuf_tensor("g_" + name, shape, dt))

        def sem(name):
            return ctx.enter_context(nc.semaphore("g_" + name))

        wi = sb("wi", [128, 2, 3, C])
        wh = sb("wh", [128, 3, 128])
        vecs = sb("vecs", [128, 8])
        ident = sb("ident", [128, 128])
        ident_s = sb("ident_s", [128, 128], F16)
        bias = sb("bias", [128, 4])
        gb = vecs[:, 1:8]
        wi_f = sb("wi_f", [128, 2, 3, C])
        wi1 = sb("wi1", [128, 2, 2, 3, C], F16)
        wi2 = sb("wi2", [128, 2, 2, 3, C], F16)
        wh1, wh2 = sb("wh1", [128, 3, 128], F16), sb("wh2", [128, 3, 128], F16)
        bias_f = sb("bias_f", [128, 4, T * B])
        bias1, bias2 = sb("bias1", [128, 4, T * B], F16), sb("bias2", [128, 4, T * B], F16)
        x = sb("x", [128, 2, 2, 2, T, HB], F16)
        h = sb("h", [128, 2, T, B])
        zero = sb("zero", [128, B], F16)
        rz, pre_n = sb("rz", [128, 2, B, 2]), sb("pre_n", [128, B, 2])
        n_, omz, zh, zn = (sb(k, [128, B]) for k in ("n", "omz", "zh", "zn"))
        one_s = sb("one_s", [128, 1])
        zh1, zh2, zn1, zn2 = (sb(k, [128, B], F16) for k in ("zh1", "zh2", "zn1", "zn2"))
        RZ = [ctx.enter_context(nc.psum_tensor(f"g_RZ{u}", [128, 2, T, B], F32)) for u in (0, 1)]
        NX = [ctx.enter_context(nc.psum_tensor(f"g_NX{u}", [128, T, B, 2], F32)) for u in (0, 1)]
        BP = ctx.enter_context(nc.psum_tensor("g_BP", [128, 512], F32))

        weights_loaded, bias_products, link, ready = sem("weights_loaded"), sem("bias_products"), sem("link"), sem("ready")
        x_loaded = [sem("x_loaded0"), sem("x_loaded1")]
        h_stored, h_ready = [sem("h_stored0"), sem("h_stored1")], sem("h_ready")
        projected = sem("projected")
        gates_ready, nh_ready, rz_ready = sem("gates_ready"), sem("nh_ready"), sem("rz_ready")
        pre_n_ready, n_ready = sem("pre_n_ready"), sem("n_ready")
        zh_ready, zh1_ready, zh2_ready, zn1_ready, zn2_ready, zn_ready = (
            sem(k) for k in ("zh_ready", "zh1_ready", "zh2_ready", "zn1_ready", "zn2_ready", "zn_ready"))
        block = ctx.enter_context(nc.Block())

        def blocks(eng, body):
            body(0, True, False)
            with eng.Fori(1, NBLK // 2 - 1) as i:
                body(i, False, False)
            body(NBLK // 2 - 1, False, True)

        flat = lambda t: t.rearrange("p a b -> p (a b)")

        @block.sync
        def _(sp):
            for dst, src in ((wi[:].rearrange("p a b c -> p (a b c)"), wih), (flat(wh[:]), whh), (vecs[:], gvec),
                             (ident[:], consts[0])):
                sp.dma_start(dst, src).then_inc(weights_loaded, 16)

            def load(k, u):
                for p in (0, 1):
                    sp.dma_start(flat(x[:, u, 0, p]), xparts[p][:, bass.ds(k * (T * HB), T * HB)]).then_inc(x_loaded[u], 16)
                    sp.dma_start(flat(x[:, u, 1, p]), xparts[p][:, bass.ds((NBLK - 1 - k) * (T * HB), T * HB)])\
                        .then_inc(x_loaded[u], 16)

            load(0, 0)
            load(1, 1)

            def body(i, first, last):
                for u in (0, 1):
                    k = i * 2 + u
                    if not last:
                        if first and u == 0:
                            sp.wait_ge(gates_ready, 1)
                        else:
                            sp.wait_ge(projected, k)
                        load(k + 2, u)
                    sp.wait_ge(h_ready, (k + 1) * T)
                    sp.dma_start(hist[:, bass.ds(k * (T * B), T * B)], flat(h[:, u])).then_inc(h_stored[u], 16)

            blocks(sp, body)
            for u in (0, 1):
                sp.wait_ge(h_stored[u], 16 * NBLK // 2)

        PROJ = [(g, d, half, w, p) for g in range(3) for d in (0, 1) for half in (0, 1)
                for w, p in ((wi1, 0), (wi2, 0), (wi1, 1))]

        @block.tensor
        def _(pe):
            def mm(dst, a, b, start=False):
                return nc.tensor.matmul(dst, a, b, start=start, stop=True, skip_group_check=True)

            pe.wait_ge(weights_loaded, 4 * 16)
            for d in (0, 1):
                for g in range(3):
                    last = mm(BP[C * d:C * d + C, g:g + 1], wi[0:C, d, g, :], gb[0:C, 6:7], start=True)
            last.then_inc(bias_products, 1)
            pe.wait_ge(ready, 1)

            def set_biases(u, i):
                bank, c = ((RZ[u], 0), (NX[u], 2))[i // 2]
                mm(bank[:].rearrange("p a b c -> p (a b c)"), ident_s[:], flat((bias1, bias2)[i % 2][:, c:c + 2]), start=i % 2 == 0)

            def project(u, i):
                g, d, half, w, p = PROJ[i]
                dst = (RZ[u][:, g] if g < 2 else NX[u][:, :, :, 1])[C * d:C * d + C, :, HB * half:HB * half + HB]
                src = x[:, u, d, p]
                return mm(dst, w[:, half, d, g, :], src[:, ::-1, :] if d else src)

            def state(part, u, j, low, last=False):
                for g, dst in enumerate((RZ[u][:, 0, j], RZ[u][:, 1, j], NX[u][:, j, :, 0])):
                    m = mm(dst, wh1[:, g, :], part[:])
                    if not low:
                        m = mm(dst, wh2[:, g, :], part[:])
                    if last and g == 1:
                        m.then_inc(gates_ready, 1)
                if last:
                    m.then_inc(nh_ready, 1)

            pe.wait_ge(x_loaded[0], 64)
            for i in range(4):
                set_biases(0, i)
            for i in range(len(PROJ)):
                m = project(0, i)
            m.then_inc(gates_ready, 1)
            mm(NX[0][:, 0, :, 0], wh1[:, 2, :], zero[:]).then_inc(nh_ready, 1)

            def body(i, first, last):
                for u in (0, 1):
                    k = i * 2 + u
                    more = not (last and u == 1)
                    for j in range(T):
                        s = k * T + j
                        if more and j < 4:
                            set_biases(1 - u, j)
                        if more and j == 4:
                            pe.wait_ge(x_loaded[1 - u], (i + 1 + u) * 64)
                        if more and j >= 4:
                            n = len(PROJ) // (T - 4)
                            for q in range(n * (j - 4), n * (j - 3)):
                                m = project(1 - u, q)
                            if j == T - 1:
                                m.then_inc(projected, 1)
                        if more or j < T - 1:
                            to = (u, j + 1) if j < T - 1 else (1 - u, 0)
                            pe.wait_ge(zh1_ready, s + 1)
                            state(zh1, *to, low=False)
                            pe.wait_ge(zh2_ready, s + 1)
                            state(zh2, *to, low=True)
                            pe.wait_ge(zn1_ready, s + 1)
                            state(zn1, *to, low=False)
                            pe.wait_ge(zn2_ready, s + 1)
                            state(zn2, *to, low=True, last=True)

            blocks(pe, body)

        @block.scalar
        def _(act):
            unscale = 1.0 / (HSCALE * WSCALE)

            def body(i, first, last):
                for u in (0, 1):
                    for j in range(T):
                        s = (i * 2 + u) * T + j
                        act.wait_ge(gates_ready, s + 1)
                        nc.scalar.activation(rz[:, :, :, 1], RZ[u][:, :, j, :], ACT.Sigmoid, scale=unscale).then_inc(rz_ready, 1)
                        act.wait_ge(rz_ready, s + 1)
                        nc.scalar.activation(omz[:], rz[:, 1, :, 1], ACT.Identity, scale=-HSCALE, bias=one_s[:])
                        act.wait_ge(pre_n_ready, s + 1)
                        nc.scalar.activation(n_[:], pre_n[:, :, 1], ACT.Tanh, scale=unscale).then_inc(n_ready, 1)

            blocks(act, body)

        @block.vector
        def _(dve):
            V = nc.vector
            count = [0]

            def chain(op):
                count[0] += 1
                op.then_inc(link, 1)
                dve.wait_ge(link, count[0])

            dve.wait_ge(weights_loaded, 4 * 16)
            for t in (wi1, wi2, h, zero, bias_f, rz):
                chain(V.memset(t[:], 0.0))
            chain(V.memset(one_s[:], HSCALE))
            dve.wait_ge(bias_products, 1)
            chain(V.tensor_tensor(bias[:, 0:3], BP[:, 0:3], gb[:, 0:3], ALU.add))
            chain(V.tensor_tensor(bias[:, 0:2], bias[:, 0:2], gb[:, 3:5], ALU.add))
            chain(V.tensor_copy(bias[:, 3:4], gb[:, 5:6]))
            chain(V.tensor_scalar(bias[:], bias[:], WSCALE, None, ALU.mult))
            chain(V.tensor_scalar(ident_s[:], ident[:], HSCALE, None, ALU.mult))
            chain(V.tensor_scalar(wi_f[:], wi[:], vecs[:, 0:1], WSCALE, ALU.mult, ALU.mult))
            chain(V.tensor_scalar(wh[:], wh[:], WSCALE, None, ALU.mult))
            for half in (0, 1):
                r = slice(C * half, C * half + C)
                chain(V.tensor_copy(wi1[r, half], wi_f[r]))
                chain(V.tensor_tensor(wi2[r, half], wi_f[r], wi1[r, half], ALU.subtract))
            chain(V.tensor_copy(wh1[:], wh[:]))
            chain(V.tensor_tensor(wh2[:], wh[:], wh1[:], ALU.subtract))
            for q in (0, 1):
                chain(V.tensor_scalar(bias_f[:, q, :], bias_f[:, q, :], bias[:, q:q + 1], None, ALU.add))
            side = flat(bias_f[:, 2:4]).rearrange("p (c e) -> p c e", e=2)
            for e, q in ((0, 3), (1, 2)):
                chain(V.tensor_scalar(side[:, :, e], side[:, :, e], bias[:, q:q + 1], None, ALU.add))
            chain(V.tensor_copy(bias1[:], bias_f[:]))
            V.tensor_tensor(bias2[:], bias_f[:], bias1[:], ALU.subtract).then_inc(ready, 1)

            def body(i, first, last):
                for u in (0, 1):
                    k = i * 2 + u
                    for j in range(T):
                        s = k * T + j
                        before = h[:, u, j - 1] if j else h[:, 1 - u, T - 1]
                        dve.wait_ge(rz_ready, s + 1)
                        dve.wait_ge(nh_ready, s + 1)
                        V.tensor_tensor_scan(pre_n[:].rearrange("p b e -> p (b e)"), rz[:, 0].rearrange("p b e -> p (b e)"),
                                             NX[u][:, j].rearrange("p b e -> p (b e)"), 0.0, ALU.mult, ALU.add)\
                            .then_inc(pre_n_ready, 1)
                        if not (first and s == 0):
                            dve.wait_ge(h_ready, s)
                        V.tensor_tensor(zh1[:], rz[:, 1, :, 1], before, ALU.mult).then_inc(zh1_ready, 1)
                        V.tensor_tensor(zh[:], rz[:, 1, :, 1], before, ALU.mult).then_inc(zh_ready, 1)
                        dve.wait_ge(zh_ready, s + 1)
                        V.tensor_tensor(zh2[:], zh[:], zh1[:], ALU.subtract).then_inc(zh2_ready, 1)
                        dve.wait_ge(n_ready, s + 1)
                        V.tensor_tensor(zn1[:], n_[:], omz[:], ALU.mult).then_inc(zn1_ready, 1)
                        V.tensor_tensor(zn[:], n_[:], omz[:], ALU.mult).then_inc(zn_ready, 1)
                        dve.wait_ge(zn_ready, s + 1)
                        V.tensor_tensor(zn2[:], zn[:], zn1[:], ALU.subtract).then_inc(zn2_ready, 1)
                        if j == 0 and not first:
                            dve.wait_ge(h_stored[u], 16 * i)
                        V.tensor_tensor(h[:, u, j], zn[:], zh[:], ALU.add).then_inc(h_ready, 1)

            blocks(dve, body)


NE = 8
TT = 48
TC = TT * HB
CH = TC // 128
MSTEP = S // TT // 2
MV_OB, MV_GB, MV_B1 = 0, 1, 2


def mixture(nc, consts, gru_w, out_w, router, wexp, b2w, sel_c, mvec, low_c, rank_c, hist, resid, out):
    with ExitStack() as ctx:
        def sb(name, shape, dt=F32):
            return ctx.enter_context(nc.sbuf_tensor("m_" + name, shape, dt))

        def sem(name):
            return ctx.enter_context(nc.semaphore("m_" + name))

        def bank(name):
            return ctx.enter_context(nc.psum_tensor("m_" + name, [128, 512], F32))

        two = lambda name, shape: [sb(f"{name}{u}", shape) for u in (0, 1)]
        ident, center, mean = sb("ident", [128, 128]), sb("center", [128, 128]), sb("mean", [128, 128])
        gw = sb("gw", [128, 3, C])
        ow, rw, we = sb("ow", [128, 128]), sb("rw", [128, 2 * NE]), sb("we", [128, NE, 2, 128])
        bw, sel = sb("bw", [2 * NE, 128]), sb("sel", [2 * NE, NE, 128])
        mv, low, rank_at = sb("mv", [128, 10]), sb("low", [128, NE, NE]), sb("rank_at", [128, NE])
        eps = sb("eps", [128, 1])
        fr, rev = two("fr", [128, TT, NIMG]), two("rev", [128, TT, NIMG])
        res, th, p = two("res", [128, TC]), two("th", [128, TC]), two("p", [128, TC])
        h2, sq, lnv, rs = (two(k, [128, TC]) for k in ("h2", "sq", "lnv", "rs"))
        xn, base = ([two(f"{k}{i}", [128, TC]) for i in (0, 1)] for k in ("xn", "base"))
        G6 = CH * 2
        lg, lx, lexp, rank, chosen, comb = (two(k, [128, G6, NE]) for k in ("lg", "lx", "lexp", "rank", "chosen", "comb"))
        beat = two("beat", [128, G6, NE, NE])
        rk2 = two("rk2", [128, G6, NE])
        lmx, lsum, lrc = (two(k, [128, G6]) for k in ("lmx", "lsum", "lrc"))
        ct = [two(f"ct{i}", [2 * NE, TC]) for i in (0, 1)]
        cs = [[sb(f"cs{i}{u}", [48, TC], F16) for u in (0, 1)] for i in (0, 1)]
        sel16 = sb("sel16", [48, NE, 128], F16)
        cen = sb("cen", [128, TC])
        LU = 256
        hg, hm = two("hg", [128, TC]), two("hm", [128, TC])
        y = two("y", [128, TC])
        A_, B_, L, W = (bank(k) for k in "ABLW")
        U, Y = ([bank(f"{k}{u}") for u in (0, 1)] for k in "UY")

        weights_loaded, scaled, ready = sem("weights_loaded"), sem("scaled"), sem("ready")
        loaded, stored = [sem("loaded0"), sem("loaded1")], [sem("stored0"), sem("stored1")]
        names = ("aligned gate_done tanh_done gated mixed summed centered squared var_ready log_ready rstd_ready normed "
                 "based routed logits_kept max_ready less_max beat_ready beat_upper ranks_a rank_ready lexp_ready chosen_ready "
                 "kept_exp sum_ready rcp_ready comb_ready comb_t comb_kept cen_kept comb_split up_done spread gelu_done weighted down_done done").split()
        on = {k: sem(k) for k in names}
        block = ctx.enter_context(nc.Block())
        SLOTS, LATER = 2 * NE + 2, 4

        def piece(i, u, apart=8):
            k = i - LATER * u
            if i < 2 * LATER:
                return k if k < LATER else None
            k = i - LATER
            return k if u == 0 or k < apart else k - 1 if k > apart else None

        def pairs(eng, body, front):
            for i in range(SLOTS):
                front(0, 0, i)
            with eng.Fori(0, (MSTEP - 1) // 2) as k:
                for par in (0, 1):
                    n = 2 * k + par
                    body(n, par, lambda i: front(n + 1, 1 - par, i))
            body(MSTEP - 1, 0, lambda i: None)

        @block.sync
        def _(sp):
            flat = lambda t: t.rearrange("p a b -> p (a b)")
            for dst, src in ((ident[:], consts[0]), (center[:], consts[1]), (mean[:], consts[2]), (flat(gw[:]), gru_w),
                             (ow[:], out_w), (rw[:], router), (we[:].rearrange("p a b c -> p (a b c)"), wexp), (bw[:], b2w),
                             (flat(sel[:]), sel_c), (mv[:], mvec), (flat(low[:]), low_c), (rank_at[:], rank_c)):
                sp.dma_start(dst, src).then_inc(weights_loaded, 16)

            def load(t, u):
                sp.dma_start(flat(fr[u][0:C]), hist[0:C, bass.ds(t * (TT * NIMG), TT * NIMG)]).then_inc(loaded[u], 16)
                sp.dma_start(flat(rev[u][C:128]), hist[C:128, bass.ds((2 * MSTEP - 1 - t) * (TT * NIMG), TT * NIMG)])\
                    .then_inc(loaded[u], 16)
                sp.dma_start(res[u][:], resid[:, bass.ds(t * TC, TC)]).then_inc(loaded[u], 16)

            def reload(n):
                for u in (0, 1):
                    sp.wait_ge(on["summed"], n * 2 + u + 1)
                    load(n * 2 + 2 + u, u)

            def store(n):
                for u in (0, 1):
                    t = n * 2 + u
                    sp.wait_ge(on["done"], t + 3)
                    sp.dma_start(out[:, bass.ds(t * TC, TC)], y[u][:]).then_inc(stored[u], 16)

            load(0, 0)
            load(1, 1)
            reload(0)
            with sp.Fori(0, MSTEP - 2) as n:
                reload(n + 1)
                store(n)
            store(MSTEP - 2)
            store(MSTEP - 1)
            for u in (0, 1):
                sp.wait_ge(stored[u], 16 * MSTEP + 1)

        @block.gpsimd
        def _(pool):
            def front(n, par, i):
                for u in (0, 1):
                    if piece(i, u) == 5:
                        pool.wait_ge(on["normed"], n * 2 + u + 1)
                        nc.gpsimd.tensor_tensor(base[par][u][:], h2[u][:], xn[par][u][:], ALU.add).then_inc(on["based"], 1)

            def body(n, par, ahead):
                for i in range(SLOTS):
                    ahead(i)

            pairs(pool, body, front)

        @block.tensor
        def _(pe):
            def mm(dst, a, b, start=True, stop=True, **k):
                return nc.tensor.matmul(dst, a, b, start=start, stop=stop, **k)

            pe.wait_ge(ready, 3)

            def front(n, par, i):
                for u in (0, 1):
                    t, k = n * 2 + u, piece(i, u)
                    if k == 0:
                        pe.wait_ge(loaded[u], n * 48 + 48)
                        pe.wait_ge(on["aligned"], t + 1)
                        if u == 1:
                            pe.wait_ge(on["summed"], t)
                            pe.wait_ge(on["cen_kept"], n + 1)
                        elif not (isinstance(t, int) and t == 0):
                            pe.wait_ge(on["normed"], t)
                            pe.wait_ge(on["comb_kept"], t)
                        for w, bk in ((0, A_), (1, B_)):
                            for half in (0, 1):
                                last = mm(bk[C * half:C * half + C, 0:TC], gw[:, w, :], fr[u][:, :, HB * half:HB * half + HB])
                        last.then_inc(on["gate_done"], 1)
                    if k == 1:
                        pe.wait_ge(on["gated"], t + 1)
                        for half in (0, 1):
                            mm(A_[C * half:C * half + C, 0:TC], gw[:, 2, :], fr[u][:, :, HB * half:HB * half + HB])
                        mm(A_[:, 0:TC], ow[:], p[u][:], start=False, skip_group_check=True).then_inc(on["mixed"], 1)
                    if k == 2:
                        pe.wait_ge(on["summed"], t + 1)
                        mm(B_[:, 0:TC], center[:], h2[u][:]).then_inc(on["centered"], 1)
                    if k == 3:
                        pe.wait_ge(on["squared"], t + 1)
                        mm((L, A_)[u][:, 0:TC], mean[:], sq[u][:]).then_inc(on["var_ready"], 1)
                    if k == 5:
                        pe.wait_ge(on["normed"], t + 1)
                        for c in range(CH):
                            last = mm(L[:, LU * u + 2 * NE * c:LU * u + 2 * NE * (c + 1)], xn[par][u][:, 128 * c:128 * (c + 1)], rw[:])
                        last.then_inc(on["routed"], 1)
                    if k == 10:
                        pe.wait_ge(on["comb_ready"], t + 1)
                        for c in range(CH):
                            last = nc.tensor.transpose((L, A_)[u][0:2 * NE, 128 * c:128 * (c + 1)],
                                                       comb[u][:, 2 * c:2 * c + 2, :].rearrange("p a b -> p (a b)"), ident[:])
                        last.then_inc(on["comb_t"], 1)

            def body(n, par, ahead):
                m = n * 2
                for i in range(SLOTS):
                    if i >= 2:
                        e, u = (i - 2) // 2, i % 2
                        pe.wait_ge(on["weighted"], m * NE + i - 2 + 1)
                        last = mm(Y[u][:, 0:TC], we[:, e, 1, :], hm[u][:], start=False, stop=e == NE - 1)
                        if e == NE - 1:
                            last.then_inc(on["down_done"], 1)
                    if i < 2 * NE:
                        e, u = i // 2, i % 2
                        mm(U[u][:, 0:TC], we[:, e, 0, :], xn[par][u][:]).then_inc(on["up_done"], 1)
                        if e == 0:
                            pe.wait_ge(on["comb_kept"], m + u + 1)
                            pe.wait_ge(on["done"], m + u + 1)
                            mm(Y[u][:, 0:TC], bw[:], ct[par][u][:], stop=False)
                        if i >= 1:
                            pe.wait_ge(on["weighted"], m * NE + i)
                        if e == 0:
                            pe.wait_ge(on["comb_split"], m + u + 1)
                        mm(W[:, 0:TC], sel16[:, e, :], cs[par][u][:]).then_inc(on["spread"], 1)
                    ahead(i)

            pairs(pe, body, front)

        @block.scalar
        def _(act):
            A = nc.scalar.activation
            act.wait_ge(ready, 3)

            def front(n, par, i):
                for u in (0, 1):
                    t, k = n * 2 + u, piece(i, u)
                    if k == 0:
                        act.wait_ge(loaded[u], n * 48 + 48)
                        A(fr[u][C:128], rev[u][C:128, ::-1, :], ACT.Copy).then_inc(on["aligned"], 1)
                    if k == 1:
                        act.wait_ge(on["gate_done"], t + 1)
                        A(th[u][:], A_[:, 0:TC], ACT.Tanh, scale=0.5, bias=mv[:, MV_GB:MV_GB + 1]).then_inc(on["tanh_done"], 1)
                    if k == 3:
                        act.wait_ge(on["centered"], t + 1)
                        A(sq[u][:], B_[:, 0:TC], ACT.Square).then_inc(on["squared"], 1)
                    if k == 4:
                        if u == 0:
                            act.preload_act_table_set(LN_EXP)
                        act.wait_ge(on["var_ready"], t + 1)
                        A(lnv[u][:], (L, A_)[u][:, 0:TC], ACT.Ln, bias=eps[:]).then_inc(on["log_ready"], 1)
                        act.wait_ge(on["log_ready"], t + 1)
                        A(rs[u][:], lnv[u][:], ACT.Exp, scale=-0.5).then_inc(on["rstd_ready"], 1)
                    if k == 7:
                        act.wait_ge(on["less_max"], t + 1)
                        A(lexp[u][:], lx[u][:], ACT.Exp).then_inc(on["lexp_ready"], 1)
                    if k == 11:
                        act.wait_ge(on["comb_t"], t + 1)
                        A(ct[par][u][:], (L, A_)[u][0:2 * NE, 0:TC], ACT.Copy)
                        A(cs[par][u][0:2 * NE], (L, A_)[u][0:2 * NE, 0:TC], ACT.Copy, scale=HSCALE).then_inc(on["comb_kept"], 1)

            def body(n, par, ahead):
                for i in range(SLOTS):
                    ahead(i)
                    if i < 2 * NE:
                        e, u = i // 2, i % 2
                        act.wait_ge(on["up_done"], n * (2 * NE) + i + 1)
                        A(hg[u][:], U[u][:, 0:TC], ACT.Gelu, bias=mv[:, MV_B1 + e:MV_B1 + e + 1]).then_inc(on["gelu_done"], 1)

            pairs(act, body, front)

        @block.vector
        def _(dve):
            V = nc.vector
            dve.wait_ge(weights_loaded, 12 * 16)
            V.memset(eps[:], EPS).then_inc(stored[0], 1)
            V.memset(lmx[0][:], 0.0).then_inc(stored[1], 1)
            V.tensor_scalar(gw[:, 0, :], gw[:, 0, :], 1.0 / HSCALE, None, ALU.mult)
            V.tensor_scalar(gw[:, 1, :], gw[:, 1, :], 0.5 / HSCALE, None, ALU.mult)
            V.tensor_scalar(gw[:, 2, :], gw[:, 2, :], 1.0 / HSCALE, None, ALU.mult)
            V.tensor_scalar(mv[:, MV_GB:MV_GB + 1], mv[:, MV_GB:MV_GB + 1], 0.5, None, ALU.mult).then_inc(on["done"], 1)
            V.memset(hg[0][:, 0:1], 0.0).then_inc(on["done"], 1)
            dve.wait_ge(on["done"], 2)
            V.memset(hg[1][:, 0:1], 0.0).then_inc(ready, 1)
            dve.wait_ge(ready, 1)
            for t in (cs[0] + cs[1]):
                V.memset(t[:], 0.0)
            V.memset(sel16[:], 0.0).then_inc(scaled, 1)
            dve.wait_ge(scaled, 1)
            for r in (0, 32):
                V.tensor_scalar(sel16[r:r + 2 * NE], sel[:], 1.0 / HSCALE, None, ALU.mult).then_inc(ready, 1)
            bc = lambda t: t.unsqueeze(2).broadcast_to([128, G6, NE])

            def front(n, par, i):
                for u in (0, 1):
                    t, k = n * 2 + u, piece(i, u, 7)
                    if k == 1:
                        dve.wait_ge(on["tanh_done"], t + 1)
                        V.scalar_tensor_tensor(p[u][:], th[u][:], 1.0, B_[:, 0:TC], ALU.add, ALU.mult).then_inc(on["gated"], 1)
                    if k == 2:
                        dve.wait_ge(on["mixed"], t + 1)
                        if not (isinstance(t, int) and t < 2):
                            dve.wait_ge(on["based"], t - 1)
                        V.scalar_tensor_tensor(h2[u][:], A_[:, 0:TC], mv[:, MV_OB:MV_OB + 1], res[u][:], ALU.add, ALU.add)\
                            .then_inc(on["summed"], 1)
                    if k == 3 and u == 0:
                        dve.wait_ge(on["squared"], t + 1)
                        V.tensor_copy(cen[:], B_[:, 0:TC]).then_inc(on["cen_kept"], 1)
                    if k == 4:
                        dve.wait_ge(on["rstd_ready"], t + 1)
                        V.tensor_tensor(xn[par][u][:], B_[:, 0:TC] if u else cen[:], rs[u][:], ALU.mult).then_inc(on["normed"], 1)
                    if k == 6:
                        dve.wait_ge(on["routed"], n * 2 + 2)
                        V.tensor_copy(lg[u][:].rearrange("p a b -> p (a b)"), L[:, LU * u:LU * u + G6 * NE]).then_inc(on["logits_kept"], 1)
                        dve.wait_ge(on["logits_kept"], t + 1)
                        V.tensor_reduce(lmx[u][:], lg[u][:], AX.X, ALU.max).then_inc(on["max_ready"], 1)
                        dve.wait_ge(on["max_ready"], t + 1)
                        V.tensor_tensor(lx[u][:], lg[u][:], bc(lmx[u][:]), ALU.subtract).then_inc(on["less_max"], 1)
                    if k == 7:
                        V.tensor_tensor(beat[u][:], lg[u][:].unsqueeze(2).broadcast_to([128, G6, NE, NE]),
                                        lg[u][:].unsqueeze(3).broadcast_to([128, G6, NE, NE]), ALU.is_gt).then_inc(on["beat_ready"], 1)
                        dve.wait_ge(on["beat_ready"], t + 1)
                        V.tensor_tensor(beat[u][:], beat[u][:], low[:].unsqueeze(1).broadcast_to([128, G6, NE, NE]), ALU.mult)\
                            .then_inc(on["beat_upper"], 1)
                    if k == 8:
                        dve.wait_ge(on["beat_upper"], t + 1)
                        V.tensor_reduce(rank[u][:], beat[u][:], AX.X, ALU.add)
                        V.tensor_reduce(rk2[u][:], beat[u][:].rearrange("p g e j -> p g j e"), AX.X, ALU.add).then_inc(on["ranks_a"], 1)
                        dve.wait_ge(on["ranks_a"], t + 1)
                        V.tensor_tensor(rank[u][:], rank[u][:], rk2[u][:], ALU.subtract).then_inc(on["rank_ready"], 1)
                        dve.wait_ge(on["rank_ready"], t + 1)
                        V.tensor_tensor(chosen[u][:], rank[u][:], rank_at[:].unsqueeze(1).broadcast_to([128, G6, NE]), ALU.is_lt)\
                            .then_inc(on["chosen_ready"], 1)
                    if k == 9:
                        dve.wait_ge(on["lexp_ready"], t + 1)
                        dve.wait_ge(on["chosen_ready"], t + 1)
                        V.tensor_tensor(lexp[u][:], lexp[u][:], chosen[u][:], ALU.mult).then_inc(on["kept_exp"], 1)
                        dve.wait_ge(on["kept_exp"], t + 1)
                        V.tensor_reduce(lsum[u][:], lexp[u][:], AX.X, ALU.add).then_inc(on["sum_ready"], 1)
                        dve.wait_ge(on["sum_ready"], t + 1)
                        V.reciprocal(lrc[u][:], lsum[u][:]).then_inc(on["rcp_ready"], 1)
                        dve.wait_ge(on["rcp_ready"], t + 1)
                        V.tensor_tensor(comb[u][:], lexp[u][:], bc(lrc[u][:]), ALU.mult).then_inc(on["comb_ready"], 1)

                    if k == 12:
                        dve.wait_ge(on["comb_kept"], t + 1)
                        V.scalar_tensor_tensor(cs[par][u][32:32 + 2 * NE], ct[par][u][:], HSCALE, cs[par][u][0:2 * NE],
                                               ALU.mult, ALU.subtract).then_inc(on["comb_split"], 1)

            def body(n, par, ahead):
                for i in range(SLOTS):
                    ahead(i)
                    if i < 2 * NE:
                        u = i % 2
                        dve.wait_ge(on["spread"], n * (2 * NE) + i + 1)
                        dve.wait_ge(on["gelu_done"], n * (2 * NE) + i + 1)
                        V.tensor_tensor(hm[u][:], hg[u][:], W[:, 0:TC], ALU.mult).then_inc(on["weighted"], 1)
                for u in (0, 1):
                    t = n * 2 + u
                    dve.wait_ge(on["down_done"], t + 1)
                    dve.wait_ge(on["based"], t + 1)
                    dve.wait_ge(stored[u], n * 16 + 1)
                    V.tensor_tensor(y[u][:], Y[u][:, 0:TC], base[par][u][:], ALU.add).then_inc(on["done"], 1)

            pairs(dve, body, front)


def _halves(a):
    return a.reshape((2, HB) + a.shape[1:])


def _dup(a):
    import numpy as np
    return np.concatenate([a, a], 0)


def _diag(a):
    import numpy as np
    z = np.zeros((2, a.shape[0], 2, a.shape[1]), a.dtype)
    z[0, :, 0], z[1, :, 1] = a, a
    return z.reshape(2 * a.shape[0], 2 * a.shape[1])


def swin_inputs(i):
    import numpy as np
    f = np.float32
    x = _halves(i["x"].reshape(NIMG, GRID, 4, GRID, 4))
    patches = x.transpose(0, 3, 5, 1, 2, 4).reshape(32, HB * NTOK)
    blocks, vecs = [], []
    for l in range(2):
        qkv = i["L0_tok_qkv_w"][l]
        blocks += [_diag(qkv[k * C:(k + 1) * C].T) for k in range(3)] + [_diag(i["L0_tok_proj_w"][l].T)]
        blocks += [_diag(i["L0_tok_w1"][l][c * C:(c + 1) * C].T) for c in range(4)]
        blocks += [_diag(i["L0_tok_w2"][l][:, c * C:(c + 1) * C].T) for c in range(4)]
        vecs += [i["L0_tok_" + k][l] for k in ("n1g", "n1b", "n2g", "n2b")]
        vecs += [i["L0_tok_qkv_b"][l][k * C:(k + 1) * C] for k in range(3)] + [i["L0_tok_proj_b"][l], i["L0_tok_b2"][l]]
        vecs += [i["L0_tok_b1"][l][c * C:(c + 1) * C] for c in range(4)]
    vecs += [i["L0_tok_pe_b"], i["L0_tok_pe_ng"], i["L0_tok_pe_nb"]]
    at = np.arange(WT)
    rel = (at[:, None] // WS - at[None] // WS + WS - 1) * (2 * WS - 1) + at[:, None] % WS - at[None] % WS + WS - 1
    part = lambda at: np.where(at < WS - SHIFT, 0, 1)
    row, col = part(at // WS), part(at % WS)
    differ = [np.zeros((WT, WT), bool), col[:, None] != col[None], row[:, None] != row[None]]
    differ.append(differ[1] | differ[2])

    def rows(t):
        z = np.zeros((2, KP, NH * WT), f)
        z[:, :WT] = t.reshape(WT, -1)
        return z.reshape(128, -1)

    rpb = np.concatenate([rows(i["L0_tok_rpb"][l][rel].transpose(0, 2, 1)) for l in range(2)], 1)
    amask = np.concatenate([rows(np.repeat(np.where(d, f(-100), f(0))[:, None], NH, 1)) for d in differ], 1)
    heads = _dup((np.arange(C)[:, None] // HD == np.arange(NH)[None]).astype(f))
    mean = _diag(np.full((C, C), 1.0 / C, f))
    consts = np.stack([np.eye(128, dtype=f), np.eye(128, dtype=f) - mean, mean])
    return {"patches": patches, "wts": np.concatenate(blocks, 1), "pew": _diag(i["L0_tok_pe_w"].reshape(C, 16).T),
            "vec": _dup(np.stack(vecs, 1)), "rpb": rpb, "amask": amask, "hmask": heads, "consts": consts}


def gru_inputs(i):
    import numpy as np
    f = np.float32
    d2 = ("fwd", "rev")
    wih = np.stack([i[f"L0_attn_{d}_w_ih"].reshape(3, C, C) for d in d2])
    wih = _dup(wih.transpose(3, 0, 1, 2).reshape(C, -1))
    whh = np.zeros((2, C, 3, 2, C), f)
    for n, d in enumerate(d2):
        whh[n, :, :, n] = i[f"L0_attn_{d}_w_hh"].reshape(3, C, C).transpose(2, 0, 1)
    bias = [np.concatenate([i[f"L0_attn_{d}_{b}"][g * C:(g + 1) * C] for d in d2]) for b in ("b_ih", "b_hh") for g in range(3)]
    gvec = np.stack([_dup(i["L0_attn_ln_g"])] + bias + [_dup(i["L0_attn_ln_b"])], 1)
    txt = _halves(i["txt"]).transpose(0, 3, 1, 2).reshape(128, HB * NTXT)
    return {"wih": wih, "whh": whh.reshape(128, -1), "gvec": gvec, "txt": txt}


def mixture_inputs(i):
    import numpy as np
    f = np.float32
    eye, zero = np.eye(C, dtype=f), np.zeros((C, C), f)
    ow = i["L0_attn_out_w"].T
    gru_w = np.concatenate([i["L0_attn_gate_w"].T, np.concatenate([eye, -eye]), np.concatenate([zero, ow])], 1)
    wexp = np.concatenate([_diag(i[k][e]) for e in range(NE) for k in ("L0_ffn_w1", "L0_ffn_w2")], 1)
    sel = np.zeros((2, NE, NE, 2, C), f)
    for h in range(2):
        for e in range(NE):
            sel[h, e, e, h] = 1
    mvec = np.stack([_dup(i["L0_attn_out_b"]), _dup(i["L0_attn_gate_b"])] + [_dup(i["L0_ffn_b1"][e]) for e in range(NE)], 1)
    e = np.arange(NE)
    after = (e[None] > e[:, None]).astype(f)
    low = np.repeat(after.reshape(1, -1), 128, 0)
    rank = np.repeat((2 - e).astype(f)[None], 128, 0)
    return {"gru_w": gru_w, "out_w": _diag(ow), "router": _diag(i["L0_ffn_router_w"].T), "wexp": wexp,
            "b2w": _diag(i["L0_ffn_b2"]), "sel_c": sel.reshape(2 * NE, -1), "mvec": mvec, "low_c": low, "rank_c": rank}


def program(nc, a, out):
    dram = lambda name, cols, dt=F32: nc.dram_tensor(name, (128, cols), dt, kind="Internal").ap()
    tok1, tok2 = dram("tok1", HB * NTOK), dram("tok2", HB * NTOK)
    xparts = (dram("x_hi", HB * S, F16), dram("x_lo", HB * S, F16))
    resid, hist = dram("resid", HB * S), dram("hist", NIMG * S)
    swin(nc, a["patches"], a["wts"], a["pew"], a["vec"], a["rpb"], a["amask"], a["hmask"], a["consts"], tok1, tok2)
    prepare(nc, a["consts"], tok2, a["txt"], xparts, resid)
    gru(nc, a["consts"], a["wih"], a["whh"], a["gvec"], xparts, hist)
    mixture(nc, a["consts"], a["gru_w"], a["out_w"], a["router"], a["wexp"], a["b2w"], a["sel_c"], a["mvec"], a["low_c"],
            a["rank_c"], hist, resid, out)


def kernel(**inputs):
    import numpy as np
    import concourse.bacc as bacc
    from concourse.bass_utils import run_bass_kernel_spmd

    i = {k: np.asarray(v) for k, v in inputs.items()}
    arrays = {**swin_inputs(i), **gru_inputs(i), **mixture_inputs(i)}
    arrays = {k: np.ascontiguousarray(v) for k, v in arrays.items()}
    nc = bacc.Bacc("TRN2", target_bir_lowering=False, num_devices=1)
    aps = {k: nc.dram_tensor(k, v.shape, mybir.dt.from_np(v.dtype), kind="ExternalInput").ap() for k, v in arrays.items()}
    out = nc.dram_tensor("out", (128, HB * S), F32, kind="ExternalOutput").ap()
    program(nc, aps, out)
    r = run_bass_kernel_spmd(nc, [arrays], core_ids=[0]).results[0]["out"]
    return r.reshape(2, C, S, HB).transpose(0, 3, 2, 1).reshape(NIMG, S, C)
```
